# Optimizing a Trainium2 kernel written in Bass

```python
import numpy as np
import jax
import jax.numpy as jnp

def _softmax(x, axis=-1):
    return jax.nn.softmax(x, axis=axis)

def _gelu(x):
    return jax.nn.gelu(x, approximate=True)

def _silu(x):
    return jax.nn.silu(x)

def _sigmoid(x):
    return jax.nn.sigmoid(x)

def _layernorm(x, axis=-1, eps=1e-05):
    m = jnp.mean(x, axis=axis, keepdims=True)
    v = jnp.var(x, axis=axis, keepdims=True)
    return (x - m) / jnp.sqrt(v + eps)

def _scatter_add(tgt, idx, src, axis=0):
    return tgt.at[idx].add(src)

def _segment_sum(src, seg, n):
    return jax.ops.segment_sum(src, seg, n)
kernel_name = 'mk_decoder_preln_d2_seqx_r4_e06c68'

def setup_inputs(seed: int=0):
    np.random.seed(seed)
    _w = jnp.asarray

    def _rec_inputs():
        import jax
        import jax.numpy as jnp
        _rk = jax.random.key(seed)
        x = -0.0003929 + 0.9999 * jax.random.normal(jax.random.fold_in(_rk, 1), (16, 128, 256), jnp.float32)
        _lenS = 128 - jax.random.randint(jax.random.fold_in(_rk, 7), (16,), 0, max(1, 128 // 4) + 1, jnp.int32)
        _lenS2 = 128 - jax.random.randint(jax.random.fold_in(_rk, 8), (16,), 0, max(1, 128 // 4) + 1, jnp.int32)
        _ctx_1024P = jax.random.normal(jax.random.fold_in(_rk, 11), (16, 16, 256), jnp.float32)
        _ctx_1024c = jax.random.dirichlet(jax.random.fold_in(_rk, 511), 0.3 * jnp.ones((16,), jnp.float32), (16, 128))
        _ctx_1024t = jnp.einsum('bsk,bkd->bsd', _ctx_1024c, _ctx_1024P)
        _ctx_1024t = _ctx_1024t * jax.lax.rsqrt(jnp.mean(jnp.square(_ctx_1024t)) + 1e-12) * 0.953939
        ctx_1024 = 2.81802e-05 + 1.00001 * (_ctx_1024t + 0.3 * jax.random.normal(jax.random.fold_in(_rk, 611), (16, 128, 256), jnp.float32))
        return (x, ctx_1024)
    x, ctx_1024 = _rec_inputs()

    def _L0_attn_setup():
        import jax, jax.numpy as jnp
        import numpy as np
        EMB, HEADS, HIDDEN = (256, 16, 64)
        BS, N = (2, 512)
        key = jax.random.key(seed)
        ks = jax.random.split(key, 7)
        s_in = 1.0 / np.sqrt(EMB)
        s_u = 1.0 / np.sqrt(HEADS * HIDDEN)
        return {'x': jax.random.normal(ks[0], (BS, N, EMB), dtype=jnp.float32), 'w_q': jax.random.uniform(ks[1], (EMB, HEADS * HIDDEN), jnp.float32, -s_in, s_in), 'w_k': jax.random.uniform(ks[2], (EMB, HEADS * HIDDEN), jnp.float32, -s_in, s_in), 'w_v': jax.random.uniform(ks[3], (EMB, HEADS * HIDDEN), jnp.float32, -s_in, s_in), 'w_u': jax.random.uniform(ks[4], (HEADS * HIDDEN, EMB), jnp.float32, -s_u, s_u), 'b_u': jax.random.uniform(ks[5], (EMB,), jnp.float32, -s_u, s_u)}
    _L0_attn_all = _L0_attn_setup()
    _L0_attn_in = {k: v for k, v in _L0_attn_all.items() if k in ('w_q', 'w_k', 'w_v', 'w_u', 'b_u')}
    del _L0_attn_all

    def _L0_xattn_setup():
        import jax, jax.numpy as jnp
        import numpy as np
        B, S, E, H = (4, 1024, 256, 16)
        rng = jax.random.key(seed)
        ks = jax.random.split(rng, 7)
        s = 0.02
        return {'query': jax.random.normal(ks[0], (B, S, E), jnp.float32), 'key': jax.random.normal(ks[1], (B, S, E), jnp.float32), 'value': jax.random.normal(ks[2], (B, S, E), jnp.float32), 'in_proj_w': jax.random.normal(ks[3], (3 * E, E), jnp.float32) * s, 'in_proj_b': jax.random.normal(ks[4], (3 * E,), jnp.float32) * s, 'out_proj_w': jax.random.normal(ks[5], (E, E), jnp.float32) * s, 'out_proj_b': jax.random.normal(ks[6], (E,), jnp.float32) * s, 'chunk_size': 64}
    _L0_xattn_all = _L0_xattn_setup()
    _L0_xattn_in = {k: v for k, v in _L0_xattn_all.items() if k in ('in_proj_w', 'in_proj_b', 'out_proj_w', 'out_proj_b')}
    del _L0_xattn_all

    def _L0_ffn_setup():
        import jax, jax.numpy as jnp
        import numpy as np
        TOPK = 8
        BN_EPS = 1e-05
        key = jax.random.key(seed)
        ks = jax.random.split(key, 5)
        b, n, d = (2, 256, 256)
        h, nk, kd = (8, 64, 128)
        ne = nk * nk
        scale = 0.02
        return {'inputs': jax.random.normal(ks[0], (b, n, d), jnp.float32), 'gamma': jnp.ones((d,), jnp.float32), 'beta': jnp.zeros((d,), jnp.float32), 'w_q': jax.random.normal(ks[1], (2 * h * kd, d), jnp.float32) * scale, 'keys': jax.random.normal(ks[2], (h, nk, 2, kd), jnp.float32) * scale, 'key_in': jax.random.normal(ks[3], (ne, d), jnp.float32) * scale, 'key_out': jax.random.normal(ks[4], (ne, d), jnp.float32) * scale}
    _L0_ffn_all = _L0_ffn_setup()
    _L0_ffn_in = {k: v for k, v in _L0_ffn_all.items() if k in ('gamma', 'beta', 'w_q', 'keys', 'key_in', 'key_out')}
    del _L0_ffn_all

    def _L1_attn_setup():
        import jax, jax.numpy as jnp
        import numpy as np
        D_MODEL = 256
        N_HEADS = 16
        HIDDEN = max(8, D_MODEL // 2)
        EPS = 1e-12
        key = jax.random.key(seed)
        ks = jax.random.split(key, 12)
        s = 0.02
        inp = {'x': jax.random.normal(ks[0], (8, 256, D_MODEL), dtype=jnp.float32), 'Wq': jax.random.normal(ks[1], (D_MODEL, D_MODEL), dtype=jnp.float32) * s, 'bq': jnp.zeros((D_MODEL,), dtype=jnp.float32), 'Wk': jax.random.normal(ks[2], (D_MODEL, D_MODEL), dtype=jnp.float32) * s, 'bk': jnp.zeros((D_MODEL,), dtype=jnp.float32), 'Wv': jax.random.normal(ks[3], (D_MODEL, D_MODEL), dtype=jnp.float32) * s, 'bv': jnp.zeros((D_MODEL,), dtype=jnp.float32), 'Wo': jax.random.normal(ks[4], (D_MODEL, D_MODEL), dtype=jnp.float32) * s, 'bo': jnp.zeros((D_MODEL,), dtype=jnp.float32), 'g': jnp.zeros((N_HEADS,), dtype=jnp.float32), 'Wg1': jax.random.normal(ks[5], (HIDDEN, D_MODEL), dtype=jnp.float32) * s, 'bg1': jnp.zeros((HIDDEN,), dtype=jnp.float32), 'Wg2': jax.random.normal(ks[6], (N_HEADS, HIDDEN), dtype=jnp.float32) * s, 'bg2': jnp.zeros((N_HEADS,), dtype=jnp.float32)}
        return inp
    _L1_attn_all = _L1_attn_setup()
    _L1_attn_in = {k: v for k, v in _L1_attn_all.items() if k in ('Wq', 'bq', 'Wk', 'bk', 'Wv', 'bv', 'Wo', 'bo', 'g', 'Wg1', 'bg1', 'Wg2', 'bg2')}
    del _L1_attn_all

    def _L1_xattn_setup():
        import jax, jax.numpy as jnp
        import numpy as np
        key = jax.random.key(seed)
        k1, k2, k3, k4 = jax.random.split(key, 4)
        B, L1, L2, D = (32, 128, 128, 256)
        ix = jax.random.normal(k1, (B, L1, D), dtype=jnp.float32)
        iother = jax.random.normal(k2, (B, L2, D), dtype=jnp.float32)
        scale = 1.0 / np.sqrt(D)
        W = jax.random.uniform(k3, (D, D), dtype=jnp.float32, minval=-scale, maxval=scale)
        b = jax.random.uniform(k4, (D,), dtype=jnp.float32, minval=-scale, maxval=scale)
        return {'ix': ix, 'iother': iother, 'W': W, 'b': b}
    _L1_xattn_all = _L1_xattn_setup()
    _L1_xattn_in = {k: v for k, v in _L1_xattn_all.items() if k in ('W', 'b')}
    del _L1_xattn_all

    def _L1_ffn_setup():
        import jax, jax.numpy as jnp
        import numpy as np
        B, S, D = (2, 128, 256)
        E, K, I = (16, 8, 256)
        I_SH = 256
        ROUTE_SCALE = 2.826
        key = jax.random.key(seed)
        ks = jax.random.split(key, 8)
        s = 0.02
        return {'x': jax.random.normal(ks[0], (B, S, D), dtype=jnp.float32), 'gate_w': jax.random.normal(ks[1], (E, D), dtype=jnp.float32) * s, 'expert_bias': jnp.zeros((E,), dtype=jnp.float32), 'w_gate': jax.random.normal(ks[2], (E, I, D), dtype=jnp.float32) * s, 'w_up': jax.random.normal(ks[3], (E, I, D), dtype=jnp.float32) * s, 'w_down': jax.random.normal(ks[4], (E, D, I), dtype=jnp.float32) * s, 'shared_gate_w': jax.random.normal(ks[5], (I_SH, D), dtype=jnp.float32) * s, 'shared_up_w': jax.random.normal(ks[6], (I_SH, D), dtype=jnp.float32) * s, 'shared_down_w': jax.random.normal(ks[7], (D, I_SH), dtype=jnp.float32) * s}
    _L1_ffn_all = _L1_ffn_setup()
    _L1_ffn_in = {k: v for k, v in _L1_ffn_all.items() if k in ('gate_w', 'expert_bias', 'w_gate', 'w_up', 'w_down', 'shared_gate_w', 'shared_up_w', 'shared_down_w')}
    del _L1_ffn_all
    return {'x': x, 'ctx_1024': ctx_1024, 'L0_attn_w_q': _L0_attn_in['w_q'], 'L0_attn_w_k': _L0_attn_in['w_k'], 'L0_attn_w_v': _L0_attn_in['w_v'], 'L0_attn_w_u': _L0_attn_in['w_u'], 'L0_attn_b_u': _L0_attn_in['b_u'], 'L0_xattn_in_proj_w': _L0_xattn_in['in_proj_w'], 'L0_xattn_in_proj_b': _L0_xattn_in['in_proj_b'], 'L0_xattn_out_proj_w': _L0_xattn_in['out_proj_w'], 'L0_xattn_out_proj_b': _L0_xattn_in['out_proj_b'], 'L0_ffn_gamma': _L0_ffn_in['gamma'], 'L0_ffn_beta': _L0_ffn_in['beta'], 'L0_ffn_w_q': _L0_ffn_in['w_q'], 'L0_ffn_keys': _L0_ffn_in['keys'], 'L0_ffn_key_in': _L0_ffn_in['key_in'], 'L0_ffn_key_out': _L0_ffn_in['key_out'], 'L1_attn_Wq': _L1_attn_in['Wq'], 'L1_attn_bq': _L1_attn_in['bq'], 'L1_attn_Wk': _L1_attn_in['Wk'], 'L1_attn_bk': _L1_attn_in['bk'], 'L1_attn_Wv': _L1_attn_in['Wv'], 'L1_attn_bv': _L1_attn_in['bv'], 'L1_attn_Wo': _L1_attn_in['Wo'], 'L1_attn_bo': _L1_attn_in['bo'], 'L1_attn_g': _L1_attn_in['g'], 'L1_attn_Wg1': _L1_attn_in['Wg1'], 'L1_attn_bg1': _L1_attn_in['bg1'], 'L1_attn_Wg2': _L1_attn_in['Wg2'], 'L1_attn_bg2': _L1_attn_in['bg2'], 'L1_xattn_W': _L1_xattn_in['W'], 'L1_xattn_b': _L1_xattn_in['b'], 'L1_ffn_gate_w': _L1_ffn_in['gate_w'], 'L1_ffn_expert_bias': _L1_ffn_in['expert_bias'], 'L1_ffn_w_gate': _L1_ffn_in['w_gate'], 'L1_ffn_w_up': _L1_ffn_in['w_up'], 'L1_ffn_w_down': _L1_ffn_in['w_down'], 'L1_ffn_shared_gate_w': _L1_ffn_in['shared_gate_w'], 'L1_ffn_shared_up_w': _L1_ffn_in['shared_up_w'], 'L1_ffn_shared_down_w': _L1_ffn_in['shared_down_w']}

def reference(x, ctx_1024, L0_attn_w_q, L0_attn_w_k, L0_attn_w_v, L0_attn_w_u, L0_attn_b_u, L0_xattn_in_proj_w, L0_xattn_in_proj_b, L0_xattn_out_proj_w, L0_xattn_out_proj_b, L0_ffn_gamma, L0_ffn_beta, L0_ffn_w_q, L0_ffn_keys, L0_ffn_key_in, L0_ffn_key_out, L1_attn_Wq, L1_attn_bq, L1_attn_Wk, L1_attn_bk, L1_attn_Wv, L1_attn_bv, L1_attn_Wo, L1_attn_bo, L1_attn_g, L1_attn_Wg1, L1_attn_bg1, L1_attn_Wg2, L1_attn_bg2, L1_xattn_W, L1_xattn_b, L1_ffn_gate_w, L1_ffn_expert_bias, L1_ffn_w_gate, L1_ffn_w_up, L1_ffn_w_down, L1_ffn_shared_gate_w, L1_ffn_shared_up_w, L1_ffn_shared_down_w):
    import jax
    import jax.numpy as jnp

    def _L0_attn_ref(x, w_q, w_k, w_v, w_u, b_u):
        import jax, jax.numpy as jnp
        import numpy as np
        EMB, HEADS, HIDDEN = (256, 16, 64)
        BS, N = (2, 512)
        bs, n, emb = x.shape
        h, hd = (HEADS, HIDDEN)
        q = (x @ w_q).reshape(bs, n, h, hd)
        k = (x @ w_k).reshape(bs, n, h, hd)
        v = (x @ w_v).reshape(bs, n, h, hd)
        scale = 1.0 / jnp.sqrt(jnp.asarray(hd, dtype=x.dtype))
        q = q * scale
        k = k * scale
        dot = jnp.einsum('bqhd,bkhd->bhqk', q, k)
        causal = jnp.tril(jnp.ones((n, n), dtype=bool))
        dot = jnp.where(causal, dot, jnp.asarray(-jnp.inf, dtype=dot.dtype))
        att = jax.nn.softmax(dot, axis=-1)
        out = jnp.einsum('bhqk,bkhd->bqhd', att, v).reshape(bs, n, h * hd)
        return out @ w_u + b_u

    def _L0_xattn_ref(query, key, value, in_proj_w, in_proj_b, out_proj_w, out_proj_b, chunk_size):
        import jax, jax.numpy as jnp
        import numpy as np
        B, S, E, H = (4, 1024, 256, 16)
        b, seq, e = query.shape
        h = H
        hd = e // h
        n = seq // chunk_size
        wq, wk, wv = jnp.split(in_proj_w, 3, axis=0)
        bq, bk, bv = jnp.split(in_proj_b, 3)
        q = query @ wq.T + bq
        k = key @ wk.T + bk
        v = value @ wv.T + bv

        def to_blocks(x):
            return x.reshape(b, n, chunk_size, h, hd)
        qh, kh, vh = (to_blocks(q), to_blocks(k), to_blocks(v))
        scores = jnp.einsum('bnqhd,bnkhd->bnhqk', qh, kh) / np.sqrt(hd)
        attn = jax.nn.softmax(scores, axis=-1)
        out = jnp.einsum('bnhqk,bnkhd->bnqhd', attn, vh).reshape(b, seq, e)
        return out @ out_proj_w.T + out_proj_b

    def _L0_ffn_ref(inputs, gamma, beta, w_q, keys, key_in, key_out):
        import jax, jax.numpy as jnp
        import numpy as np
        TOPK = 8
        BN_EPS = 1e-05
        b, n, d = inputs.shape
        h, nk, _, kd = keys.shape
        k = TOPK
        x = inputs.reshape(b * n, d)
        mu = jnp.mean(x, axis=0)
        var = jnp.mean(jnp.square(x - mu), axis=0)
        xn = (x - mu) * jax.lax.rsqrt(var + BN_EPS) * gamma + beta
        q = (xn @ w_q.T).reshape(b, n, 2, h, kd).transpose(2, 0, 1, 3, 4)
        sim = jnp.einsum('pbnhd,hkpd->pbnhk', q, keys)
        s, i = jax.lax.top_k(sim, k)
        sx, sy = (s[0], s[1])
        ix, iy = (i[0], i[1])
        all_scores = (sx[..., :, None] + sy[..., None, :]).reshape(b, n, h, k * k)
        all_idx = (ix[..., :, None] * nk + iy[..., None, :]).reshape(b, n, h, k * k)
        scores, pk = jax.lax.top_k(all_scores, k)
        idx = jnp.take_along_axis(all_idx, pk, axis=-1)
        w_down = key_in[idx]
        w_up = key_out[idx]
        o = jnp.einsum('bnd,bnhkd->bnhk', inputs, w_down)
        o = jax.nn.gelu(o, approximate=False) * jax.nn.softmax(scores, axis=-1)
        return jnp.einsum('bnhk,bnhkd->bnd', o, w_up)

    def _L1_attn_ref(x, Wq, bq, Wk, bk, Wv, bv, Wo, bo, g, Wg1, bg1, Wg2, bg2):
        import jax, jax.numpy as jnp
        import numpy as np
        D_MODEL = 256
        N_HEADS = 16
        HIDDEN = max(8, D_MODEL // 2)
        EPS = 1e-12
        B, T, D = x.shape
        H, dk = (N_HEADS, D // N_HEADS)

        def proj(W, b):
            return (x @ W.T + b).reshape(B, T, H, dk).transpose(0, 2, 1, 3)
        Q = proj(Wq, bq)
        K = proj(Wk, bk)
        V = proj(Wv, bv)
        Qn = Q / jnp.maximum(jnp.linalg.norm(Q, axis=-1, keepdims=True), EPS)
        Kn = K / jnp.maximum(jnp.linalg.norm(K, axis=-1, keepdims=True), EPS)
        scores = jnp.einsum('bhqd,bhkd->bhqk', Qn, Kn) / jnp.sqrt(jnp.float32(dk))
        attn = jax.nn.softmax(scores, axis=-1)
        head_outs = jnp.einsum('bhqk,bhkd->bhqd', attn, V)
        gate_static = jax.nn.sigmoid(g)[None, :, None, None]
        h = jax.nn.gelu(x @ Wg1.T + bg1, approximate=False)
        gate_logits = (h @ Wg2.T + bg2).mean(axis=1)
        gate_dynamic = jax.nn.sigmoid(gate_logits)[:, :, None, None]
        head_outs = head_outs * (gate_static * gate_dynamic)
        out = head_outs.transpose(0, 2, 1, 3).reshape(B, T, D)
        return out @ Wo.T + bo

    def _L1_xattn_ref(ix, iother, W, b):
        import jax, jax.numpy as jnp
        import numpy as np
        ex = jnp.einsum('bld,ed->ble', ix, W) + b
        eother = jnp.einsum('bld,ed->ble', iother, W) + b
        scores = jnp.einsum('bld,bmd->blm', ex, eother)
        attn = jax.nn.softmax(scores, axis=-1)
        aligned = jnp.einsum('blm,bmd->bld', attn, iother)
        return aligned

    def _L1_ffn_ref(x, gate_w, expert_bias, w_gate, w_up, w_down, shared_gate_w, shared_up_w, shared_down_w):
        import jax, jax.numpy as jnp
        import numpy as np
        B, S, D = (2, 128, 256)
        E, K, I = (16, 8, 256)
        I_SH = 256
        ROUTE_SCALE = 2.826
        gates = jnp.einsum('bsd,ed->bse', x, gate_w)
        scores = jax.nn.sigmoid(gates.astype(jnp.float32))
        sel_scores = scores + expert_bias
        _, inds = jax.lax.top_k(sel_scores, K)
        selected = jnp.take_along_axis(scores, inds, axis=-1)
        selected = selected / selected.sum(axis=-1, keepdims=True)
        selected = selected * ROUTE_SCALE
        onehot = jax.nn.one_hot(inds, E, dtype=selected.dtype)
        combine = jnp.einsum('bske,bsk->bse', onehot, selected)
        hg = jnp.einsum('bsd,eid->bsei', x, w_gate)
        hu = jnp.einsum('bsd,eid->bsei', x, w_up)
        h = jax.nn.silu(hg) * hu
        ye = jnp.einsum('bsei,edi->bsed', h, w_down)
        y = jnp.einsum('bsed,bse->bsd', ye, combine).astype(x.dtype)
        g = jnp.einsum('bsd,id->bsi', x, shared_gate_w)
        u = jnp.einsum('bsd,id->bsi', x, shared_up_w)
        y = y + jnp.einsum('bsi,di->bsd', jax.nn.silu(g) * u, shared_down_w)
        return y
    x = x + _L0_attn_ref(_layernorm(x, axis=-1), L0_attn_w_q, L0_attn_w_k, L0_attn_w_v, L0_attn_w_u, L0_attn_b_u)
    x = x + _L0_xattn_ref(_layernorm(x, axis=-1), ctx_1024, ctx_1024, L0_xattn_in_proj_w, L0_xattn_in_proj_b, L0_xattn_out_proj_w, L0_xattn_out_proj_b, 64)
    x = x + _L0_ffn_ref(_layernorm(x, axis=-1), L0_ffn_gamma, L0_ffn_beta, L0_ffn_w_q, L0_ffn_keys, L0_ffn_key_in, L0_ffn_key_out)
    x = x + _L1_attn_ref(_layernorm(x, axis=-1), L1_attn_Wq, L1_attn_bq, L1_attn_Wk, L1_attn_bk, L1_attn_Wv, L1_attn_bv, L1_attn_Wo, L1_attn_bo, L1_attn_g, L1_attn_Wg1, L1_attn_bg1, L1_attn_Wg2, L1_attn_bg2)
    x = x + _L1_xattn_ref(_layernorm(x, axis=-1), ctx_1024, L1_xattn_W, L1_xattn_b)
    x = x + _L1_ffn_ref(_layernorm(x, axis=-1), L1_ffn_gate_w, L1_ffn_expert_bias, L1_ffn_w_gate, L1_ffn_w_up, L1_ffn_w_down, L1_ffn_shared_gate_w, L1_ffn_shared_up_w, L1_ffn_shared_down_w)
    return x

_drawn_inputs = setup_inputs


def setup_inputs(seed=0):
    import zlib

    import numpy as np

    out = dict(_drawn_inputs(seed))
    spreads = {'L0_ffn_gamma': (1.0, 0.6),
     'L0_ffn_beta': (0.0, 0.8),
     'L1_attn_bq': (0.0, 0.8),
     'L1_attn_bk': (0.0, 0.8),
     'L1_attn_bv': (0.0, 0.687),
     'L1_attn_bo': (0.0, 0.1),
     'L1_attn_g': (0.0, 0.8),
     'L1_attn_bg1': (0.0, 0.8),
     'L1_attn_bg2': (0.0, 0.8),
     'L1_ffn_expert_bias': (0.0, 0.8)}
    factors = {'L0_attn_w_q': 8.0,
     'L0_attn_w_k': 8.0,
     'L0_xattn_in_proj_b': 5.753,
     'L0_ffn_w_q': 8.0,
     'L0_ffn_keys': 8.0,
     'L0_ffn_key_in': 8.0,
     'L0_ffn_key_out': 8.0,
     'L1_attn_Wq': 8.0,
     'L1_attn_Wk': 8.0,
     'L1_attn_Wv': 8.0,
     'L1_attn_Wo': 4.328,
     'L1_attn_Wg1': 8.0,
     'L1_attn_Wg2': 8.0,
     'L1_ffn_gate_w': 8.0,
     'L1_ffn_w_gate': 5.132,
     'L1_ffn_w_up': 5.08,
     'L1_ffn_w_down': 5.072,
     'L1_ffn_shared_gate_w': 5.151,
     'L1_ffn_shared_up_w': 5.123,
     'L1_ffn_shared_down_w': 5.091}
    for name, (base, spread) in spreads.items():
        noise = np.random.default_rng([zlib.crc32(name.encode()), seed]).standard_normal(out[name].shape)
        drawn = base * np.exp(spread * noise) if base else spread * noise
        out[name] = jnp.asarray(drawn.astype(out[name].dtype))
    for name, factor in factors.items():
        out[name] = (out[name] * factor).astype(out[name].dtype)
    return out
```

```python
from contextlib import ExitStack

import concourse.bass as bass
from concourse import mybir

P = 128
D = 256
KD = D // P
NB = 16
PAIRS = NB // 2
NH = 16
UNITS = 8
LN_EPS = 1e-5
NEG = -1.0e30

ALU = mybir.AluOpType
ACT = mybir.ActivationFunctionType
AX = mybir.AxisListType
F32 = mybir.dt.float32
BF16 = mybir.dt.bfloat16
F16 = mybir.dt.float16
U32 = mybir.dt.uint32


class Signal:

    def __init__(self, sem, per):
        self.sem, self.per = sem, per

    def at(self, i, k):
        return self.per * i + k


class Chain:

    def __init__(self, sem, per=None):
        self.sem, self.per, self.i, self.k = sem, per, 0, 0

    def begin(self, i):
        self.i, self.k = i, 0

    def link(self, eng, ins):
        self.k += 1
        ins.then_inc(self.sem, 1)
        eng.wait_ge(self.sem, (self.per or 0) * self.i + self.k)

    def end(self):
        assert self.per is None or self.k == self.per, (self.k, self.per)


class Scope:

    def __init__(self, nc, ctx, tag):
        self.nc, self.ctx, self.tag, self.sems = nc, ctx, tag, []

    def sb(self, name, shape, dt=F32):
        return self.ctx.enter_context(self.nc.sbuf_tensor(f"{self.tag}_{name}", shape, dt))

    def ps(self, name, shape, dt=F32):
        return self.ctx.enter_context(self.nc.psum_tensor(f"{self.tag}_{name}", shape, dt))

    def sem(self, name):
        sem = self.ctx.enter_context(self.nc.semaphore(f"{self.tag}_{name}"))
        self.sems.append(sem)
        return sem

    def _clear(self):
        for sem in self.sems:
            self.nc.sync.sem_clear(sem)
        self.nc.all_engine_barrier()

    def block(self):
        self.ctx.callback(self._clear)
        return self.ctx.enter_context(self.nc.Block())


class LayerNorm:

    def __init__(self, s, x, eps):
        self.x, self.eps = x, eps
        self.stats = s.sb("ln_stats", [P, 2, 6])
        self.mv = s.sb("ln_mv", [P, 2, 2])
        self.var_eps = s.sb("ln_var_eps", [P, 2])
        self.rstd = s.sb("ln_rstd", [P, 2])
        self.power = s.sb("ln_power", [P, 2])
        self.xn = s.sb("ln_xn", [P, 2, D])
        self.spare = s.sb("ln_spare", [1, 1])
        self.var_ready = s.sem("ln_var_ready")
        self.rstd_ready = s.sem("ln_rstd_ready")
        self.xn_ready = s.sem("ln_xn_ready")
        self.power_set = s.sem("ln_power_set")

    LINKS = 2

    def setup(self, pool):
        pool.memset(self.power[:, :], -0.5).then_inc(self.power_set, 1)
        pool.wait_ge(self.power_set, 1)

    def statistics(self, dve, chain, n):
        for b in range(2):
            last = dve.bn_stats(self.stats[:, b, :], self.x[:, bass.ds(2 * n + b, 1), :].rearrange("p a d -> p (a d)"))
        chain.link(dve, last)
        self.nudge(dve)
        for b in range(2):
            last = dve.bn_aggr(self.mv[:, b, :], self.stats[:, b, :])
        chain.link(dve, last)
        dve.tensor_scalar(self.var_eps[:, :], self.mv[:, :, 1], LN_EPS, None, ALU.add).then_inc(self.var_ready, 1)

    def nudge(self, dve):
        dve.memset(self.spare[:, :], 0.0)

    def root(self, pool, n):
        pool.wait_ge(self.var_ready, n + 1)
        pool.tensor_tensor(self.rstd[:, :], self.var_eps[:, :], self.power[:, :], ALU.pow).then_inc(self.rstd_ready, 1)

    def apply(self, dve, n):
        dve.wait_ge(self.rstd_ready, n + 1)
        for b in range(2):
            last = dve.tensor_scalar(self.xn[:, b, :], self.x[:, bass.ds(2 * n + b, 1), :].rearrange("p a d -> p (a d)"),
                                     self.mv[:, b, 0:1], self.rstd[:, b:b + 1], ALU.subtract, ALU.mult)
        last.then_inc(self.xn_ready, 1)

    def transposed(self, pe, bank, ident, n):
        pe.wait_ge(self.xn_ready, n + 1)
        for b in range(2):
            for k in range(KD):
                last = pe.transpose(bank[:, k * 2 * P + b * P:k * 2 * P + (b + 1) * P],
                                    self.xn[:, b, k * P:(k + 1) * P], ident[:, :])
        return last


class HeadAttention:

    def __init__(self, s, head_dim, heads, q_ap, k_ap, v_ap, ident, mask, out):
        self.hd, self.heads, self.q_ap, self.k_ap, self.v_ap = head_dim, heads, q_ap, k_ap, v_ap
        self.ident, self.mask, self.out = ident, mask, out
        self.score_bank = [s.ps(f"score{n}", [P, 512]) for n in range(2)]
        self.probT_bank = [s.ps(f"probT{n}", [P, 512]) for n in range(2)]
        self.out_bank = [s.ps(f"out{n}", [P, 512]) for n in range(2)]
        self.neg_max = s.sb("neg_max", [P, UNITS, 4])
        self.row_sum = s.sb("row_sum", [P, UNITS, 4])
        self.norm = s.sb("norm", [P, UNITS, 2, 2])
        self.prob = s.sb("prob", [P, 2, 4, P])
        self.probT = s.sb("probT", [P, 2, 4 * P])
        self.scored = [Signal(s.sem(f"scored{n}"), 4) for n in range(2)]
        self.max_ready = [Signal(s.sem(f"max_ready{n}"), 4) for n in range(2)]
        self.exp_ready = [Signal(s.sem(f"exp_ready{n}"), 4) for n in range(2)]
        self.transposed = [Signal(s.sem(f"transposed{n}"), 4) for n in range(2)]
        self.probT_ready = [Signal(s.sem(f"probT_ready{n}"), 4) for n in range(2)]
        self.weighted = [Signal(s.sem(f"weighted{n}"), 4) for n in range(2)]
        self.out_ready = [Signal(s.sem(f"out_ready{n}"), 4) for n in range(2)]

    def pe_scores(self, pe, i, u):
        b, g, n = u // 4, u % 4, u % 2
        pe.wait_ge(self.exp_ready[n].sem, self.exp_ready[n].at(i, u // 2))
        if self.mask is not None:
            ident_bf, mask_bf = self.mask
            pe.matmul(self.score_bank[n][:, :], ident_bf[:, :], mask_bf[:, :], start=True, stop=False,
                      skip_group_check=True)
        for j, h in enumerate(self.heads[g]):
            last = pe.matmul(self.score_bank[n][:, j * P:(j + 1) * P], self.q_ap(b, h), self.k_ap(b, h),
                             start=self.mask is None and j == 0, stop=True, skip_group_check=True)
        last.then_inc(self.scored[n].sem, 1)

    def dve_max(self, dve, i, u):
        n = u % 2
        dve.wait_ge(self.scored[n].sem, self.scored[n].at(i, u // 2 + 1))
        dve.tensor_reduce(self.neg_max[:, u, :], self.score_bank[n][:, :].rearrange("p (j k) -> p j k", j=4),
                          AX.X, ALU.max, negate=True).then_inc(self.max_ready[n].sem, 1)

    def act_exp(self, act, i, u):
        n = u % 2
        act.wait_ge(self.max_ready[n].sem, self.max_ready[n].at(i, u // 2 + 1))
        act.wait_ge(self.transposed[n].sem, self.transposed[n].at(i, u // 2))
        for j in range(4):
            last = act.activation(self.prob[:, n, j, :], self.score_bank[n][:, j * P:(j + 1) * P], ACT.Exp,
                                  bias=self.neg_max[:, u, j:j + 1], accum_out=self.row_sum[:, u, j:j + 1])
        last.then_inc(self.exp_ready[n].sem, 1)

    def pe_transpose(self, pe, i, u):
        n = u % 2
        pe.wait_ge(self.exp_ready[n].sem, self.exp_ready[n].at(i, u // 2 + 1))
        pe.wait_ge(self.probT_ready[n].sem, self.probT_ready[n].at(i, u // 2))
        for j in range(4):
            last = pe.transpose(self.probT_bank[n][:, j * P:(j + 1) * P], self.prob[:, n, j, :], self.ident[:, :])
        last.then_inc(self.transposed[n].sem, 1)

    def copy_probT(self, eng, i, u, copy):
        n = u % 2
        eng.wait_ge(self.transposed[n].sem, self.transposed[n].at(i, u // 2 + 1))
        eng.wait_ge(self.weighted[n].sem, self.weighted[n].at(i, u // 2))
        copy(self.probT[:, n, :], self.probT_bank[n][:, :]).then_inc(self.probT_ready[n].sem, 1)

    def pe_weighted(self, pe, i, u):
        b, g, n = u // 4, u % 4, u % 2
        pe.wait_ge(self.probT_ready[n].sem, self.probT_ready[n].at(i, u // 2 + 1))
        pe.wait_ge(self.out_ready[n].sem, self.out_ready[n].at(i, u // 2))
        for j, h in enumerate(self.heads[g]):
            last = pe.matmul(self.out_bank[n][:, j * self.hd:(j + 1) * self.hd], self.probT[:, n, j * P:(j + 1) * P],
                             self.v_ap(b, h), start=True, stop=True)
        last.then_inc(self.weighted[n].sem, 1)

    def dve_out(self, dve, chain, i, u, gate=None):
        b, g, n = u // 4, u % 4, u % 2
        dve.wait_ge(self.weighted[n].sem, self.weighted[n].at(i, u // 2 + 1))
        chain.link(dve, dve.reciprocal(self.norm[:, u, :, :].rearrange("p t a -> p (t a)"), self.row_sum[:, u, :]))
        if gate is not None:
            chain.link(dve, dve.tensor_tensor(self.norm[:, u, :, :], self.norm[:, u, :, :], gate(b, g), ALU.mult))
        dve.tensor_tensor(self.out(b, g), self.out_bank[n][:, 0:4 * self.hd].rearrange("p (t a d) -> p t a d", t=2, a=2),
                          self.norm[:, u, :, :].unsqueeze(3).broadcast_to([P, 2, 2, self.hd]), ALU.mult) \
            .then_inc(self.out_ready[n].sem, 1)


def stage_causal_attention(nc, x, ident, ones_row, ident_bf, mask_bf, x_in, w_q, w_k, w_v, w_u, b_u):
    HD = 64
    HW = NH * HD
    MT = HW // P
    QK_SCALE = 1.0 / HD
    RING = 18
    with ExitStack() as ctx:
        s = Scope(nc, ctx, "a0")
        wq, wk, wv = (s.sb(n, [P, KD, HW]) for n in ("wq", "wk", "wv"))
        wu = s.sb("wu", [P, MT, D])
        bu = s.sb("bu", [1, D])
        xnT = s.sb("xnT", [P, KD, 2 * P])
        qT, kT = (s.sb(n, [P, MT, 2 * P]) for n in ("qT", "kT"))
        v = s.sb("v", [P, 2, HW])
        attn = s.sb("attn", [P, 2, HW])
        attnT = s.sb("attnT", [P, 2, MT, P])
        ln = LayerNorm(s, x, None)
        proj_bank = [s.ps(f"proj{n}", [P, 512]) for n in range(2)]
        heads = [[0, 2, 4, 6], [1, 3, 5, 7], [8, 10, 12, 14], [9, 11, 13, 15]]
        att = HeadAttention(
            s, HD, heads,
            lambda b, h: qT[HD * (h % 2):HD * (h % 2) + HD, h // 2, b * P:(b + 1) * P],
            lambda b, h: kT[HD * (h % 2):HD * (h % 2) + HD, h // 2, b * P:(b + 1) * P],
            lambda b, h: v[:, b, h * HD:(h + 1) * HD],
            ident, (ident_bf, mask_bf),
            lambda b, g: attn[:, b, :].rearrange("p (s t a d) -> p s t a d", t=2, a=2, d=HD)[
                :, 2 * (g // 2):2 * (g // 2) + 2, :, g % 2, :])
        loaded = s.sem("loaded")
        x_loaded = s.sem("x_loaded")
        padded = s.sem("padded")
        first_T = s.sem("first_T")
        first_copied = s.sem("first_copied")
        produced = [Signal(s.sem(f"produced{n}"), RING // 2) for n in range(2)]
        evacuated = [Signal(s.sem(f"evacuated{n}"), RING // 2) for n in range(2)]
        links = Chain(s.sem("links"), 2 + UNITS)
        first_links = Chain(s.sem("first_links"))
        block = s.block()

        @block.sync
        def _(sp):
            sp.dma_start(x[:, 0:2, :], x_in.rearrange("b t d -> t b d")[:, 0:2, :]).then_inc(x_loaded, 16)
            for dst, src, k in ((wq, w_q, KD), (wk, w_k, KD), (wv, w_v, KD), (wu, w_u, MT)):
                sp.dma_start(dst[:, :, :], src.rearrange("(k p) n -> p k n", p=P)).then_inc(loaded, 16)
            sp.dma_start(bu[:, :], b_u.rearrange("(a d) -> a d", a=1)).then_inc(loaded, 16)
            sp.wait_ge(x_loaded, 16)
            sp.dma_start(x[:, 2:NB, :], x_in.rearrange("b t d -> t b d")[:, 2:NB, :]).then_inc(x_loaded, 16)

        @block.gpsimd
        def _(pool):
            ln.setup(pool)
            ln.root(pool, 0)
            with pool.Fori(0, PAIRS) as i:
                ln.root(pool, i + 1)

        @block.tensor
        def _(pe):
            ln.transposed(pe, proj_bank[0], ident, 0).then_inc(first_T, 1)
            pe.wait_ge(loaded, 80)
            pe.wait_ge(first_copied, 1)
            with pe.Fori(0, PAIRS) as i:
                def free(r):
                    pe.wait_ge(evacuated[r % 2].sem, evacuated[r % 2].at(i, r // 2))

                for r in range(12):
                    free(r)
                    if r == 0:
                        pe.wait_ge(first_copied, 1)
                    bank = proj_bank[r % 2]
                    if r < 8:
                        w = wq if r < 4 else wk
                        for m in range(2):
                            t = 2 * (r % 4) + m
                            for k in range(KD):
                                last = pe.matmul(bank[:, m * 256:(m + 1) * 256], w[:, k, t * P:(t + 1) * P],
                                                 xnT[:, k, :], start=(k == 0), stop=(k == KD - 1))
                    else:
                        b, half = (r - 8) // 2, (r - 8) % 2
                        for k in range(KD):
                            last = pe.matmul(bank[:, :], xnT[:, k, b * P:(b + 1) * P],
                                             wv[:, k, half * 512:(half + 1) * 512], start=(k == 0), stop=(k == KD - 1))
                    last.then_inc(produced[r % 2].sem, 1)

                def turn_out(r):
                    b, half = (r - 13) // 2, (r - 13) % 2
                    free(r)
                    for n in range(2):
                        pe.wait_ge(att.out_ready[n].sem, att.out_ready[n].at(i, 2 * b + 2))
                    for j in range(4):
                        t = 4 * half + j
                        last = pe.transpose(proj_bank[r % 2][:, j * P:(j + 1) * P], attn[:, b, t * P:(t + 1) * P],
                                            ident[:, :])
                    last.then_inc(produced[r % 2].sem, 1)

                pe.wait_ge(evacuated[0].sem, evacuated[0].at(i, 4))
                pe.wait_ge(evacuated[1].sem, evacuated[1].at(i, 4))
                att.pe_scores(pe, i, 0)
                for u in range(UNITS):
                    if u + 1 < UNITS:
                        att.pe_scores(pe, i, u + 1)
                    att.pe_transpose(pe, i, u)
                    if u >= 1:
                        if u == 1:
                            pe.wait_ge(evacuated[0].sem, evacuated[0].at(i, 6))
                            pe.wait_ge(evacuated[1].sem, evacuated[1].at(i, 6))
                        att.pe_weighted(pe, i, u - 1)
                    if u == 3:
                        free(12)
                        ln.transposed(pe, proj_bank[0], ident, i + 1).then_inc(produced[0].sem, 1)
                    if u == 5:
                        turn_out(13)
                        turn_out(14)
                att.pe_weighted(pe, i, UNITS - 1)
                turn_out(15)
                turn_out(16)
                free(17)
                pe.wait_ge(evacuated[0].sem, evacuated[0].at(i, 9))
                for b in range(2):
                    for t in range(MT):
                        pe.matmul(proj_bank[1][:, b * D:(b + 1) * D], attnT[:, b, t, :], wu[:, t, :],
                                  start=(t == 0), stop=False)
                    last = pe.matmul(proj_bank[1][:, b * D:(b + 1) * D], ones_row[:, :], bu[:, :],
                                     start=False, stop=True)
                last.then_inc(produced[1].sem, 1)

        @block.scalar
        def _(act):
            act.wait_ge(first_T, 1)
            act.copy(xnT[:, :, :], proj_bank[0][:, :].rearrange("p (k t) -> p k t", k=KD)).then_inc(first_copied, 1)
            with act.Fori(0, PAIRS) as i:
                def evacuate(r, dst, scale=1.0):
                    act.wait_ge(produced[0].sem, produced[0].at(i, r // 2 + 1))
                    act.activation(dst, proj_bank[0][:, :], ACT.Copy, scale=scale).then_inc(evacuated[0].sem, 1)

                for r in range(0, 12, 2):
                    if r < 4:
                        evacuate(r, qT[:, 2 * r:2 * r + 2, :].rearrange("p a t -> p (a t)"), QK_SCALE)
                    elif r < 8:
                        evacuate(r, kT[:, 2 * (r - 4):2 * (r - 4) + 2, :].rearrange("p a t -> p (a t)"))
                    else:
                        evacuate(r, v[:, (r - 8) // 2, 0:512])
                att.act_exp(act, i, 0)
                for u in range(UNITS):
                    if u + 1 < UNITS:
                        att.act_exp(act, i, u + 1)
                    if u % 2:
                        att.copy_probT(act, i, u, act.copy)
                    if u == 4:
                        evacuate(12, xnT[:, :, :].rearrange("p k t -> p (k t)"))
                    if u == 6:
                        evacuate(14, attnT[:, 0, 4:8, :].rearrange("p a t -> p (a t)"))
                evacuate(16, attnT[:, 1, 4:8, :].rearrange("p a t -> p (a t)"))

        @block.vector
        def _(dve):
            dve.memset(x[:, NB:NB + 2, :], 0.0).then_inc(padded, 1)
            dve.wait_ge(padded, 1)
            dve.wait_ge(x_loaded, 16)
            ln.statistics(dve, first_links, 0)
            ln.apply(dve, 0)
            dve.wait_ge(x_loaded, 32)
            with dve.Fori(0, PAIRS) as i:
                links.begin(i)

                def evacuate(r, dst, scale=1.0):
                    dve.wait_ge(produced[1].sem, produced[1].at(i, r // 2 + 1))
                    dve.tensor_scalar(dst, proj_bank[1][:, :], scale, None, ALU.mult).then_inc(evacuated[1].sem, 1)

                for r in range(1, 12, 2):
                    if r < 4:
                        evacuate(r, qT[:, 2 * r:2 * r + 2, :].rearrange("p a t -> p (a t)"), QK_SCALE)
                    elif r < 8:
                        evacuate(r, kT[:, 2 * (r - 4):2 * (r - 4) + 2, :].rearrange("p a t -> p (a t)"))
                    else:
                        evacuate(r, v[:, (r - 8) // 2, 512:1024])
                att.dve_max(dve, i, 0)
                for u in range(UNITS):
                    if u + 1 < UNITS:
                        att.dve_max(dve, i, u + 1)
                    if u == 0:
                        ln.statistics(dve, links, i + 1)
                    if u == 1:
                        ln.apply(dve, i + 1)
                    if u % 2 == 0:
                        att.copy_probT(dve, i, u, dve.tensor_copy)
                    if u >= 1:
                        att.dve_out(dve, links, i, u - 1)
                    if u == 6:
                        evacuate(13, attnT[:, 0, 0:4, :].rearrange("p a t -> p (a t)"))
                att.dve_out(dve, links, i, UNITS - 1)
                evacuate(15, attnT[:, 1, 0:4, :].rearrange("p a t -> p (a t)"))
                dve.wait_ge(produced[1].sem, produced[1].at(i, 9))
                dve.tensor_tensor(x[:, bass.ds(2 * i, 2), :], proj_bank[1][:, :].rearrange("p (b d) -> p b d", b=2),
                                  x[:, bass.ds(2 * i, 2), :], ALU.add).then_inc(evacuated[1].sem, 1)
                links.end()


HEADS16 = [[2 * g, 2 * g + 1, 8 + 2 * g, 8 + 2 * g + 1] for g in range(4)]


def rows16(h):
    return slice(32 * ((h % 8) // 2), 32 * ((h % 8) // 2) + 32)


class Turner:

    def __init__(self, s, banks, ident):
        self.banks, self.ident, self.jobs = banks, ident, []
        self.turned = [s.sem(f"w_turned{n}") for n in range(2)]
        self.copied = [s.sem(f"w_copied{n}") for n in range(2)]

    def weight(self, w, wT, tiles):
        for k in range(KD):
            for t in range(0, tiles, 4):
                m = min(4, tiles - t)
                self.jobs.append(([w[:, t + j, k * P:(k + 1) * P] for j in range(m)], wT[:, k, t * P:(t + m) * P]))

    def on_pe(self, pe):
        for n, (blocks, _) in enumerate(self.jobs):
            pe.wait_ge(self.copied[n % 2], n // 2)
            at = 0
            for b in blocks:
                rows = b.shape[0]
                last = pe.transpose(self.banks[n % 2][:, at:at + rows], b, self.ident[0:rows, 0:rows])
                at += rows
            last.then_inc(self.turned[n % 2], 1)

    def _copy(self, eng, copy, parity):
        for n, (blocks, dst) in enumerate(self.jobs):
            if n % 2 == parity:
                eng.wait_ge(self.turned[parity], n // 2 + 1)
                cols = sum(b.shape[0] for b in blocks)
                copy(dst, self.banks[parity][:, 0:cols]).then_inc(self.copied[parity], 1)

    def on_act(self, act):
        self._copy(act, act.copy, 0)

    def on_dve(self, dve):
        self._copy(dve, dve.tensor_copy, 1)

    def wait_all(self, pe):
        for parity in range(2):
            pe.wait_ge(self.copied[parity], len(self.jobs[parity::2]))


def stage_chunked_attention(nc, x, ident, ones_row, ident_bf, mask_bf, par_mask, ctx_in, w_in, b_in, w_out, b_out):
    HD = D // NH
    RING = 8
    with ExitStack() as ctx:
        s = Scope(nc, ctx, "x0")
        w_nat = s.sb("w_nat", [P, 8, D])
        wT = s.sb("wT", [P, KD, 8 * P])
        bqk = s.sb("bqk", [P, 2, 2])
        bv, bo = s.sb("bv", [1, D]), s.sb("bo", [1, D])
        ctx_sb = s.sb("ctx", [P, 2, D])
        ctxT = s.sb("ctxT", [P, KD, 2 * P])
        xnT = s.sb("xnT", [P, KD, 2 * P])
        qm = s.sb("qm", [P, 2, KD, 2 * P])
        kT = s.sb("kT", [P, KD, 2 * P])
        v = s.sb("v", [P, 2, D])
        attn = s.sb("attn", [P, 2, D])
        attnT = s.sb("attnT", [P, 2, KD, P])
        ln = LayerNorm(s, x, None)
        proj_bank = [s.ps(f"proj{n}", [P, 512]) for n in range(2)]
        att = HeadAttention(
            s, HD, HEADS16,
            lambda b, h: qm[rows16(h), h % 2, h // 8, b * P:(b + 1) * P],
            lambda b, h: kT[rows16(h), h // 8, b * P:(b + 1) * P],
            lambda b, h: v[:, b, h * HD:(h + 1) * HD],
            ident, (ident_bf, mask_bf),
            lambda b, g: attn[:, b, :].rearrange("p (t g a d) -> p t g a d", t=2, g=4, a=2)[:, :, g, :, :])
        turner = Turner(s, proj_bank, ident)
        turner.weight(w_nat, wT, 8)
        loaded = s.sem("loaded")
        ctx_loaded = s.sem("ctx_loaded")
        ctx_turned = s.sem("ctx_turned")
        first_T = s.sem("first_T")
        first_copied = s.sem("first_copied")
        produced = [Signal(s.sem("produced0"), RING // 2 - 1), Signal(s.sem("produced1"), RING // 2)]
        evacuated = [Signal(s.sem(f"evacuated{n}"), RING // 2) for n in range(2)]
        links = Chain(s.sem("links"), 2 + UNITS)
        first_links = Chain(s.sem("first_links"))
        block = s.block()

        @block.sync
        def _(sp):
            sp.dma_start(w_nat[:, 0:6, :], w_in.rearrange("(t p) n -> p t n", p=P)).then_inc(loaded, 16)
            sp.dma_start(w_nat[:, 6:8, :], w_out.rearrange("(t p) n -> p t n", p=P)).then_inc(loaded, 16)
            sp.dma_start(ctx_sb[:, :, :], ctx_in.rearrange("b t d -> t b d")[:, 0:2, :]).then_inc(ctx_loaded, 16)
            for c in range(2):
                sp.dma_start(bqk[:, c, :], b_in[c * D:(c + 1) * D].rearrange("(k p) -> p k", p=P),
                             allow_slow_non_contiguous=True).then_inc(loaded, 16)
            sp.dma_start(bv[:, :], b_in[2 * D:3 * D].rearrange("(a d) -> a d", a=1)).then_inc(loaded, 16)
            sp.dma_start(bo[:, :], b_out.rearrange("(a d) -> a d", a=1)).then_inc(loaded, 16)
            with sp.Fori(1, PAIRS) as n:
                sp.wait_ge(ctx_turned, n)
                sp.dma_start(ctx_sb[:, :, :], ctx_in.rearrange("b t d -> t b d")[:, bass.ds(2 * n, 2), :]) \
                    .then_inc(ctx_loaded, 16)
            sp.wait_ge(ctx_turned, PAIRS)
            sp.dma_start(ctx_sb[:, :, :], ctx_in.rearrange("b t d -> t b d")[:, 0:2, :]).then_inc(ctx_loaded, 16)
            sp.wait_ge(ctx_loaded, 16 * PAIRS + 16)

        @block.gpsimd
        def _(pool):
            ln.setup(pool)
            ln.root(pool, 0)
            with pool.Fori(0, PAIRS) as i:
                ln.root(pool, i + 1)

        def turn_context(pe, bank):
            for b in range(2):
                for k in range(KD):
                    last = pe.transpose(bank[:, k * 2 * P + b * P:k * 2 * P + (b + 1) * P],
                                        ctx_sb[:, b, k * P:(k + 1) * P], ident[:, :])
            return last

        @block.tensor
        def _(pe):
            pe.wait_ge(loaded, 96)
            turner.on_pe(pe)
            turner.wait_all(pe)
            ln.transposed(pe, proj_bank[0], ident, 0).then_inc(first_T, 1)
            pe.wait_ge(ctx_loaded, 16)
            turn_context(pe, proj_bank[1]).then_inc(ctx_turned, 1)
            pe.wait_ge(first_copied, 2)
            with pe.Fori(0, PAIRS) as i:
                def free(r):
                    pe.wait_ge(evacuated[r % 2].sem, evacuated[r % 2].at(i, r // 2))

                def channels(r, w0, act):
                    free(r)
                    for m in range(2):
                        for k in range(KD):
                            last = pe.matmul(proj_bank[r % 2][:, m * 256:(m + 1) * 256],
                                             wT[:, k, w0 + m * P:w0 + (m + 1) * P], act[:, k, :],
                                             start=(k == 0), stop=(k == KD - 1))
                    last.then_inc(produced[r % 2].sem, 1)

                def tokens(r, w0, acts, bias):
                    free(r)
                    for b in range(2):
                        for k in range(KD):
                            pe.matmul(proj_bank[r % 2][:, b * D:(b + 1) * D], acts(b, k), wT[:, k, w0:w0 + D],
                                      start=(k == 0), stop=False)
                        last = pe.matmul(proj_bank[r % 2][:, b * D:(b + 1) * D], ones_row[:, :], bias[:, :],
                                         start=False, stop=True)
                    last.then_inc(produced[r % 2].sem, 1)

                def turn_out(r, b):
                    free(r)
                    for n in range(2):
                        pe.wait_ge(att.out_ready[n].sem, att.out_ready[n].at(i, 2 * b + 2))
                    for k in range(KD):
                        last = pe.transpose(proj_bank[r % 2][:, k * P:(k + 1) * P], attn[:, b, k * P:(k + 1) * P],
                                            ident[:, :])
                    last.then_inc(produced[r % 2].sem, 1)

                channels(0, D, ctxT)
                channels(1, 0, xnT)
                tokens(2, 2 * D, lambda b, k: ctxT[:, k, b * P:(b + 1) * P], bv)
                pe.wait_ge(evacuated[0].sem, evacuated[0].at(i, 1))
                pe.wait_ge(evacuated[1].sem, evacuated[1].at(i, 1))
                att.pe_scores(pe, i, 0)
                for u in range(UNITS):
                    if u + 1 < UNITS:
                        att.pe_scores(pe, i, u + 1)
                    att.pe_transpose(pe, i, u)
                    if u >= 1:
                        if u == 1:
                            pe.wait_ge(evacuated[0].sem, evacuated[0].at(i, 2))
                        att.pe_weighted(pe, i, u - 1)
                    if u == 3:
                        free(3)
                        ln.transposed(pe, proj_bank[1], ident, i + 1).then_inc(produced[1].sem, 1)
                        free(4)
                        pe.wait_ge(ctx_loaded, 16 * i + 32)
                        turn_context(pe, proj_bank[0]).then_inc(ctx_turned, 1)
                    if u == 5:
                        turn_out(5, 0)
                att.pe_weighted(pe, i, UNITS - 1)
                turn_out(6, 1)
                pe.wait_ge(evacuated[1].sem, evacuated[1].at(i, 3))
                pe.wait_ge(evacuated[0].sem, evacuated[0].at(i, 4))
                tokens(7, 3 * D, lambda b, k: attnT[:, b, k, :], bo)

        @block.scalar
        def _(act):
            turner.on_act(act)
            act.wait_ge(first_T, 1)
            act.copy(xnT[:, :, :].rearrange("p k t -> p (k t)"), proj_bank[0][:, :]).then_inc(first_copied, 1)
            with act.Fori(0, PAIRS) as i:
                def arrived(r):
                    act.wait_ge(produced[0].sem, produced[0].at(i, r // 2 + 1 - (r > 4)))

                arrived(0)
                for m in range(2):
                    last = act.activation(kT[:, m, :], proj_bank[0][:, m * 256:(m + 1) * 256], ACT.Identity,
                                          bias=bqk[:, 1, m:m + 1])
                last.then_inc(evacuated[0].sem, 1)
                arrived(2)
                act.copy(v[:, :, :].rearrange("p b d -> p (b d)"), proj_bank[0][:, :]).then_inc(evacuated[0].sem, 1)
                att.act_exp(act, i, 0)
                for u in range(UNITS):
                    if u + 1 < UNITS:
                        att.act_exp(act, i, u + 1)
                    if u % 2:
                        att.copy_probT(act, i, u, act.copy)
                    if u == 4:
                        act.wait_ge(ctx_turned, i + 2)
                        act.copy(ctxT[:, :, :].rearrange("p k t -> p (k t)"), proj_bank[0][:, :]) \
                            .then_inc(evacuated[0].sem, 1)
                arrived(6)
                act.copy(attnT[:, 1, :, :].rearrange("p k t -> p (k t)"), proj_bank[0][:, 0:D]) \
                    .then_inc(evacuated[0].sem, 1)

        @block.vector
        def _(dve):
            ln.statistics(dve, first_links, 0)
            ln.apply(dve, 0)
            turner.on_dve(dve)
            dve.wait_ge(ctx_turned, 1)
            dve.tensor_copy(ctxT[:, :, :].rearrange("p k t -> p (k t)"), proj_bank[1][:, :]).then_inc(first_copied, 1)
            with dve.Fori(0, PAIRS) as i:
                links.begin(i)

                def arrived(r):
                    dve.wait_ge(produced[1].sem, produced[1].at(i, r // 2 + 1))

                arrived(1)
                for m in range(2):
                    for par in range(2):
                        last = dve.tensor_scalar(qm[:, par, m, :], proj_bank[1][:, m * 256:(m + 1) * 256],
                                                 bqk[:, 0, m:m + 1], par_mask[:, par:par + 1], ALU.add, ALU.mult)
                last.then_inc(evacuated[1].sem, 1)
                att.dve_max(dve, i, 0)
                for u in range(UNITS):
                    if u + 1 < UNITS:
                        att.dve_max(dve, i, u + 1)
                    if u == 0:
                        ln.statistics(dve, links, i + 1)
                    if u == 1:
                        ln.apply(dve, i + 1)
                    if u % 2 == 0:
                        att.copy_probT(dve, i, u, dve.tensor_copy)
                    if u >= 1:
                        att.dve_out(dve, links, i, u - 1)
                    if u == 4:
                        arrived(3)
                        dve.tensor_copy(xnT[:, :, :].rearrange("p k t -> p (k t)"), proj_bank[1][:, :]) \
                            .then_inc(evacuated[1].sem, 1)
                    if u == 6:
                        arrived(5)
                        dve.tensor_copy(attnT[:, 0, :, :].rearrange("p k t -> p (k t)"), proj_bank[1][:, 0:D]) \
                            .then_inc(evacuated[1].sem, 1)
                att.dve_out(dve, links, i, UNITS - 1)
                arrived(7)
                dve.tensor_tensor(x[:, bass.ds(2 * i, 2), :], proj_bank[1][:, :].rearrange("p (b d) -> p b d", b=2),
                                  x[:, bass.ds(2 * i, 2), :], ALU.add).then_inc(evacuated[1].sem, 1)
                links.end()


def stage_gated_attention(nc, x, ident, ones_row, par_mask, w_q, b_q, w_k, b_k, w_v, b_v, w_o, b_o, g_in,
                          w_g1, b_g1, w_g2, b_g2):
    HD = D // NH
    GH = P
    NORM_EPS2 = 1e-24
    RING = 10
    NQ, NK, NV, NO = 0, D, 2 * D, 3 * D
    with ExitStack() as ctx:
        s = Scope(nc, ctx, "a1")
        w_nat = s.sb("w_nat", [P, 9, D])
        wT = s.sb("wT", [P, KD, 9 * P])
        wg2 = s.sb("wg2", [NH, GH])
        wg2T = s.sb("wg2T", [P, NH])
        bqk, bv, bo = s.sb("bqk", [1, 2 * D]), s.sb("bv", [1, D]), s.sb("bo", [1, D])
        bg1 = s.sb("bg1", [P, 1])
        bg2, g_row = s.sb("bg2", [1, NH]), s.sb("g_row", [1, NH])
        xnT = s.sb("xnT", [P, KD, 2 * P])
        qk = s.sb("qk", [P, 2, 2 * D])
        sq = s.sb("sq", [P, 2, 2 * D])
        ss = s.sb("ss", [P, 2 * 2 * NH])
        inv = s.sb("inv", [P, 2 * 2 * NH])
        inv_power = s.sb("inv_power", [P, 2 * 2 * NH])
        qm = s.sb("qm", [P, 2, 2, KD, P])
        kT = s.sb("kT", [P, 2, KD, P])
        v = s.sb("v", [P, 2, D])
        attn = s.sb("attn", [P, 2, D])
        attnT = s.sb("attnT", [P, 2, KD, P])
        gelu = s.sb("gelu", [P, 2 * P])
        hsum = s.sb("hsum", [P, 2])
        hrep = s.sb("hrep", [P, 2, P])
        gate_static = s.sb("gate_static", [P, NH])
        gate = s.sb("gate", [P, 2, NH])
        gate_bias = s.sb("gate_bias", [P, NH])
        ones_sq = s.sb("ones_sq", [P, P])
        ln = LayerNorm(s, x, None)
        proj_bank = [s.ps(f"proj{n}", [P, 512]) for n in range(2)]
        att = HeadAttention(
            s, HD, HEADS16,
            lambda b, h: qm[rows16(h), h % 2, b, h // 8, :],
            lambda b, h: kT[rows16(h), b, h // 8, :],
            lambda b, h: v[:, b, h * HD:(h + 1) * HD],
            ident, None,
            lambda b, g: attn[:, b, :].rearrange("p (t g a d) -> p t g a d", t=2, g=4, a=2)[:, :, g, :, :])
        turner = Turner(s, proj_bank, ident)
        turner.weight(w_nat, wT, 9)
        turner.jobs.append(([wg2[:, :]], wg2T[:, :]))
        loaded = s.sem("loaded")
        first_T = s.sem("first_T")
        first_copied = s.sem("first_copied")
        static_spread = s.sem("static_spread")
        static_exp = s.sem("static_exp")
        power_set = s.sem("power_set")
        ones_set = s.sem("ones_set")
        squares_ready = s.sem("squares_ready")
        inverse_ready = s.sem("inverse_ready")
        scaled = s.sem("scaled")
        hidden_spread = s.sem("hidden_spread")
        logits_exp = s.sem("logits_exp")
        produced = [Signal(s.sem(f"produced{n}"), RING // 2) for n in range(2)]
        evacuated = [Signal(s.sem(f"evacuated{n}"), RING // 2) for n in range(2)]
        links = Chain(s.sem("links"), 2 + 2 * UNITS + 6)
        first_links = Chain(s.sem("first_links"))
        block = s.block()

        @block.sync
        def _(sp):
            for n, w in enumerate((w_q, w_k, w_v, w_o)):
                sp.dma_start(w_nat[:, 2 * n:2 * n + 2, :], w.rearrange("(t p) n -> p t n", p=P)).then_inc(loaded, 16)
            sp.dma_start(w_nat[:, 8, :], w_g1).then_inc(loaded, 16)
            sp.dma_start(wg2[:, :], w_g2).then_inc(loaded, 16)
            for dst, b in ((bqk[:, 0:D], b_q), (bqk[:, D:2 * D], b_k), (bv[:, :], b_v), (bo[:, :], b_o),
                           (bg2[:, :], b_g2), (g_row[:, :], g_in)):
                sp.dma_start(dst, b.rearrange("(a d) -> a d", a=1)).then_inc(loaded, 16)
            sp.dma_start(bg1[:, :], b_g1.rearrange("(p a) -> p a", a=1)).then_inc(loaded, 16)

        @block.gpsimd
        def _(pool):
            ln.setup(pool)
            pool.memset(inv_power[:, :], -0.5).then_inc(power_set, 1)
            pool.memset(ones_sq[:, :], 1.0).then_inc(ones_set, 1)
            pool.wait_ge(power_set, 1)
            ln.root(pool, 0)
            with pool.Fori(0, PAIRS) as i:
                pool.wait_ge(squares_ready, i + 1)
                pool.tensor_tensor(inv[:, :], ss[:, :], inv_power[:, :], ALU.pow).then_inc(inverse_ready, 1)
                ln.root(pool, i + 1)

        @block.tensor
        def _(pe):
            pe.wait_ge(loaded, 13 * 16)
            turner.on_pe(pe)
            turner.wait_all(pe)
            ln.transposed(pe, proj_bank[0], ident, 0).then_inc(first_T, 1)
            pe.matmul(proj_bank[1][:, 0:NH], ones_row[:, :], g_row[:, :], start=True, stop=True) \
                .then_inc(static_spread, 1)
            pe.wait_ge(first_copied, 1)
            pe.wait_ge(static_exp, 1)
            with pe.Fori(0, PAIRS) as i:
                def free(r):
                    pe.wait_ge(evacuated[r % 2].sem, evacuated[r % 2].at(i, r // 2))

                def tokens(r, b, cols, act, w0, n, bias):
                    dst = proj_bank[r % 2][:, cols:cols + n]
                    for k in range(KD):
                        pe.matmul(dst, act(b, k), wT[:, k, w0:w0 + n], start=(k == 0), stop=False)
                    return pe.matmul(dst, ones_row[:, :], bias, start=False, stop=True)

                def of_x(b, k):
                    return xnT[:, k, b * P:(b + 1) * P]

                free(0)
                pe.wait_ge(evacuated[1].sem, evacuated[1].at(i, 0))
                for k in range(KD):
                    last = pe.matmul(proj_bank[0][:, 0:2 * P], wT[:, k, 8 * P:9 * P], xnT[:, k, :],
                                     start=(k == 0), stop=(k == KD - 1))
                last.then_inc(produced[0].sem, 1)
                for b in range(2):
                    free(1 + b)
                    tokens(1 + b, b, 0, of_x, NQ, 2 * D, bqk[:, :]).then_inc(produced[(1 + b) % 2].sem, 1)
                free(3)
                pe.wait_ge(hidden_spread, i + 1)
                for b in range(2):
                    pe.matmul(proj_bank[1][:, b * NH:(b + 1) * NH], hrep[:, b, :], wg2T[:, :], start=True, stop=True)
                last = pe.matmul(proj_bank[1][:, 2 * NH:3 * NH], ones_row[:, :], bg2[:, :], start=True, stop=True)
                last.then_inc(produced[1].sem, 1)
                free(4)
                for b in range(2):
                    last = tokens(4, b, b * D, of_x, NV, D, bv[:, :])
                last.then_inc(produced[0].sem, 1)
                pe.wait_ge(scaled, i + 1)
                for b in range(2):
                    free(5 + b)
                    for t in range(4):
                        last = pe.transpose(proj_bank[(5 + b) % 2][:, t * P:(t + 1) * P], qk[:, b, t * P:(t + 1) * P],
                                            ident[:, :])
                    last.then_inc(produced[(5 + b) % 2].sem, 1)
                pe.wait_ge(evacuated[1].sem, evacuated[1].at(i, 3))
                att.pe_scores(pe, i, 0)
                for u in range(UNITS):
                    if u + 1 < UNITS:
                        if u == 3:
                            pe.wait_ge(evacuated[0].sem, evacuated[0].at(i, 4))
                        att.pe_scores(pe, i, u + 1)
                    att.pe_transpose(pe, i, u)
                    if u >= 1:
                        if u == 1:
                            pe.wait_ge(evacuated[0].sem, evacuated[0].at(i, 3))
                        att.pe_weighted(pe, i, u - 1)
                    if u == 3:
                        free(7)
                        ln.transposed(pe, proj_bank[1], ident, i + 1).then_inc(produced[1].sem, 1)
                att.pe_weighted(pe, i, UNITS - 1)
                free(8)
                for n in range(2):
                    pe.wait_ge(att.out_ready[n].sem, att.out_ready[n].at(i, 4))
                for b in range(2):
                    for k in range(KD):
                        last = pe.transpose(proj_bank[0][:, (2 * b + k) * P:(2 * b + k + 1) * P],
                                            attn[:, b, k * P:(k + 1) * P], ident[:, :])
                last.then_inc(produced[0].sem, 1)
                free(9)
                pe.wait_ge(evacuated[0].sem, evacuated[0].at(i, 5))
                for b in range(2):
                    last = tokens(9, b, b * D, lambda b, k: attnT[:, b, k, :], NO, D, bo[:, :])
                last.then_inc(produced[1].sem, 1)

        @block.scalar
        def _(act):
            turner.on_act(act)
            act.wait_ge(first_T, 1)
            act.copy(xnT[:, :, :].rearrange("p k t -> p (k t)"), proj_bank[0][:, :]).then_inc(first_copied, 1)
            act.wait_ge(static_spread, 1)
            act.activation(gate_static[:, :], proj_bank[1][:, 0:NH], ACT.Exp, scale=-1.0).then_inc(static_exp, 1)
            act.wait_ge(loaded, 13 * 16)
            with act.Fori(0, PAIRS) as i:
                def arrived(r):
                    act.wait_ge(produced[0].sem, produced[0].at(i, r // 2 + 1))

                arrived(0)
                for b in range(2):
                    last = act.activation(gelu[:, b * P:(b + 1) * P], proj_bank[0][:, b * P:(b + 1) * P], ACT.Gelu,
                                          bias=bg1[:, :], accum_out=hsum[:, b:b + 1])
                last.then_inc(evacuated[0].sem, 1)
                act.wait_ge(evacuated[0].sem, evacuated[0].at(i, 1))
                for b in range(2):
                    last = act.activation(hrep[:, b, :], ones_sq[:, :], ACT.Copy, scale=hsum[:, b:b + 1])
                last.then_inc(hidden_spread, 1)
                arrived(2)
                act.copy(qk[:, 1, :], proj_bank[0][:, :]).then_inc(evacuated[0].sem, 1)
                arrived(4)
                act.copy(v[:, :, :].rearrange("p b d -> p (b d)"), proj_bank[0][:, :]).then_inc(evacuated[0].sem, 1)
                act.wait_ge(evacuated[1].sem, evacuated[1].at(i, 2))
                act.activation(gate[:, :, :], gate[:, :, :], ACT.Exp, scale=-1.0).then_inc(logits_exp, 1)
                arrived(6)
                for par in range(2):
                    act.activation(qm[:, par, 1, :, :].rearrange("p k t -> p (k t)"), proj_bank[0][:, 0:D], ACT.Copy,
                                   scale=par_mask[:, par:par + 1])
                act.copy(kT[:, 1, :, :].rearrange("p k t -> p (k t)"), proj_bank[0][:, D:2 * D]) \
                    .then_inc(evacuated[0].sem, 1)
                att.act_exp(act, i, 0)
                for u in range(UNITS):
                    if u + 1 < UNITS:
                        att.act_exp(act, i, u + 1)
                    if u % 2:
                        att.copy_probT(act, i, u, act.copy)
                arrived(8)
                act.copy(attnT[:, :, :, :].rearrange("p b k t -> p (b k t)"), proj_bank[0][:, :]) \
                    .then_inc(evacuated[0].sem, 1)

        @block.vector
        def _(dve):
            ln.statistics(dve, first_links, 0)
            ln.apply(dve, 0)
            turner.on_dve(dve)
            dve.wait_ge(static_exp, 1)
            first_links.link(dve, dve.tensor_scalar(gate_static[:, :], gate_static[:, :], 1.0, None, ALU.add))
            dve.reciprocal(gate_static[:, :], gate_static[:, :]).then_inc(static_exp, 1)
            dve.wait_ge(static_exp, 2)
            with dve.Fori(0, PAIRS) as i:
                links.begin(i)

                def arrived(r):
                    dve.wait_ge(produced[1].sem, produced[1].at(i, r // 2 + 1))

                arrived(1)
                dve.tensor_copy(qk[:, 0, :], proj_bank[1][:, :]).then_inc(evacuated[1].sem, 1)
                dve.wait_ge(evacuated[1].sem, evacuated[1].at(i, 1))
                dve.wait_ge(evacuated[0].sem, evacuated[0].at(i, 2))
                links.link(dve, dve.tensor_tensor(sq[:, :, :], qk[:, :, :], qk[:, :, :], ALU.mult))
                links.link(dve, dve.tensor_reduce(ss[:, :], sq[:, :, :].rearrange("p b (h d) -> p (b h) d", d=HD),
                                                  AX.X, ALU.add))
                dve.tensor_scalar(ss[:, :], ss[:, :], NORM_EPS2, None, ALU.max).then_inc(squares_ready, 1)
                arrived(3)
                links.link(dve, dve.tensor_copy(gate_bias[:, :], proj_bank[1][:, 2 * NH:3 * NH]))
                dve.scalar_tensor_tensor(gate[:, :, :], proj_bank[1][:, 0:2 * NH].rearrange("p (b h) -> p b h", b=2),
                                         1.0 / P, gate_bias[:, :].unsqueeze(1).broadcast_to([P, 2, NH]),
                                         ALU.mult, ALU.add).then_inc(evacuated[1].sem, 1)
                dve.wait_ge(inverse_ready, i + 1)
                dve.tensor_tensor(qk[:, :, :].rearrange("p b (h d) -> p (b h) d", d=HD),
                                  qk[:, :, :].rearrange("p b (h d) -> p (b h) d", d=HD),
                                  inv[:, :].unsqueeze(2).broadcast_to([P, 4 * NH, HD]), ALU.mult).then_inc(scaled, 1)
                arrived(5)
                for par in range(2):
                    dve.tensor_scalar(qm[:, par, 0, :, :].rearrange("p k t -> p (k t)"), proj_bank[1][:, 0:D],
                                      par_mask[:, par:par + 1], None, ALU.mult)
                dve.tensor_copy(kT[:, 0, :, :].rearrange("p k t -> p (k t)"), proj_bank[1][:, D:2 * D]) \
                    .then_inc(evacuated[1].sem, 1)
                dve.wait_ge(logits_exp, i + 1)
                links.link(dve, dve.tensor_scalar(gate[:, :, :], gate[:, :, :], 1.0, None, ALU.add))
                links.link(dve, dve.reciprocal(gate[:, :, :], gate[:, :, :]))
                links.link(dve, dve.tensor_tensor(gate[:, :, :], gate[:, :, :],
                                                  gate_static[:, :].unsqueeze(1).broadcast_to([P, 2, NH]), ALU.mult))

                def gate_of(b, g):
                    return gate[:, b, :].rearrange("p (t g a) -> p t g a", t=2, g=4)[:, :, g, :]

                att.dve_max(dve, i, 0)
                for u in range(UNITS):
                    if u + 1 < UNITS:
                        att.dve_max(dve, i, u + 1)
                    if u == 0:
                        ln.statistics(dve, links, i + 1)
                    if u == 1:
                        ln.apply(dve, i + 1)
                    if u % 2 == 0:
                        att.copy_probT(dve, i, u, dve.tensor_copy)
                    if u >= 1:
                        att.dve_out(dve, links, i, u - 1, gate_of)
                    if u == 4:
                        arrived(7)
                        dve.tensor_copy(xnT[:, :, :].rearrange("p k t -> p (k t)"), proj_bank[1][:, :]) \
                            .then_inc(evacuated[1].sem, 1)
                att.dve_out(dve, links, i, UNITS - 1, gate_of)
                arrived(9)
                dve.tensor_tensor(x[:, bass.ds(2 * i, 2), :], proj_bank[1][:, :].rearrange("p (b d) -> p b d", b=2),
                                  x[:, bass.ds(2 * i, 2), :], ALU.add).then_inc(evacuated[1].sem, 1)
                links.end()


def stage_aligned_attention(nc, x, ident, ones_row, ctx_in, w_in, b_in):
    RING = 6
    with ExitStack() as ctx:
        s = Scope(nc, ctx, "x1")
        w_nat = s.sb("w_nat", [P, 2, D])
        wT = s.sb("wT", [P, KD, D])
        bias = s.sb("bias", [P, KD])
        ctx_next = s.sb("ctx_next", [P, 2, D])
        ctx_now = s.sb("ctx_now", [P, 2, D])
        ctxT = s.sb("ctxT", [P, KD, 2 * P])
        xnT = s.sb("xnT", [P, KD, 2 * P])
        exT = s.sb("exT", [P, KD, 2 * P])
        eoT = s.sb("eoT", [P, KD, 2 * P])
        neg_max, row_sum, norm = (s.sb(n, [P, 2]) for n in ("neg_max", "row_sum", "norm"))
        prob = s.sb("prob", [P, 2, P])
        probT = s.sb("probT", [P, 2, P])
        ln = LayerNorm(s, x, None)
        proj_bank = [s.ps(f"proj{n}", [P, 512]) for n in range(2)]
        out_bank = s.ps("out", [P, 512])
        turner = Turner(s, proj_bank, ident)
        turner.weight(w_nat, wT, 2)
        loaded = s.sem("loaded")
        ctx_loaded = s.sem("ctx_loaded")
        ctx_turned = s.sem("ctx_turned")
        values_loaded = s.sem("values_loaded")
        first_T = s.sem("first_T")
        first_copied = s.sem("first_copied")
        max_ready = s.sem("max_ready")
        weighted = s.sem("weighted")
        added = s.sem("added")
        produced = [Signal(s.sem("produced0"), RING // 2 - 1), Signal(s.sem("produced1"), RING // 2)]
        evacuated = [Signal(s.sem(f"evacuated{n}"), RING // 2) for n in range(2)]
        links = Chain(s.sem("links"), 3)
        first_links = Chain(s.sem("first_links"))
        block = s.block()

        @block.sync
        def _(sp):
            ctx_pairs = ctx_in.rearrange("b t d -> t b d")
            sp.dma_start(w_nat[:, :, :], w_in.rearrange("(t p) n -> p t n", p=P)).then_inc(loaded, 16)
            sp.dma_start(bias[:, :], b_in.rearrange("(k p) -> p k", p=P),
                         allow_slow_non_contiguous=True).then_inc(loaded, 16)
            sp.dma_start(ctx_next[:, :, :], ctx_pairs[:, 0:2, :]).then_inc(ctx_loaded, 16)
            with sp.Fori(0, PAIRS - 1) as n:
                sp.wait_ge(weighted, n)
                sp.dma_start(ctx_now[:, :, :], ctx_pairs[:, bass.ds(2 * n, 2), :]).then_inc(values_loaded, 16)
                sp.wait_ge(ctx_turned, n + 1)
                sp.dma_start(ctx_next[:, :, :], ctx_pairs[:, bass.ds(2 * n + 2, 2), :]).then_inc(ctx_loaded, 16)
            sp.wait_ge(weighted, PAIRS - 1)
            sp.dma_start(ctx_now[:, :, :], ctx_pairs[:, NB - 2:NB, :]).then_inc(values_loaded, 16)
            sp.wait_ge(ctx_turned, PAIRS)
            sp.dma_start(ctx_next[:, :, :], ctx_pairs[:, 0:2, :]).then_inc(ctx_loaded, 16)
            sp.wait_ge(ctx_loaded, 16 * PAIRS + 16)

        @block.gpsimd
        def _(pool):
            ln.setup(pool)
            ln.root(pool, 0)
            with pool.Fori(0, PAIRS) as i:
                ln.root(pool, i + 1)

        def turn_context(pe, bank):
            for b in range(2):
                for k in range(KD):
                    last = pe.transpose(bank[:, k * 2 * P + b * P:k * 2 * P + (b + 1) * P],
                                        ctx_next[:, b, k * P:(k + 1) * P], ident[:, :])
            return last

        @block.tensor
        def _(pe):
            pe.wait_ge(loaded, 32)
            turner.on_pe(pe)
            turner.wait_all(pe)
            ln.transposed(pe, proj_bank[0], ident, 0).then_inc(first_T, 1)
            pe.wait_ge(ctx_loaded, 16)
            turn_context(pe, proj_bank[1]).then_inc(ctx_turned, 1)
            pe.wait_ge(first_copied, 2)
            with pe.Fori(0, PAIRS) as i:
                def free(r):
                    pe.wait_ge(evacuated[r % 2].sem, evacuated[r % 2].at(i, r // 2))

                for r, act in ((0, xnT), (1, ctxT)):
                    free(0)
                    free(1)
                    for m in range(2):
                        for k in range(KD):
                            last = pe.matmul(proj_bank[r][:, m * 256:(m + 1) * 256], wT[:, k, m * P:(m + 1) * P],
                                             act[:, k, :], start=(k == 0), stop=(k == KD - 1))
                    last.then_inc(produced[r].sem, 1)
                free(2)
                pe.wait_ge(evacuated[1].sem, evacuated[1].at(i, 1))
                for b in range(2):
                    for k in range(KD):
                        last = pe.matmul(proj_bank[0][:, b * P:(b + 1) * P], exT[:, k, b * P:(b + 1) * P],
                                         eoT[:, k, b * P:(b + 1) * P], start=(k == 0), stop=(k == KD - 1))
                last.then_inc(produced[0].sem, 1)
                free(3)
                ln.transposed(pe, proj_bank[1], ident, i + 1).then_inc(produced[1].sem, 1)
                free(4)
                pe.wait_ge(ctx_loaded, 16 * i + 32)
                turn_context(pe, proj_bank[0]).then_inc(ctx_turned, 1)
                free(5)
                for b in range(2):
                    last = pe.transpose(proj_bank[1][:, b * P:(b + 1) * P], prob[:, b, :], ident[:, :])
                last.then_inc(produced[1].sem, 1)
                pe.wait_ge(evacuated[1].sem, evacuated[1].at(i, 3))
                pe.wait_ge(values_loaded, 16 * i + 16)
                pe.wait_ge(added, i)
                for b in range(2):
                    last = pe.matmul(out_bank[:, b * D:(b + 1) * D], probT[:, b, :], ctx_now[:, b, :],
                                     start=True, stop=True)
                last.then_inc(weighted, 1)

        @block.scalar
        def _(act):
            turner.on_act(act)
            act.wait_ge(first_T, 1)
            act.copy(xnT[:, :, :].rearrange("p k t -> p (k t)"), proj_bank[0][:, :]).then_inc(first_copied, 1)
            act.wait_ge(loaded, 32)
            with act.Fori(0, PAIRS) as i:
                act.wait_ge(produced[0].sem, produced[0].at(i, 1))
                for m in range(2):
                    last = act.activation(exT[:, m, :], proj_bank[0][:, m * 256:(m + 1) * 256], ACT.Identity,
                                          bias=bias[:, m:m + 1])
                last.then_inc(evacuated[0].sem, 1)
                act.wait_ge(max_ready, i + 1)
                for b in range(2):
                    last = act.activation(prob[:, b, :], proj_bank[0][:, b * P:(b + 1) * P], ACT.Exp,
                                          bias=neg_max[:, b:b + 1], accum_out=row_sum[:, b:b + 1])
                last.then_inc(evacuated[0].sem, 1)
                act.wait_ge(ctx_turned, i + 2)
                act.copy(ctxT[:, :, :].rearrange("p k t -> p (k t)"), proj_bank[0][:, :]) \
                    .then_inc(evacuated[0].sem, 1)

        @block.vector
        def _(dve):
            ln.statistics(dve, first_links, 0)
            ln.apply(dve, 0)
            turner.on_dve(dve)
            dve.wait_ge(ctx_turned, 1)
            dve.tensor_copy(ctxT[:, :, :].rearrange("p k t -> p (k t)"), proj_bank[1][:, :]).then_inc(first_copied, 1)
            dve.wait_ge(loaded, 32)
            with dve.Fori(0, PAIRS) as i:
                links.begin(i)
                dve.wait_ge(produced[1].sem, produced[1].at(i, 1))
                for m in range(2):
                    last = dve.tensor_scalar(eoT[:, m, :], proj_bank[1][:, m * 256:(m + 1) * 256],
                                             bias[:, m:m + 1], None, ALU.add)
                last.then_inc(evacuated[1].sem, 1)
                ln.statistics(dve, links, i + 1)
                dve.wait_ge(produced[0].sem, produced[0].at(i, 2))
                dve.tensor_reduce(neg_max[:, :], proj_bank[0][:, 0:2 * P].rearrange("p (b k) -> p b k", b=2),
                                  AX.X, ALU.max, negate=True).then_inc(max_ready, 1)
                ln.apply(dve, i + 1)
                dve.wait_ge(produced[1].sem, produced[1].at(i, 2))
                dve.tensor_copy(xnT[:, :, :].rearrange("p k t -> p (k t)"), proj_bank[1][:, :]) \
                    .then_inc(evacuated[1].sem, 1)
                dve.wait_ge(produced[1].sem, produced[1].at(i, 3))
                dve.tensor_copy(probT[:, :, :].rearrange("p b t -> p (b t)"), proj_bank[1][:, 0:2 * P]) \
                    .then_inc(evacuated[1].sem, 1)
                links.link(dve, dve.reciprocal(norm[:, :], row_sum[:, :]))
                dve.wait_ge(weighted, i + 1)
                for b in range(2):
                    xb = x[:, bass.ds(2 * i + b, 1), :].rearrange("p a d -> p (a d)")
                    last = dve.scalar_tensor_tensor(xb, out_bank[:, b * D:(b + 1) * D], norm[:, b:b + 1], xb,
                                                    ALU.mult, ALU.add)
                last.then_inc(added, 1)
                links.end()


def stage_product_keys(nc, x, ident, gamma, beta, w_q, keys, key_in, key_out):
    H, NK, TOP = 8, 64, 8
    KW = P
    R = NK // 2
    PICKS = H * TOP
    TOKENS = NB * P
    HALF = P // 2
    W_SCALE = 4096.0
    GT = 16
    GU = HALF // GT
    with ExitStack() as ctx:
        s = Scope(nc, ctx, "f")
        hT = s.sb("hT", [P, KD, TOKENS + 2 * P])
        kiT = s.sb("kiT", [P, KD, R, P])
        ko = s.sb("ko", [P, R, D])
        gel = s.sb("gel", [P, R, 2 * P])
        fused = s.sb("fused", [P, KD, 2 * H * NK])
        bn_scale, bn_shift = s.sb("bn_scale", [P, KD]), s.sb("bn_shift", [P, KD])
        with ExitStack() as prep_ctx:
            p = Scope(nc, prep_ctx, "fp")
            wq_nat = p.sb("wq_nat", [P, 2 * H, D])
            keys_nat = p.sb("keys_nat", [NK, H, 2, KW])
            keysT = p.sb("keysT", [P, H, 2, NK])
            gamma_col, beta_col = p.sb("gamma_col", [P, KD]), p.sb("beta_col", [P, KD])
            stats, mv = p.sb("stats", [P, KD, 4, 6]), p.sb("mv", [P, KD, 2])
            bn_scale_power = p.sb("bn_power", [P, KD])
            var_eps, rstd = p.sb("var_eps", [P, KD]), p.sb("rstd", [P, KD])
            ln = LayerNorm(p, x, None)
            banks = [p.ps(f"bank{n}", [P, 512]) for n in range(2)]
            pair_bank = p.ps("pair", [P, 512])
            turner = Turner(p, banks, ident)
            for k in range(KD):
                for r in range(0, R, 4):
                    turner.jobs.append(([gel[:, r + j, k * P:(k + 1) * P] for j in range(4)],
                                        kiT[:, k, r:r + 4, :].rearrange("p r c -> p (r c)")))
            for h in range(0, H, 4):
                turner.jobs.append(([keys_nat[:, h + j, ax, :] for j in range(4) for ax in range(2)],
                                    keysT[:, h:h + 4, :, :].rearrange("p h a n -> p (h a n)")))
            loaded = p.sem("loaded")
            kept = p.sem("kept")
            fused_ready = [p.sem(f"fused_ready{n}") for n in range(2)]
            fused_copied = [p.sem(f"fused_copied{n}") for n in range(2)]
            pair_turned = p.sem("pair_turned")
            pair_copied = p.sem("pair_copied")
            power_set = p.sem("power_set")
            bn_var_ready = p.sem("bn_var_ready")
            bn_rstd_ready = p.sem("bn_rstd_ready")
            links = Chain(p.sem("links"), 2)
            bn_links = Chain(p.sem("bn_links"))
            block = p.block()

            @block.sync
            def _(sp):
                for b in range(2):
                    sp.dma_start(gel[b * NK:(b + 1) * NK, :, :],
                                 key_in.rearrange("(i r b) d -> b i r d", r=R, b=2)[b]).then_inc(loaded, 16)
                sp.dma_start(keys_nat[:, :, :, :], keys.rearrange("h n a w -> n h a w")).then_inc(loaded, 16)
                sp.dma_start(wq_nat[:, :, :], w_q.rearrange("(j p) d -> p j d", p=P)).then_inc(loaded, 16)
                for dst, src in ((gamma_col, gamma), (beta_col, beta)):
                    sp.dma_start(dst[:, :], src.rearrange("(k p) -> p k", p=P),
                                 allow_slow_non_contiguous=True).then_inc(loaded, 16)
                for b in range(2):
                    sp.dma_start(ko[b * NK:(b + 1) * NK, :, :],
                                 key_out.rearrange("(i r b) d -> b i r d", r=R, b=2)[b]).then_inc(kept, 16)
                sp.wait_ge(kept, 32)

            @block.gpsimd
            def _(pool):
                ln.setup(pool)
                pool.memset(hT[:, :, TOKENS:TOKENS + 2 * P], 0.0)
                pool.memset(bn_scale_power[:, :], -0.5).then_inc(power_set, 1)
                with pool.Fori(0, PAIRS) as i:
                    ln.root(pool, i)
                pool.wait_ge(power_set, 1)
                pool.wait_ge(bn_var_ready, 1)
                pool.tensor_tensor(rstd[:, :], var_eps[:, :], bn_scale_power[:, :], ALU.pow).then_inc(bn_rstd_ready, 1)

            @block.tensor
            def _(pe):
                with pe.Fori(0, PAIRS) as i:
                    pe.wait_ge(pair_copied, i)
                    ln.transposed(pe, pair_bank, ident, i).then_inc(pair_turned, 1)
                pe.wait_ge(loaded, 96)
                turner.on_pe(pe)
                turner.wait_all(pe)
                for n in range(4):
                    k, ax = n // 2, n % 2
                    pe.wait_ge(fused_copied[n % 2], n // 2)
                    for h in range(H):
                        last = pe.matmul(banks[n % 2][:, h * NK:(h + 1) * NK],
                                         wq_nat[:, ax * H + h, k * P:(k + 1) * P], keysT[:, h, ax, :],
                                         start=True, stop=True)
                    last.then_inc(fused_ready[n % 2], 1)

            def copy_fused(eng, copy, par):
                for n in range(par, 4, 2):
                    eng.wait_ge(fused_ready[par], n // 2 + 1)
                    copy(fused[:, n // 2, par * H * NK:(par + 1) * H * NK], banks[par][:, :]) \
                        .then_inc(fused_copied[par], 1)

            @block.scalar
            def _(act):
                with act.Fori(0, PAIRS) as i:
                    act.wait_ge(pair_turned, i + 1)
                    act.copy(hT[:, :, bass.ds(i * 2 * P, 2 * P)],
                             pair_bank[:, :].rearrange("p (k t) -> p k t", k=KD)).then_inc(pair_copied, 1)
                turner.on_act(act)
                copy_fused(act, act.copy, 0)

            @block.vector
            def _(dve):
                with dve.Fori(0, PAIRS) as i:
                    links.begin(i)
                    ln.statistics(dve, links, i)
                    dve.wait_ge(pair_turned, i)
                    ln.apply(dve, i)
                    links.end()
                dve.wait_ge(pair_copied, PAIRS)
                for k in range(KD):
                    for c in range(4):
                        last = dve.bn_stats(stats[:, k, c, :], hT[:, k, c * 512:(c + 1) * 512])
                bn_links.link(dve, last)
                for k in range(KD):
                    last = dve.bn_aggr(mv[:, k, :], stats[:, k, :, :].rearrange("p c s -> p (c s)"))
                bn_links.link(dve, last)
                dve.tensor_scalar(var_eps[:, :], mv[:, :, 1], LN_EPS, None, ALU.add).then_inc(bn_var_ready, 1)
                turner.on_dve(dve)
                dve.wait_ge(loaded, 96)
                dve.wait_ge(bn_rstd_ready, 1)
                bn_links.link(dve, dve.tensor_tensor(bn_scale[:, :], gamma_col[:, :], rstd[:, :], ALU.mult))
                bn_links.link(dve, dve.tensor_tensor(bn_shift[:, :], mv[:, :, 0], bn_scale[:, :], ALU.mult))
                dve.tensor_tensor(bn_shift[:, :], beta_col[:, :], bn_shift[:, :], ALU.subtract)
                copy_fused(dve, dve.tensor_copy, 1)

        xbT = s.sb("xbT", [P, KD, 2 * P])
        spare = s.sb("spare", [1, 1])
        ints = s.sb("ints", [P, P], mybir.dt.int32)
        iota = s.sb("iota", [P, P])
        best = s.sb("best", [P, 2, H, TOP])
        best_key = s.sb("best_key", [P, 2, H, TOP], U32)
        sums = s.sb("sums", [P, H, TOP, TOP])
        pick = s.sb("pick", [P, H, TOP])
        pick_at = s.sb("pick_at", [P, H, TOP], U32)
        rank = s.sb("rank", [P, 2, PICKS], U32)
        match = s.sb("match", [P, 2, PICKS, TOP])
        index = s.sb("index", [P, 2, PICKS], U32)
        high = s.sb("high", [P, 2, PICKS], U32)
        weight = s.sb("weight", [P, H, TOP])
        weight_sum = s.sb("weight_sum", [P, H])
        codes = s.sb("codes", [P, 3, 2, PICKS])
        codesT = s.sb("codesT", [P, 3, HALF])
        w_split = s.sb("w_split", [P, 2, HALF], F16)
        row_hot = [s.sb(f"row_hot{t}", [P, HALF, P], F16) for t in range(2)]
        col_hot = [s.sb(f"col_hot{t}", [P, 2, HALF, R], F16) for t in range(2)]
        sim_bank = [s.ps(f"sim{n}", [P, 512]) for n in range(2)]
        act_bank = [s.ps(f"act{n}", [P, 512]) for n in range(2)]
        g_bank = [s.ps(f"g{n}", [P, 512]) for n in range(2)]
        out_bank = s.ps("out", [P, 2, D])
        turn_bank = s.ps("turn", [P, 512])
        iota_made = s.sem("iota_made")
        iota_ready = s.sem("iota_ready")
        xb_ready = s.sem("xb_ready")
        sims_ready = s.sem("sims_ready")
        sims_used = s.sem("sims_used")
        weight_in = s.sem("weight_in")
        weight_exp = s.sem("weight_exp")
        codes_ready = s.sem("codes_ready")
        codes_turned = s.sem("codes_turned")
        codes_copied = s.sem("codes_copied")
        hot_ready = s.sem("hot_ready")
        g_ready = [s.sem(f"g_ready{q}") for q in range(2)]
        g_used = [s.sem(f"g_used{q}") for q in range(2)]
        act_ready = [s.sem(f"act_ready{q}") for q in range(2)]
        act_used = [s.sem(f"act_used{q}") for q in range(2)]
        out_ready = s.sem("out_ready")
        out_used = [s.sem(f"out_used{t}") for t in range(2)]
        PICK_LINKS, HOT_LINKS = 11, 3
        first_links = Chain(s.sem("first_links"))
        links = Chain(s.sem("links"), 2 * (PICK_LINKS + HOT_LINKS))
        block = s.block()

        @block.gpsimd
        def _(pool):
            pool.iota(ints[:, :], pattern=[[1, P]], base=0, channel_multiplier=0).then_inc(iota_made, 1)

        def batch_norm(act, n):
            for k in range(KD):
                last = act.activation(xbT[:, k, :], hT[:, k, bass.ds(n * 2 * P, 2 * P)], ACT.Identity,
                                      bias=bn_shift[:, k:k + 1], scale=bn_scale[:, k:k + 1])
            last.then_inc(xb_ready, 1)

        @block.tensor
        def _(pe):
            def similarities(i, t):
                n = 2 * i + t
                pe.wait_ge(xb_ready, i + 1)
                pe.wait_ge(sims_used, n)
                for ax in range(2):
                    for k in range(KD):
                        last = pe.matmul(sim_bank[ax][:, :], xbT[:, k, t * P:(t + 1) * P],
                                         fused[:, k, ax * 512:(ax + 1) * 512], start=(k == 0), stop=(k == KD - 1))
                last.then_inc(sims_ready, 1)

            def turn_codes(i, t):
                n = 2 * i + t
                pe.wait_ge(codes_ready, n + 1)
                pe.wait_ge(codes_copied, n)
                for m in range(3):
                    last = pe.transpose(turn_bank[:, m * P:(m + 1) * P],
                                        codes[:, m, :, :].rearrange("p a n -> p (a n)"), ident[:, :])
                last.then_inc(codes_turned, 1)

            similarities(0, 0)
            turn_codes(0, 0)
            similarities(0, 1)
            with pe.Fori(0, PAIRS) as i:
                def activations(u):
                    q = u % 2
                    pe.wait_ge(act_used[q], 8 * i + u // 2)
                    for j in range(2):
                        for k in range(KD):
                            last = pe.matmul(act_bank[q][:, j * 2 * P:(j + 1) * 2 * P], kiT[:, k, 2 * u + j, :],
                                             hT[:, k, bass.ds(i * 2 * P, 2 * P)], start=(k == 0), stop=(k == KD - 1))
                    last.then_inc(act_ready[q], 1)

                def weights(t):
                    n = 2 * i + t
                    pe.wait_ge(hot_ready, n + 1)
                    for m in range(GU):
                        for q in range(2):
                            rows = slice(q * HALF, (q + 1) * HALF)
                            pe.wait_ge(g_used[q], GU * n + m)
                            for j in range(GT):
                                for part in range(2):
                                    last = pe.matmul(g_bank[q][:, j * R:(j + 1) * R], row_hot[t][rows, GT * m + j, :],
                                                     col_hot[t][rows, part, GT * m + j, :],
                                                     start=(part == 0), stop=(part == 1))
                            last.then_inc(g_ready[q], 1)

                def outputs(t):
                    n = 2 * i + t
                    for q in range(2):
                        pe.wait_ge(g_used[q], GU * n + GU)
                    pe.wait_ge(out_used[t], i)
                    for r in range(R):
                        last = pe.matmul(out_bank[:, t, :], gel[:, r, t * P:(t + 1) * P], ko[:, r, :],
                                         start=(r == 0), stop=(r == R - 1))
                    last.then_inc(out_ready, 1)

                for u in range(4):
                    activations(u)
                turn_codes(i, 1)
                for u in range(4, 16):
                    activations(u)
                weights(0)
                similarities(i + 1, 0)
                outputs(0)
                turn_codes(i + 1, 0)
                weights(1)
                similarities(i + 1, 1)
                outputs(1)

        @block.scalar
        def _(act):
            def exponentials(i, t):
                n = 2 * i + t
                act.wait_ge(weight_in, n + 1)
                act.activation(weight[:, :, :], weight[:, :, :], ACT.Exp).then_inc(weight_exp, 1)

            batch_norm(act, 0)
            exponentials(0, 0)
            exponentials(0, 1)
            with act.Fori(0, PAIRS) as i:
                act.wait_ge(sims_ready, 2 * i + 2)
                batch_norm(act, i + 1)
                act.wait_ge(out_ready, 2 * i)
                for u in range(16):
                    q = u % 2
                    act.wait_ge(act_ready[q], 8 * i + u // 2 + 1)
                    act.activation(gel[:, 2 * u:2 * u + 2, :].rearrange("p r t -> p (r t)"), act_bank[q][:, :],
                                   ACT.Gelu).then_inc(act_used[q], 1)
                exponentials(i + 1, 0)
                exponentials(i + 1, 1)

        @block.vector
        def _(dve):
            def choose(chain, i, t):
                n = 2 * i + t
                dve.wait_ge(sims_ready, n + 1)
                dve.memset(spare[:, :], 0.0)
                for ax in range(2):
                    for h in range(H):
                        last = dve.max(best[:, ax, h, :], sim_bank[ax][:, h * NK:(h + 1) * NK])
                chain.link(dve, last)
                dve.memset(spare[:, :], 0.0)
                for ax in range(2):
                    for h in range(H):
                        last = dve.max_index(best_key[:, ax, h, :], best[:, ax, h, :],
                                             sim_bank[ax][:, h * NK:(h + 1) * NK])
                last.then_inc(sims_used, 1)
                chain.link(dve, dve.tensor_tensor(
                    sums[:, :, :, :], best[:, 0, :, :].unsqueeze(3).broadcast_to([P, H, TOP, TOP]),
                    best[:, 1, :, :].unsqueeze(2).broadcast_to([P, H, TOP, TOP]), ALU.add))
                dve.memset(spare[:, :], 0.0)
                for h in range(H):
                    last = dve.max(pick[:, h, :], sums[:, h, :, :].rearrange("p a b -> p (a b)"))
                chain.link(dve, last)
                dve.tensor_tensor(weight[:, :, :], pick[:, :, :], pick[:, :, 0:1].broadcast_to([P, H, TOP]),
                                  ALU.subtract).then_inc(weight_in, 1)
                for h in range(H):
                    last = dve.max_index(pick_at[:, h, :], pick[:, h, :], sums[:, h, :, :].rearrange("p a b -> p (a b)"))
                chain.link(dve, last)
                dve.tensor_single_scalar(rank[:, 0, :], pick_at[:, :, :].rearrange("p h k -> p (h k)"), 3,
                                         ALU.logical_shift_right)
                chain.link(dve, dve.tensor_single_scalar(rank[:, 1, :], pick_at[:, :, :].rearrange("p h k -> p (h k)"), 7,
                                                         ALU.bitwise_and))
                chain.link(dve, dve.tensor_tensor(
                    match[:, :, :, :].rearrange("p a n k -> p (a n) k"),
                    rank[:, :, :].rearrange("p a n -> p (a n)").unsqueeze(2).broadcast_to([P, 2 * PICKS, TOP]),
                    iota[:, 0:TOP].unsqueeze(1).broadcast_to([P, 2 * PICKS, TOP]), ALU.is_equal))
                mv4 = match[:, :, :, :].rearrange("p a (h n) k -> p (a h) n k", h=H)
                chain.link(dve, dve.tensor_tensor(
                    mv4, mv4, best_key[:, :, :, :].rearrange("p a h k -> p (a h) k").unsqueeze(2)
                    .broadcast_to([P, 2 * H, TOP, TOP]), ALU.mult))
                with nc.allow_low_precision(reason="one key below 64 and seven zeros: exact"):
                    chain.link(dve, dve.tensor_reduce(index[:, :, :].rearrange("p a n -> p (a n)"),
                                                      match[:, :, :, :].rearrange("p a n k -> p (a n) k"), AX.X, ALU.add))
                dve.tensor_scalar(high[:, 0, :], index[:, 1, :], 1, 6, ALU.bitwise_and, ALU.logical_shift_left)
                chain.link(dve, dve.tensor_single_scalar(high[:, 1, :], index[:, 1, :], 1, ALU.logical_shift_right))
                dve.wait_ge(codes_turned, n)
                for d in range(2):
                    dve.tensor_tensor(codes[:, 0, d, :], high[:, 0, :], index[:, 0, :], ALU.add)
                    dve.tensor_copy(codes[:, 1, d, :], high[:, 1, :])
                dve.wait_ge(weight_exp, n + 1)
                chain.link(dve, dve.tensor_reduce(weight_sum[:, :], weight[:, :, :], AX.X, ALU.add))
                chain.link(dve, dve.reciprocal(weight_sum[:, :], weight_sum[:, :]))
                for d in range(2):
                    last = dve.scalar_tensor_tensor(
                        codes[:, 2, d, :].rearrange("p (h k) -> p h k", h=H), weight[:, :, :], W_SCALE,
                        weight_sum[:, :].unsqueeze(2).broadcast_to([P, H, TOP]), ALU.mult, ALU.mult)
                last.then_inc(codes_ready, 1)

            def one_hot(chain, i, t):
                n = 2 * i + t
                dve.wait_ge(codes_turned, n + 1)
                turned = turn_bank[:, 0:3 * P].rearrange("p (m a t) -> p m a t", m=3, a=2)
                for q in range(2):
                    rows = slice(q * HALF, (q + 1) * HALF)
                    last = dve.tensor_copy(codesT[rows, :, :], turned[rows, :, q, :])
                last.then_inc(codes_copied, 1)
                dve.wait_ge(codes_copied, n + 1)
                if chain is not first_links:
                    dve.wait_ge(g_ready[1], GU * (n - 1))
                chain.link(dve, dve.tensor_copy(w_split[:, 0, :], codesT[:, 2, :]))
                dve.tensor_tensor(w_split[:, 1, :], codesT[:, 2, :], w_split[:, 0, :], ALU.subtract)
                match_r, w_low = col_hot[t][:, 0, :, :], col_hot[t][:, 1, :, :]
                chain.link(dve, dve.tensor_tensor(
                    match_r, codesT[:, 1, :].unsqueeze(2).broadcast_to([P, HALF, R]),
                    iota[:, 0:R].unsqueeze(1).broadcast_to([P, HALF, R]), ALU.is_equal))
                chain.link(dve, dve.tensor_tensor(
                    w_low, match_r, w_split[:, 1, :].unsqueeze(2).broadcast_to([P, HALF, R]), ALU.mult))
                dve.tensor_tensor(match_r, match_r, w_split[:, 0, :].unsqueeze(2).broadcast_to([P, HALF, R]), ALU.mult)
                dve.tensor_tensor(row_hot[t][:, :, :], codesT[:, 0, :].unsqueeze(2).broadcast_to([P, HALF, P]),
                                  iota[:, :].unsqueeze(1).broadcast_to([P, HALF, P]), ALU.is_equal).then_inc(hot_ready, 1)

            def apply_weights(i, t):
                n = 2 * i + t
                for q in range(2):
                    dve.wait_ge(act_used[q], 8 * i + 8)
                for m in range(GU):
                    for q in range(2):
                        t0 = t * P + q * HALF + GT * m
                        g = gel[:, :, t0:t0 + GT].rearrange("p r t -> p t r")
                        dve.wait_ge(g_ready[q], GU * n + m + 1)
                        dve.scalar_tensor_tensor(g, g_bank[q][:, :].rearrange("p (t r) -> p t r", r=R), 1.0 / W_SCALE, g,
                                                 ALU.mult, ALU.mult).then_inc(g_used[q], 1)

            def residual(i, t):
                dve.wait_ge(out_ready, 2 * i + t + 1)
                xb = x[:, bass.ds(2 * i + t, 1), :].rearrange("p a d -> p (a d)")
                dve.tensor_tensor(xb, out_bank[:, t, :], xb, ALU.add).then_inc(out_used[t], 1)

            dve.wait_ge(iota_made, 1)
            dve.tensor_copy(iota[:, :], ints[:, :]).then_inc(iota_ready, 1)
            dve.wait_ge(iota_ready, 1)
            choose(first_links, 0, 0)
            one_hot(first_links, 0, 0)
            choose(first_links, 0, 1)
            with dve.Fori(0, PAIRS) as i:
                links.begin(i)
                one_hot(links, i, 1)
                apply_weights(i, 0)
                choose(links, i + 1, 0)
                residual(i, 0)
                apply_weights(i, 1)
                one_hot(links, i + 1, 0)
                choose(links, i + 1, 1)
                residual(i, 1)
                links.end()


def stage_experts(nc, x, ident, ones_row, gate_w, gate_b, w_gate, w_up, w_down, s_gate, s_up, s_down):
    NE = 16
    TOP = 8
    ROUTE_SCALE = 2.826
    HID = 256
    TOKENS = NB * P
    GROUP = 512
    GROUPS = TOKENS // GROUP
    TAKEN = -3.0e38
    with ExitStack() as ctx:
        s = Scope(nc, ctx, "m")
        gw = s.sb("gw", [NE, D])
        gwT = s.sb("gwT", [P, KD, NE])
        gb_row = s.sb("gb_row", [1, NE])
        gate_bias = s.sb("gate_bias", [P, NE])
        xnT_pair = s.sb("xnT_pair", [P, KD, 2 * P])
        xnT = s.sb("xnT", [P, KD, TOKENS])
        score = s.sb("score", [P, 2, NE])
        chosen_by = s.sb("chosen_by", [P, 2, NE])
        top = s.sb("top", [P, 2, TOP])
        left = s.sb("left", [P, 2, NE])
        total = s.sb("total", [P, 2])
        combine = s.sb("combine", [P, NB, NE + 1])
        w_nat = s.sb("w_nat", [P, 6, D])
        wT = [s.sb(f"wT{n}", [P, 3, KD, HID]) for n in range(2)]
        silu = s.sb("silu", [P, 2, GROUP])
        hidden = s.sb("hidden", [P, 2, 2, GROUP])
        ln = LayerNorm(s, x, None)
        gate_bank = [s.ps(f"gate{n}", [P, GROUP]) for n in range(2)]
        up_bank = [s.ps(f"up{n}", [P, GROUP]) for n in range(2)]
        y_bank = [s.ps(f"y{n}", [P, 2 * D]) for n in range(2)]
        turn_bank = s.ps("turn", [P, 512])
        route_bank = s.ps("route", [P, 512])
        loaded = s.sem("loaded")
        gate_T = s.sem("gate_T")
        gate_T_copied = s.sem("gate_T_copied")
        ones_set = s.sem("ones_set")
        pair_turned = s.sem("pair_turned")
        pair_copied = s.sem("pair_copied")
        all_copied = s.sem("all_copied")
        logits_ready = s.sem("logits_ready")
        logits_exp = s.sem("logits_exp")
        routed = s.sem("routed")
        w_loaded = s.sem("w_loaded")
        w_turned = s.sem("w_turned")
        w_copied = s.sem("w_copied")
        gate_ready = [s.sem(f"gate_ready{n}") for n in range(2)]
        up_ready = [s.sem(f"up_ready{n}") for n in range(2)]
        silu_ready = [s.sem(f"silu_ready{n}") for n in range(2)]
        hidden_ready = [s.sem(f"hidden_ready{n}") for n in range(2)]
        y_ready = [s.sem(f"y_ready{n}") for n in range(2)]
        y_added = [s.sem(f"y_added{n}") for n in range(2)]
        links = Chain(s.sem("links"), 2 + 9)
        block = s.block()
        UN = GROUPS

        @block.sync
        def _(sp):
            sp.dma_start(gw[:, :], gate_w).then_inc(loaded, 16)
            sp.dma_start(gb_row[:, :], gate_b.rearrange("(a d) -> a d", a=1)).then_inc(loaded, 16)

            def load(n, parts):
                if n is not None:
                    sp.wait_ge(w_turned, n)
                for m, w in enumerate(parts):
                    sp.dma_start(w_nat[:, 2 * m:2 * m + 2, :], w.rearrange("(t p) n -> p t n", p=P)).then_inc(w_loaded, 16)

            load(None, (w_gate[0], w_up[0], w_down[0]))
            with sp.Fori(1, NE) as e:
                load(3 * e, [w[bass.ds(e, 1), :, :].rearrange("a o n -> (a o) n") for w in (w_gate, w_up, w_down)])
            load(3 * NE, (s_gate, s_up, s_down))
            sp.wait_ge(w_loaded, 48 * (NE + 1))

        @block.gpsimd
        def _(pool):
            ln.setup(pool)
            pool.memset(combine[:, :, NE:NE + 1], 1.0).then_inc(ones_set, 1)
            with pool.Fori(0, PAIRS) as i:
                ln.root(pool, i)

        def turn_weights(pe, e, m):
            pe.wait_ge(w_loaded, 48 * e + 16 * 3)
            pe.wait_ge(w_copied, 3 * e + m)
            for k in range(KD):
                for t in range(2):
                    last = pe.transpose(turn_bank[:, k * HID + t * P:k * HID + (t + 1) * P],
                                        w_nat[:, 2 * m + t, k * P:(k + 1) * P], ident[:, :])
            last.then_inc(w_turned, 1)

        def expert_on_pe(pe, e, par, last_one=False):
            w = wT[par]
            pe.wait_ge(w_copied, 3 * e + 3)

            def hidden_unit(g, m):
                pe.wait_ge(silu_ready[m], UN * e + g)
                for k in range(KD):
                    last = pe.matmul(gate_bank[m][:, :], w[:, 0, k, m * P:(m + 1) * P],
                                     xnT[:, k, g * GROUP:(g + 1) * GROUP], start=(k == 0), stop=(k == KD - 1))
                last.then_inc(gate_ready[m], 1)
                pe.wait_ge(hidden_ready[m], UN * e + g)
                for k in range(KD):
                    last = pe.matmul(up_bank[m][:, :], w[:, 1, k, m * P:(m + 1) * P],
                                     xnT[:, k, g * GROUP:(g + 1) * GROUP], start=(k == 0), stop=(k == KD - 1))
                last.then_inc(up_ready[m], 1)

            def down(g):
                for m in range(2):
                    pe.wait_ge(hidden_ready[m], UN * e + g + 1)
                for n in range(2):
                    pe.wait_ge(y_added[n], UN * e + g)
                    for t in range(2):
                        for k in range(2):
                            last = pe.matmul(y_bank[n][:, t * D:(t + 1) * D],
                                             hidden[:, g % 2, k, (2 * n + t) * P:(2 * n + t + 1) * P],
                                             w[:, 2, k, :], start=(k == 0), stop=(k == 1))
                    last.then_inc(y_ready[n], 1)

            for g in range(GROUPS):
                hidden_unit(g, 0)
                hidden_unit(g, 1)
                if g >= 1:
                    down(g - 1)
                if g < 3 and not last_one:
                    turn_weights(pe, e + 1, g)
            down(GROUPS - 1)

        @block.tensor
        def _(pe):
            pe.wait_ge(loaded, 32)
            for k in range(KD):
                last = pe.transpose(gate_bank[0][:, k * NE:(k + 1) * NE], gw[:, k * P:(k + 1) * P], ident[0:NE, 0:NE])
            last.then_inc(gate_T, 1)
            pe.matmul(gate_bank[1][:, 0:NE], ones_row[:, :], gb_row[:, :], start=True, stop=True).then_inc(gate_T, 1)
            for m in range(3):
                turn_weights(pe, 0, m)
            pe.wait_ge(gate_T_copied, 2)
            with pe.Fori(0, PAIRS) as i:
                pe.wait_ge(pair_copied, i)
                pe.wait_ge(all_copied, i)
                ln.transposed(pe, up_bank[0], ident, i).then_inc(pair_turned, 1)
                pe.wait_ge(pair_copied, i + 1)
                for b in range(2):
                    for k in range(KD):
                        last = pe.matmul(route_bank[:, b * NE:(b + 1) * NE], xnT_pair[:, k, b * P:(b + 1) * P],
                                         gwT[:, k, :], start=(k == 0), stop=(k == KD - 1))
                last.then_inc(logits_ready, 1)
                pe.wait_ge(logits_exp, i + 1)
            pe.wait_ge(all_copied, PAIRS)
            with pe.Fori(0, NE // 2) as h:
                for par in range(2):
                    expert_on_pe(pe, 2 * h + par, par)
            expert_on_pe(pe, NE, 0, last_one=True)

        @block.scalar
        def _(act):
            def copy_weights(e, par, m):
                act.wait_ge(w_turned, 3 * e + m + 1)
                act.copy(wT[par][:, m, :, :].rearrange("p k n -> p (k n)"), turn_bank[:, :]).then_inc(w_copied, 1)

            for m in range(3):
                copy_weights(0, 0, m)
            with act.Fori(0, PAIRS) as i:
                act.wait_ge(pair_turned, i + 1)
                act.copy(xnT_pair[:, :, :].rearrange("p k t -> p (k t)"), up_bank[0][:, :]).then_inc(pair_copied, 1)
                act.wait_ge(logits_ready, i + 1)
                act.wait_ge(routed, i)
                act.activation(score[:, :, :].rearrange("p b e -> p (b e)"), route_bank[:, 0:2 * NE], ACT.Exp,
                               scale=-1.0).then_inc(logits_exp, 1)

            def expert_on_act(e, par, last_one=False):
                for g in range(GROUPS):
                    for m in range(2):
                        act.wait_ge(gate_ready[m], UN * e + g + 1)
                        act.wait_ge(hidden_ready[m], UN * e + g)
                        act.activation(silu[:, m, :], gate_bank[m][:, :], ACT.Silu).then_inc(silu_ready[m], 1)
                    if g < 3 and not last_one:
                        if g == 0:
                            act.wait_ge(y_added[1], UN * e)
                        copy_weights(e + 1, 1 - par, g)

            with act.Fori(0, NE // 2) as h:
                for par in range(2):
                    expert_on_act(2 * h + par, par)
            expert_on_act(NE, 0, last_one=True)

        @block.vector
        def _(dve):
            dve.wait_ge(gate_T, 2)
            dve.tensor_copy(gwT[:, :, :].rearrange("p k n -> p (k n)"), gate_bank[0][:, 0:KD * NE]).then_inc(gate_T_copied, 1)
            dve.tensor_copy(gate_bias[:, :], gate_bank[1][:, 0:NE]).then_inc(gate_T_copied, 1)
            dve.wait_ge(gate_T_copied, 2)
            with dve.Fori(0, PAIRS) as i:
                links.begin(i)
                ln.statistics(dve, links, i)
                dve.wait_ge(pair_turned, i)
                ln.apply(dve, i)
                dve.wait_ge(pair_copied, i + 1)
                dve.tensor_copy(xnT[:, :, bass.ds(i * 2 * P, 2 * P)],
                                up_bank[0][:, :].rearrange("p (k t) -> p k t", k=KD)).then_inc(all_copied, 1)
                dve.wait_ge(logits_exp, i + 1)
                links.link(dve, dve.tensor_scalar(score[:, :, :], score[:, :, :], 1.0, None, ALU.add))
                links.link(dve, dve.reciprocal(score[:, :, :], score[:, :, :]))
                links.link(dve, dve.tensor_tensor(chosen_by[:, :, :], score[:, :, :],
                                                  gate_bias[:, :].unsqueeze(1).broadcast_to([P, 2, NE]), ALU.add))
                ln.nudge(dve)
                for b in range(2):
                    last = dve.max(top[:, b, :], chosen_by[:, b, :])
                links.link(dve, last)
                ln.nudge(dve)
                for b in range(2):
                    last = dve.match_replace(left[:, b, :], top[:, b, :], chosen_by[:, b, :], TAKEN)
                links.link(dve, last)
                links.link(dve, dve.tensor_tensor(left[:, :, :], left[:, :, :], chosen_by[:, :, :], ALU.not_equal))
                links.link(dve, dve.tensor_tensor(score[:, :, :], score[:, :, :], left[:, :, :], ALU.mult))
                links.link(dve, dve.tensor_reduce(total[:, :], score[:, :, :], AX.X, ALU.add))
                links.link(dve, dve.reciprocal(total[:, :], total[:, :]))
                for b in range(2):
                    last = dve.tensor_scalar(combine[:, bass.ds(2 * i + b, 1), 0:NE].rearrange("p a e -> p (a e)"),
                                             score[:, b, :], total[:, b:b + 1], ROUTE_SCALE, ALU.mult, ALU.mult)
                last.then_inc(routed, 1)
                links.end()
            dve.wait_ge(routed, PAIRS)
            dve.wait_ge(ones_set, 1)

            def expert_on_dve(e):
                def add(g):
                    for n in range(2):
                        dve.wait_ge(y_ready[n], UN * e + g + 1)
                        for t in range(2):
                            tile = 4 * g + 2 * n + t
                            weight = combine[:, tile, bass.ds(e, 1)] if not isinstance(e, int) else combine[:, tile, e:e + 1]
                            last = dve.scalar_tensor_tensor(x[:, tile, :], y_bank[n][:, t * D:(t + 1) * D], weight,
                                                            x[:, tile, :], ALU.mult, ALU.add)
                        last.then_inc(y_added[n], 1)

                for g in range(GROUPS):
                    for m in range(2):
                        dve.wait_ge(silu_ready[m], UN * e + g + 1)
                        dve.wait_ge(up_ready[m], UN * e + g + 1)
                        dve.tensor_tensor(hidden[:, g % 2, m, :], silu[:, m, :], up_bank[m][:, :], ALU.mult) \
                            .then_inc(hidden_ready[m], 1)
                    if g >= 1:
                        add(g - 1)
                add(GROUPS - 1)

            with dve.Fori(0, NE // 2) as h:
                for par in range(2):
                    expert_on_dve(2 * h + par)
            expert_on_dve(NE)


def stage_constants(nc, ident, ident_bf, causal_bf, chunk_bf, ones_row, par_mask):
    with ExitStack() as ctx:
        s = Scope(nc, ctx, "c")
        zeroed = s.sem("zeroed")
        made = s.sem("made")
        block = s.block()

        @block.gpsimd
        def _(pool):
            pool.memset(ident[:, :], 0.0).then_inc(zeroed, 1)
            pool.memset(ident_bf[:, :], 0.0).then_inc(zeroed, 1)
            pool.memset(causal_bf[:, :], 0.0).then_inc(zeroed, 1)
            pool.memset(chunk_bf[:, :], 0.0).then_inc(zeroed, 1)
            pool.memset(ones_row[:, :], 1.0).then_inc(zeroed, 1)
            pool.memset(par_mask[:, :], 0.25).then_inc(zeroed, 1)
            pool.wait_ge(zeroed, 6)
            for m in (ident, ident_bf):
                pool.affine_select(out=m[:, :], in_=m[:, :], compare_op=ALU.not_equal, fill=1.0, base=0,
                                   pattern=[[-1, P]], channel_multiplier=1).then_inc(made, 1)
            pool.affine_select(out=causal_bf[:, :], in_=causal_bf[:, :], compare_op=ALU.is_ge, fill=NEG, base=0,
                               pattern=[[0, 4], [-1, P]], channel_multiplier=1).then_inc(made, 1)
            cv = chunk_bf[:, :].rearrange("p (j c k) -> p j c k", j=4, c=2)
            pool.affine_select(out=cv[:, :, 0, :], in_=cv[:, :, 0, :], compare_op=ALU.is_ge, fill=NEG, base=63,
                               pattern=[[0, 4], [0, 64]], channel_multiplier=-1).then_inc(made, 1)
            pool.affine_select(out=cv[:, :, 1, :], in_=cv[:, :, 1, :], compare_op=ALU.is_ge, fill=NEG, base=-64,
                               pattern=[[0, 4], [0, 64]], channel_multiplier=1).then_inc(made, 1)
            pool.wait_ge(made, 5)
            for slot in range(4):
                for col, lo in ((0, 32 * slot + 16), (1, 32 * slot)):
                    pool.affine_select(out=par_mask[:, 2 + 2 * slot + col:3 + 2 * slot + col],
                                       in_=par_mask[:, 2 + 2 * slot + col:3 + 2 * slot + col],
                                       compare_op=ALU.is_ge, fill=0.0, base=-lo, pattern=[[0, 1]],
                                       channel_multiplier=1).then_inc(made, 1)
            pool.wait_ge(made, 13)
            for slot in range(4):
                for col, lo in ((0, 32 * slot + 16), (1, 32 * slot)):
                    pool.affine_select(out=par_mask[:, 2 + 2 * slot + col:3 + 2 * slot + col],
                                       in_=par_mask[:, 2 + 2 * slot + col:3 + 2 * slot + col],
                                       compare_op=ALU.is_ge, fill=0.0, base=lo + 15, pattern=[[0, 1]],
                                       channel_multiplier=-1).then_inc(made, 1)

        @block.vector
        def _(dve):
            dve.wait_ge(made, 21)
            blocks = par_mask[:, 2:10].rearrange("p (s c) -> p c s", c=2)
            dve.tensor_reduce(par_mask[:, 10:12], blocks, AX.X, ALU.add).then_inc(made, 1)
            dve.wait_ge(made, 22)
            dve.tensor_tensor(par_mask[:, 0:2], par_mask[:, 0:2], par_mask[:, 10:12], ALU.subtract).then_inc(made, 1)


def decoder(nc, out, a):
    with ExitStack() as ctx:
        s = Scope(nc, ctx, "g")
        x = s.sb("x", [P, NB + 2, D])
        ident = s.sb("ident", [P, P])
        ident_bf = s.sb("ident_bf", [P, P], BF16)
        causal_bf = s.sb("causal_bf", [P, 4 * P], BF16)
        chunk_bf = s.sb("chunk_bf", [P, 4 * P], BF16)
        ones_row = s.sb("ones_row", [1, P])
        par_mask = s.sb("par_mask", [P, 12])
        stored = s.sem("stored")
        stage_constants(nc, ident, ident_bf, causal_bf, chunk_bf, ones_row, par_mask)
        stage_causal_attention(nc, x, ident, ones_row, ident_bf, causal_bf, a["x"], a["L0_attn_w_q"],
                               a["L0_attn_w_k"], a["L0_attn_w_v"], a["L0_attn_w_u"], a["L0_attn_b_u"])
        stage_chunked_attention(nc, x, ident, ones_row, ident_bf, chunk_bf, par_mask, a["ctx_1024"],
                                a["L0_xattn_in_proj_w"], a["L0_xattn_in_proj_b"], a["L0_xattn_out_proj_w"],
                                a["L0_xattn_out_proj_b"])
        stage_product_keys(nc, x, ident, a["L0_ffn_gamma"], a["L0_ffn_beta"], a["L0_ffn_w_q"], a["L0_ffn_keys"],
                           a["L0_ffn_key_in"], a["L0_ffn_key_out"])
        stage_gated_attention(nc, x, ident, ones_row, par_mask, a["L1_attn_Wq"], a["L1_attn_bq"],
                              a["L1_attn_Wk"], a["L1_attn_bk"], a["L1_attn_Wv"], a["L1_attn_bv"],
                              a["L1_attn_Wo"], a["L1_attn_bo"], a["L1_attn_g"], a["L1_attn_Wg1"],
                              a["L1_attn_bg1"], a["L1_attn_Wg2"], a["L1_attn_bg2"])
        stage_aligned_attention(nc, x, ident, ones_row, a["ctx_1024"], a["L1_xattn_W"], a["L1_xattn_b"])
        stage_experts(nc, x, ident, ones_row, a["L1_ffn_gate_w"], a["L1_ffn_expert_bias"], a["L1_ffn_w_gate"],
                      a["L1_ffn_w_up"], a["L1_ffn_w_down"], a["L1_ffn_shared_gate_w"],
                      a["L1_ffn_shared_up_w"], a["L1_ffn_shared_down_w"])
        block = s.block()

        @block.sync
        def _(sp):
            sp.dma_start(out.rearrange("b t d -> t b d"), x[:, 0:NB, :]).then_inc(stored, 16)
            sp.wait_ge(stored, 16)


_INS = ['x', 'ctx_1024', 'L0_attn_w_q', 'L0_attn_w_k', 'L0_attn_w_v', 'L0_attn_w_u', 'L0_attn_b_u',
        'L0_xattn_in_proj_w', 'L0_xattn_in_proj_b', 'L0_xattn_out_proj_w', 'L0_xattn_out_proj_b',
        'L0_ffn_gamma', 'L0_ffn_beta', 'L0_ffn_w_q', 'L0_ffn_keys', 'L0_ffn_key_in', 'L0_ffn_key_out',
        'L1_attn_Wq', 'L1_attn_bq', 'L1_attn_Wk', 'L1_attn_bk', 'L1_attn_Wv', 'L1_attn_bv', 'L1_attn_Wo',
        'L1_attn_bo', 'L1_attn_g', 'L1_attn_Wg1', 'L1_attn_bg1', 'L1_attn_Wg2', 'L1_attn_bg2',
        'L1_xattn_W', 'L1_xattn_b', 'L1_ffn_gate_w', 'L1_ffn_expert_bias', 'L1_ffn_w_gate', 'L1_ffn_w_up',
        'L1_ffn_w_down', 'L1_ffn_shared_gate_w', 'L1_ffn_shared_up_w', 'L1_ffn_shared_down_w']


def kernel(**inputs):
    import numpy as np
    from concourse import bacc
    from concourse.bass_utils import run_bass_kernel_spmd

    nc = bacc.Bacc("TRN2", target_bir_lowering=False, num_devices=1)
    arrays, args = {}, {}
    for name in _INS:
        a = np.ascontiguousarray(inputs[name])
        arrays[f"in_{name}"] = a
        args[name] = nc.dram_tensor(f"in_{name}", a.shape, mybir.dt.from_np(a.dtype), kind="ExternalInput").ap()
    out = nc.dram_tensor("out", (NB, P, D), F32, kind="ExternalOutput").ap()
    decoder(nc, out, args)
    r = run_bass_kernel_spmd(nc, [arrays], core_ids=[0])
    return r.results[0]["out"]
```

```python
from contextlib import ExitStack

import concourse.bass as bass
from concourse import mybir

P = 128
D = 256
KD = D // P
NB = 16
PAIRS = NB // 2
NH = 16
UNITS = 8
LN_EPS = 1e-5
NEG = -1.0e30

ALU = mybir.AluOpType
ACT = mybir.ActivationFunctionType
AX = mybir.AxisListType
F32 = mybir.dt.float32
BF16 = mybir.dt.bfloat16
F16 = mybir.dt.float16
U32 = mybir.dt.uint32


class Signal:

    def __init__(self, sem, per):
        self.sem, self.per = sem, per

    def at(self, i, k):
        return self.per * i + k


class Chain:

    def __init__(self, sem, per=None, ahead=0):
        self.sem, self.per, self.ahead, self.i, self.k = sem, per, ahead, 0, 0

    def begin(self, i):
        self.i, self.k = i, self.ahead

    def link(self, eng, ins):
        self.k += 1
        ins.then_inc(self.sem, 1)
        eng.wait_ge(self.sem, (self.per or 0) * self.i + self.k)

    def end(self):
        assert self.per is None or self.k == self.per + self.ahead, (self.k, self.per, self.ahead)


class Scope:

    def __init__(self, nc, ctx, tag):
        self.nc, self.ctx, self.tag, self.sems = nc, ctx, tag, []

    def sb(self, name, shape, dt=F32):
        return self.ctx.enter_context(self.nc.sbuf_tensor(f"{self.tag}_{name}", shape, dt))

    def ps(self, name, shape, dt=F32):
        return self.ctx.enter_context(self.nc.psum_tensor(f"{self.tag}_{name}", shape, dt))

    def sem(self, name):
        sem = self.ctx.enter_context(self.nc.semaphore(f"{self.tag}_{name}"))
        self.sems.append(sem)
        return sem

    def _clear(self):
        for sem in self.sems:
            self.nc.sync.sem_clear(sem)
        self.nc.all_engine_barrier()

    def block(self):
        self.ctx.callback(self._clear)
        return self.ctx.enter_context(self.nc.Block())


class LayerNorm:

    def __init__(self, s, x):
        self.x = x
        self.links = Chain(s.sem("ln_links"), 2)
        self.stats = s.sb("ln_stats", [P, 2, 6])
        self.mv = s.sb("ln_mv", [P, 2, 2])
        self.var_eps = s.sb("ln_var_eps", [P, 2])
        self.rstd = s.sb("ln_rstd", [P, 2])
        self.power = s.sb("ln_power", [P, 2])
        self.xn = s.sb("ln_xn", [P, 2, D])
        self.spare = s.sb("ln_spare", [1, 1])
        self.var_ready = s.sem("ln_var_ready")
        self.rstd_ready = s.sem("ln_rstd_ready")
        self.xn_ready = s.sem("ln_xn_ready")
        self.power_set = s.sem("ln_power_set")

    def setup(self, pool):
        pool.memset(self.power[:, :], -0.5).then_inc(self.power_set, 1)
        pool.wait_ge(self.power_set, 1)

    def statistics(self, dve, n):
        chain = self.links
        chain.begin(n)
        for b in range(2):
            last = dve.bn_stats(self.stats[:, b, :], self.x[:, bass.ds(2 * n + b, 1), :].rearrange("p a d -> p (a d)"))
        chain.link(dve, last)
        self.nudge(dve)
        for b in range(2):
            last = dve.bn_aggr(self.mv[:, b, :], self.stats[:, b, :])
        chain.link(dve, last)
        dve.tensor_scalar(self.var_eps[:, :], self.mv[:, :, 1], LN_EPS, None, ALU.add).then_inc(self.var_ready, 1)

    def nudge(self, dve):
        dve.memset(self.spare[:, :], 0.0)

    def root(self, pool, n):
        pool.wait_ge(self.var_ready, n + 1)
        pool.tensor_tensor(self.rstd[:, :], self.var_eps[:, :], self.power[:, :], ALU.pow).then_inc(self.rstd_ready, 1)

    def apply(self, dve, n):
        dve.wait_ge(self.rstd_ready, n + 1)
        for b in range(2):
            last = dve.tensor_scalar(self.xn[:, b, :], self.x[:, bass.ds(2 * n + b, 1), :].rearrange("p a d -> p (a d)"),
                                     self.mv[:, b, 0:1], self.rstd[:, b:b + 1], ALU.subtract, ALU.mult)
        last.then_inc(self.xn_ready, 1)

    def transposed(self, pe, bank, ident, n, one=None):
        pe.wait_ge(self.xn_ready, n + 1)
        for m, b in enumerate(range(2) if one is None else (one,)):
            for k in range(KD):
                at = (k * 2 + m) * P if one is None else k * P
                last = pe.transpose(bank[:, at:at + P], self.xn[:, b, k * P:(k + 1) * P], ident[:, :])
        return last


class HeadAttention:

    def __init__(self, s, head_dim, ident, mask, attnT, gated=False, vector_copies=()):
        self.ident, self.mask, self.attnT, self.vector_copies = ident, mask, attnT, vector_copies
        per_unit = 2 if gated else 1
        self.links = Chain(s.sem("att_links"), per_unit * UNITS, ahead=per_unit)
        self.rows = 64 if head_dim == 64 else 32
        self.tile_heads = P // head_dim
        self.chunk_units = 2 if head_dim == 64 else 4
        self.chunks = UNITS // self.chunk_units
        self.score_bank = [s.ps(f"score{n}", [P, 512]) for n in range(2)]
        self.probT_bank = [s.ps(f"probT_bank{n}", [P, 512]) for n in range(2)]
        self.out_bank = s.ps("out_bank", [P, 512])
        self.neg_max = s.sb("neg_max", [P, UNITS, 4])
        self.row_sum = s.sb("row_sum", [P, UNITS, 4])
        self.norm = s.sb("norm", [P, UNITS, 4])
        self.prob = s.sb("prob", [P, 4, 4, P])
        self.probT = s.sb("probT", [P, 2, 4 * P])
        self.scored = Signal(s.sem("scored"), UNITS)
        self.max_ready = Signal(s.sem("max_ready"), UNITS)
        self.exp_ready = Signal(s.sem("exp_ready"), UNITS)
        self.normed = Signal(s.sem("normed"), UNITS)
        self.transposed = Signal(s.sem("transposed"), UNITS)
        self.probT_ready = [Signal(s.sem(f"probT_ready{n}"), UNITS // 2) for n in range(2)]
        self.weighted = Signal(s.sem("weighted"), UNITS)
        self.out_ready = Signal(s.sem("out_ready"), self.chunks + 1)
        self.projected = s.sem("projected")

    def pe_scores(self, pe, i, u, par, scores, first=False):
        b, g, n = u // 4, u % 4, u % 2
        if not first:
            pe.wait_ge(self.exp_ready.sem, self.exp_ready.at(i, u - 1))
        if self.mask is not None:
            ident_bf, mask_bf = self.mask
            pe.matmul(self.score_bank[n][:, :], ident_bf[:, :], mask_bf[:, :], start=True, stop=False,
                      skip_group_check=True)
        scores(par, self.score_bank[n], b, g, self.mask is None).then_inc(self.scored.sem, 1)

    def dve_max(self, dve, i, u):
        dve.wait_ge(self.scored.sem, self.scored.at(i, u + 1))
        dve.tensor_reduce(self.neg_max[:, u, :], self.score_bank[u % 2][:, :].rearrange("p (j k) -> p j k", j=4),
                          AX.X, ALU.max, negate=True).then_inc(self.max_ready.sem, 1)

    def act_exp(self, act, i, u, first=False):
        act.wait_ge(self.max_ready.sem, self.max_ready.at(i, u + 1))
        if not first:
            act.wait_ge(self.transposed.sem, self.transposed.at(i, u - 3 if u != 2 else 0))
        for j in range(4):
            last = act.activation(self.prob[:, u % 4, j, :], self.score_bank[u % 2][:, j * P:(j + 1) * P], ACT.Exp,
                                  bias=self.neg_max[:, u, j:j + 1], accum_out=self.row_sum[:, u, j:j + 1])
        last.then_inc(self.exp_ready.sem, 1)

    def dve_normalise(self, dve, i, u, par, gate):
        n = u % 4
        dve.wait_ge(self.exp_ready.sem, self.exp_ready.at(i, u + 1))
        self.links.link(dve, dve.reciprocal(self.norm[:, u, :], self.row_sum[:, u, :]))
        if gate is not None:
            self.links.link(dve, dve.tensor_tensor(self.norm[:, u, :], self.norm[:, u, :], gate(par, u // 4, u % 4), ALU.mult))
        for j in range(4):
            last = dve.tensor_scalar(self.prob[:, n, j, :], self.prob[:, n, j, :], self.norm[:, u, j:j + 1], None,
                                     ALU.mult)
        last.then_inc(self.normed.sem, 1)

    def pe_transpose(self, pe, i, u):
        pe.wait_ge(self.normed.sem, self.normed.at(i, u + 1))
        before = self.probT_ready[u % 2]
        pe.wait_ge(before.sem, before.at(i, u // 2))
        for j in range(4):
            last = pe.transpose(self.probT_bank[u % 2][:, j * P:(j + 1) * P], self.prob[:, u % 4, j, :], self.ident[:, :])
        last.then_inc(self.transposed.sem, 1)

    def copy_probT(self, eng, i, u, copy):
        eng.wait_ge(self.transposed.sem, self.transposed.at(i, u + 1))
        eng.wait_ge(self.weighted.sem, self.weighted.at(i, max(u - 1, 0)))
        copy(self.probT[:, u % 2, :], self.probT_bank[u % 2][:, :]).then_inc(self.probT_ready[u % 2].sem, 1)

    def pe_weighted(self, pe, i, u, par, v_ap):
        b, g = u // 4, u % 4
        ready = self.probT_ready[u % 2]
        pe.wait_ge(ready.sem, ready.at(i, u // 2 + 1))
        if u % self.chunk_units == 0:
            pe.wait_ge(self.out_ready.sem, self.out_ready.at(i, u // self.chunk_units))
        for j in range(4):
            h = 4 * g + j
            shared = self.rows == 32
            row = 64 * (h % 2) if not shared else 32 * ((h % self.tile_heads) // 2)
            col = (h // self.tile_heads) % (2 * self.chunk_units if not shared else 2)
            last = pe.matmul(self.out_bank[row:row + self.rows, col * P:(col + 1) * P], v_ap(par, b, h),
                             self.probT[:, u % 2, j * P:(j + 1) * P], start=not shared or h % 2 == 0,
                             stop=not shared or h % 2 == 1)
        last.then_inc(self.weighted.sem, 1)

    def copy_out(self, copy, eng, i, c):
        eng.wait_ge(self.weighted.sem, self.weighted.at(i, (c + 1) * self.chunk_units))
        dst = self.attnT(c)
        copy(dst, self.out_bank[:, 0:dst.shape[1]]).then_inc(self.out_ready.sem, 1)


    def pe_first(self, pe, scores):
        self.pe_scores(pe, 0, 0, 0, scores, first=True)
        self.pe_scores(pe, 0, 1, 0, scores, first=True)

    def on_pe(self, pe, i, par, scores, v_ap, before, after):
        for u in range(UNITS):
            before(u)
            if u + 2 < UNITS:
                self.pe_scores(pe, i, u + 2, par, scores)
            else:
                self.pe_scores(pe, i + 1, u + 2 - UNITS, 1 - par, scores)
            self.pe_transpose(pe, i, u)
            if u >= 1:
                self.pe_weighted(pe, i, u - 1, par, v_ap)
            after(u)
        self.pe_weighted(pe, i, UNITS - 1, par, v_ap)

    def pe_project(self, pe, i, terms, ones_row, bias):
        pe.wait_ge(self.out_ready.sem, self.out_ready.at(i, self.chunks))
        for b in range(2):
            dst = self.out_bank[:, b * D:(b + 1) * D]
            for n, (a, w) in enumerate(terms(b)):
                pe.matmul(dst, a, w, start=(n == 0), stop=False)
            last = pe.matmul(dst, ones_row[:, :], bias[:, :], start=False, stop=True)
        last.then_inc(self.projected, 1)

    def dve_residual(self, dve, i, x):
        dve.wait_ge(self.projected, i + 1)
        pair = x[:, bass.ds(2 * i, 2), :]
        dve.tensor_tensor(pair, self.out_bank[:, :].rearrange("p (b d) -> p b d", b=2), pair, ALU.add) \
            .then_inc(self.out_ready.sem, 1)

    def act_first(self, act):
        self.act_exp(act, 0, 0, first=True)
        self.act_exp(act, 0, 1, first=True)

    def on_act(self, act, i, before, after):
        for u in range(UNITS):
            before(u)
            if u + 2 < UNITS:
                self.act_exp(act, i, u + 2)
            else:
                self.act_exp(act, i + 1, u + 2 - UNITS)
            if u not in self.vector_copies:
                self.copy_probT(act, i, u, act.copy)
            after(u)

    def dve_first(self, dve, gate=None):
        self.dve_max(dve, 0, 0)
        self.dve_max(dve, 0, 1)
        self.dve_normalise(dve, 0, 0, 0, gate)

    def on_dve(self, dve, i, par, before, after, gate=None):
        self.links.begin(i)
        for u in range(UNITS):
            before(u)
            if u + 2 < UNITS:
                self.dve_max(dve, i, u + 2)
            else:
                self.dve_max(dve, i + 1, u + 2 - UNITS)
            if u + 1 < UNITS:
                self.dve_normalise(dve, i, u + 1, par, gate)
            else:
                self.dve_normalise(dve, i + 1, 0, 1 - par, gate)
            if u in self.vector_copies:
                self.copy_probT(dve, i, u, dve.tensor_copy)
            if u >= 1 and u % self.chunk_units == 0:
                self.copy_out(dve.tensor_copy, dve, i, u // self.chunk_units - 1)
            after(u)
        self.copy_out(dve.tensor_copy, dve, i, self.chunks - 1)
        self.links.end()


def stage_causal_attention(nc, x, ident, ones_row, ident_bf, mask_bf, half_mask, x_in, w_q, w_k, w_v, w_u, b_u):
    HD = 64
    HW = NH * HD
    MT = HW // P
    QK_SCALE = 1.0 / HD
    SLOTS = 14
    AFTER = {0: (2, 3), 1: (4, 5), 2: (6, 7), 3: (8, 9), 5: (10, 11), 7: (12, 13)}
    with ExitStack() as ctx:
        s = Scope(nc, ctx, "a0")
        wq, wk, wv = (s.sb(n, [P, KD, HW]) for n in ("wq", "wk", "wv"))
        wu = s.sb("wu", [P, MT, D])
        bu = s.sb("bu", [1, D])
        xnT = s.sb("xnT", [P, KD, 2 * P])
        qT = [s.sb(f"qT{n}", [P, MT, 2 * P]) for n in range(2)]
        kM = [s.sb(f"kM{n}", [P, MT, 2, 2, P]) for n in range(2)]
        v = [s.sb(f"v{n}", [P, 2, HW]) for n in range(2)]
        attnT = s.sb("attnT", [P, 2, MT, P])
        ln = LayerNorm(s, x)
        ring = Ring(s, SLOTS)
        att = HeadAttention(s, HD, ident, (ident_bf, mask_bf),
                            lambda c: attnT[:, c // 2, 4 * (c % 2):4 * (c % 2) + 4, :].rearrange("p t q -> p (t q)"),
                            vector_copies=(0, 2, 4, 6))
        loaded = s.sem("loaded")
        x_loaded = s.sem("x_loaded")
        padded = s.sem("padded")
        block = s.block()

        @block.sync
        def _(sp):
            x_tiles = x_in.rearrange("b t d -> t b d")
            sp.dma_start(x[:, 0:4, :], x_tiles[:, 0:4, :]).then_inc(x_loaded, 16)
            for dst, src, k in ((wq, w_q, KD), (wk, w_k, KD), (wv, w_v, KD), (wu, w_u, MT)):
                sp.dma_start(dst[:, :, :], src.rearrange("(k p) n -> p k n", p=P)).then_inc(loaded, 16)
            sp.dma_start(bu[:, :], b_u.rearrange("(a d) -> a d", a=1)).then_inc(loaded, 16)
            sp.wait_ge(x_loaded, 16)
            sp.dma_start(x[:, 4:NB, :], x_tiles[:, 4:NB, :]).then_inc(x_loaded, 16)

        @block.gpsimd
        def _(pool):
            ln.setup(pool)
            ln.root(pool, 0)
            ln.root(pool, 1)
            with pool.Fori(0, PAIRS) as i:
                ln.root(pool, i + 2)

        @block.tensor
        def _(pe):
            def produce(n, r):
                bank = ring.free(pe, n, r)
                if r < 2:
                    last = ln.transposed(pe, bank, ident, n, r)
                elif r < 10:
                    w = wq if r < 6 else wk
                    for m in range(2):
                        t = 2 * ((r - 2) % 4) + m
                        for k in range(KD):
                            last = pe.matmul(bank[:, m * 256:(m + 1) * 256], w[:, k, t * P:(t + 1) * P],
                                             xnT[:, k, :], start=(k == 0), stop=(k == KD - 1))
                else:
                    b, half = (r - 10) // 2, (r - 10) % 2
                    for k in range(KD):
                        last = pe.matmul(bank[:, :], xnT[:, k, b * P:(b + 1) * P],
                                         wv[:, k, half * 512:(half + 1) * 512], start=(k == 0), stop=(k == KD - 1))
                last.then_inc(ring.filled(r), 1)

            def produce_all(n):
                ring.wait_slot(pe, n, 0)
                ring.wait_slot(pe, n, 1)
                for r in range(2, SLOTS):
                    produce(n, r)

            produce(0, 0)
            produce(0, 1)
            pe.wait_ge(loaded, 80)
            produce_all(0)
            produce(1, 0)
            produce(1, 1)

            def scores(par, bank, b, g, fresh):
                for j in range(2):
                    t = 2 * g + j
                    last = pe.matmul(bank[:, j * 2 * P:(j + 1) * 2 * P], qT[par][:, t, b * P:(b + 1) * P],
                                     kM[par][:, t, b, :, :].rearrange("p a k -> p (a k)"), start=fresh,
                                     stop=True, skip_group_check=True)
                return last

            def head_values(par, b, h):
                return v[par][:, b, h * HD:(h + 1) * HD]

            att.pe_first(pe, scores)
            for i, par in pairs_by_two(pe):
                def before(u):
                    if u == 1:
                        ring.wait_slot(pe, i, 12)
                        ring.wait_slot(pe, i, 13)
                    if u == 6:
                        ring.wait_slot(pe, i + 1, 8)
                        ring.wait_slot(pe, i + 1, 9)

                def after(u):
                    if u == 0:
                        ring.wait_slot(pe, i + 1, 0)
                        ring.wait_slot(pe, i + 1, 1)
                    for r in AFTER.get(u, ()):
                        produce(i + 1, r)

                att.on_pe(pe, i, par, scores, head_values, before, after)
                produce(i + 2, 0)
                produce(i + 2, 1)
                att.pe_project(pe, i, lambda b: [(attnT[:, b, t, :], wu[:, t, :]) for t in range(MT)], ones_row, bu)

        def empty(eng, n, r, par, scaled_copy):
            bank = ring.arrived(eng, n, r)
            if r < 2:
                last = scaled_copy(xnT[:, :, r * P:(r + 1) * P], bank[:, 0:2 * P].rearrange("p (k t) -> p k t", k=KD), 1.0)
            elif r < 6:
                last = scaled_copy(qT[par][:, 2 * r - 4:2 * r - 2, :].rearrange("p a t -> p (a t)"), bank[:, :], QK_SCALE)
            elif r < 10:
                for a in range(2):
                    for m in range(2):
                        last = scaled_copy(kM[par][:, 2 * (r - 6) + m, :, a, :],
                                           bank[:, m * 2 * P:(m + 1) * 2 * P].rearrange("p (b k) -> p b k", b=2),
                                           half_mask[:, a:a + 1])
            else:
                b, half = (r - 10) // 2, (r - 10) % 2
                last = scaled_copy(v[par][:, b, half * 512:(half + 1) * 512], bank[:, :], 1.0)
            last.then_inc(ring.done(r), 1)

        @block.scalar
        def _(act):
            def scaled_copy(dst, src, scale):
                return act.activation(dst, src, ACT.Copy, scale=scale)

            for r in range(0, SLOTS, 2):
                empty(act, 0, r, 0, scaled_copy)
            empty(act, 1, 0, 1, scaled_copy)
            att.act_first(act)
            for i, par in pairs_by_two(act):
                def before(u):
                    if u - 1 in AFTER:
                        empty(act, i + 1, AFTER[u - 1][0], 1 - par, scaled_copy)

                att.on_act(act, i, before, lambda u: None)
                before(UNITS)
                empty(act, i + 2, 0, par, scaled_copy)

        @block.vector
        def _(dve):
            def scaled_copy(dst, src, scale):
                return dve.tensor_scalar(dst, src, scale, None, ALU.mult)

            dve.memset(x[:, NB:NB + 4, :], 0.0).then_inc(padded, 1)
            dve.wait_ge(padded, 1)
            dve.wait_ge(x_loaded, 16)
            ln.statistics(dve, 0)
            ln.apply(dve, 0)
            ln.statistics(dve, 1)
            for r in range(1, SLOTS, 2):
                empty(dve, 0, r, 0, scaled_copy)
                if r == 1:
                    ln.apply(dve, 1)
            empty(dve, 1, 1, 1, scaled_copy)
            dve.wait_ge(x_loaded, 32)
            att.dve_first(dve)
            for i, par in pairs_by_two(dve):
                def before(u):
                    if u - 1 in AFTER:
                        empty(dve, i + 1, AFTER[u - 1][1], 1 - par, scaled_copy)

                def after(u):
                    if u == 3:
                        ln.statistics(dve, i + 2)
                    if u == 5:
                        ln.apply(dve, i + 2)
                    if u == 7:
                        before(UNITS)

                att.on_dve(dve, i, par, before, after)
                empty(dve, i + 2, 1, par, scaled_copy)
                att.dve_residual(dve, i, x)


def masked_keys(eng, kM, kT, head_mask, b, t):
    return eng.tensor_tensor(kM[:, b, t, :, :], kT[:, b, t, :].unsqueeze(1).broadcast_to([P, 8, P]),
                             head_mask[:, :].unsqueeze(2).broadcast_to([P, 8, P]), ALU.mult)


class Ring:

    def __init__(self, s, slots):
        self.bank = [s.ps(f"ring{n}", [P, 512]) for n in range(2)]
        self.produced = [Signal(s.sem(f"produced{n}"), (slots + 1 - n) // 2) for n in range(2)]
        self.emptied = [Signal(s.sem(f"emptied{n}"), (slots + 1 - n) // 2) for n in range(2)]

    def free(self, pe, n, r):
        pe.wait_ge(self.emptied[r % 2].sem, self.emptied[r % 2].at(n, r // 2))
        return self.bank[r % 2]

    def filled(self, r):
        return self.produced[r % 2].sem

    def arrived(self, eng, n, r):
        eng.wait_ge(self.produced[r % 2].sem, self.produced[r % 2].at(n, r // 2 + 1))
        return self.bank[r % 2]

    def done(self, r):
        return self.emptied[r % 2].sem

    def wait_slot(self, eng, n, r):
        eng.wait_ge(self.emptied[r % 2].sem, self.emptied[r % 2].at(n, r // 2 + 1))


def pairs_by_two(eng):
    with eng.Fori(0, PAIRS // 2) as h:
        for par in range(2):
            yield 2 * h + par, par


class Turner:

    def __init__(self, s, banks, ident):
        self.banks, self.ident, self.jobs = banks, ident, []
        self.turned = [s.sem(f"w_turned{n}") for n in range(2)]
        self.copied = [s.sem(f"w_copied{n}") for n in range(2)]

    def weight(self, w, wT, tiles):
        for k in range(KD):
            for t in range(0, tiles, 4):
                m = min(4, tiles - t)
                self.jobs.append(([w[:, t + j, k * P:(k + 1) * P] for j in range(m)], wT[:, k, t * P:(t + m) * P]))

    def on_pe(self, pe):
        for n, (blocks, _) in enumerate(self.jobs):
            pe.wait_ge(self.copied[n % 2], n // 2)
            at = 0
            for b in blocks:
                rows = b.shape[0]
                last = pe.transpose(self.banks[n % 2][:, at:at + rows], b, self.ident[0:rows, 0:rows])
                at += rows
            last.then_inc(self.turned[n % 2], 1)

    def _copy(self, eng, copy, parity):
        for n, (blocks, dst) in enumerate(self.jobs):
            if n % 2 == parity:
                eng.wait_ge(self.turned[parity], n // 2 + 1)
                cols = sum(b.shape[0] for b in blocks)
                copy(dst, self.banks[parity][:, 0:cols]).then_inc(self.copied[parity], 1)

    def on_act(self, act):
        self._copy(act, act.copy, 0)

    def on_dve(self, dve):
        self._copy(dve, dve.tensor_copy, 1)

    def wait_all(self, pe):
        for parity in range(2):
            pe.wait_ge(self.copied[parity], len(self.jobs[parity::2]))


def copy_by_parity(copy, dst, src, head_dim):
    for a in range(2):
        for b in range(2):
            last = copy(dst[:, b, a, :].rearrange("p (h a d) -> p h a d", a=2, d=head_dim)[:, :, a, :],
                        src[:, b * D:(b + 1) * D].rearrange("p (h a d) -> p h a d", a=2, d=head_dim)[:, :, a, :])
    return last


def token_major(pe, dst, rows, w, ones_row, bias):
    for k in range(KD):
        pe.matmul(dst, rows(k), w(k), start=(k == 0), stop=False)
    return pe.matmul(dst, ones_row[:, :], bias, start=False, stop=True)


def stage_chunked_attention(nc, x, ident, ones_row, ident_bf, mask_bf, head_mask, ctx_in, w_in, b_in, w_out, b_out):
    HD = D // NH
    NQ, NK, NV, NO = 0, D, 2 * D, 3 * D
    SLOTS = 5
    AFTER = {0: (2, 3), 7: (4,), 8: (0, 1)}
    with ExitStack() as ctx:
        s = Scope(nc, ctx, "x0")
        w_nat = s.sb("w_nat", [P, 8, D])
        wT = s.sb("wT", [P, KD, 8 * P])
        bqk = s.sb("bqk", [P, 2, 2])
        bv, bo = s.sb("bv", [1, D]), s.sb("bo", [1, D])
        ctx_sb = s.sb("ctx", [P, 2, D])
        ctxT = s.sb("ctxT", [P, KD, 2 * P])
        xnT = s.sb("xnT", [P, KD, 2 * P])
        qT = [s.sb(f"qT{n}", [P, KD, 2 * P]) for n in range(2)]
        kT = s.sb("kT", [P, 2, KD, P])
        kM = [s.sb(f"kM{n}", [P, 2, KD, 8, P]) for n in range(2)]
        v = [s.sb(f"v{n}", [P, 2, 2, D]) for n in range(2)]
        attnT = s.sb("attnT", [P, 2, KD, P])
        ln = LayerNorm(s, x)
        ring = Ring(s, SLOTS)
        att = HeadAttention(s, HD, ident, (ident_bf, mask_bf), lambda b: attnT[:, b, :, :].rearrange("p k t -> p (k t)"))
        turner = Turner(s, ring.bank, ident)
        turner.weight(w_nat, wT, 8)
        loaded = s.sem("loaded")
        ctx_loaded = s.sem("ctx_loaded")
        v_zeroed = s.sem("v_zeroed")
        k_masked = Signal(s.sem("k_masked"), 2 * KD)
        block = s.block()

        @block.sync
        def _(sp):
            sp.dma_start(w_nat[:, 0:6, :], w_in.rearrange("(t p) n -> p t n", p=P)).then_inc(loaded, 16)
            sp.dma_start(w_nat[:, 6:8, :], w_out.rearrange("(t p) n -> p t n", p=P)).then_inc(loaded, 16)
            sp.dma_start(ctx_sb[:, :, :], ctx_in.rearrange("b t d -> t b d")[:, 0:2, :]).then_inc(ctx_loaded, 16)
            for c in range(2):
                sp.dma_start(bqk[:, c, :], b_in[c * D:(c + 1) * D].rearrange("(k p) -> p k", p=P),
                             allow_slow_non_contiguous=True).then_inc(loaded, 16)
            sp.dma_start(bv[:, :], b_in[2 * D:3 * D].rearrange("(a d) -> a d", a=1)).then_inc(loaded, 16)
            sp.dma_start(bo[:, :], b_out.rearrange("(a d) -> a d", a=1)).then_inc(loaded, 16)
            with sp.Fori(1, PAIRS) as n:
                ring.arrived(sp, n - 1, 1)
                sp.dma_start(ctx_sb[:, :, :], ctx_in.rearrange("b t d -> t b d")[:, bass.ds(2 * n, 2), :]) \
                    .then_inc(ctx_loaded, 16)
            for n in (PAIRS, PAIRS + 1):
                ring.arrived(sp, n - 1, 1)
                sp.dma_start(ctx_sb[:, :, :], ctx_in.rearrange("b t d -> t b d")[:, 0:2, :]).then_inc(ctx_loaded, 16)
            sp.wait_ge(ctx_loaded, 16 * (PAIRS + 2))

        @block.gpsimd
        def _(pool):
            def mask_keys(n, par):
                ring.wait_slot(pool, n, 2)
                for b in range(2):
                    for t in range(KD):
                        masked_keys(pool, kM[par], kT, head_mask, b, t).then_inc(k_masked.sem, 1)

            ln.setup(pool)
            ln.root(pool, 0)
            ln.root(pool, 1)
            for n in range(2):
                pool.memset(v[n][:, :, :, :], 0.0).then_inc(v_zeroed, 1)
            mask_keys(0, 0)
            for i, par in pairs_by_two(pool):
                ln.root(pool, i + 2)
                mask_keys(i + 1, 1 - par)

        @block.tensor
        def _(pe):
            def produce(n, r):
                bank = ring.free(pe, n, r)
                if r == 0:
                    last = ln.transposed(pe, bank, ident, n)
                elif r == 1:
                    pe.wait_ge(ctx_loaded, 16 * n + 16)
                    for b in range(2):
                        for k in range(KD):
                            last = pe.transpose(bank[:, k * 2 * P + b * P:k * 2 * P + (b + 1) * P],
                                                ctx_sb[:, b, k * P:(k + 1) * P], ident[:, :])
                elif r < 4:
                    w0, act = (NK, ctxT) if r == 2 else (NQ, xnT)
                    for m in range(2):
                        for k in range(KD):
                            last = pe.matmul(bank[:, m * 256:(m + 1) * 256], wT[:, k, w0 + m * P:w0 + (m + 1) * P],
                                             act[:, k, :], start=(k == 0), stop=(k == KD - 1))
                else:
                    for b in range(2):
                        last = token_major(pe, bank[:, b * D:(b + 1) * D], lambda k: ctxT[:, k, b * P:(b + 1) * P],
                                           lambda k: wT[:, k, NV:NV + D], ones_row, bv[:, :])
                last.then_inc(ring.filled(r), 1)

            def scores(par, bank, b, g, fresh):
                return pe.matmul(bank[:, :], qT[par][:, g // 2, b * P:(b + 1) * P],
                                 kM[par][:, b, g // 2, 4 * (g % 2):4 * (g % 2) + 4, :].rearrange("p a k -> p (a k)"),
                                 start=fresh, stop=True, skip_group_check=True)

            def head_values(par, b, h):
                return v[par][:, b, h % 2, 32 * (h // 2):32 * (h // 2) + 32]

            pe.wait_ge(loaded, 96)
            turner.on_pe(pe)
            turner.wait_all(pe)
            for n, r in ((0, 0), (0, 1), (0, 2), (0, 3), (0, 4), (1, 0), (1, 1)):
                if r == 2:
                    ring.wait_slot(pe, 0, 0)
                    ring.wait_slot(pe, 0, 1)
                produce(n, r)
            ring.wait_slot(pe, 0, 3)
            pe.wait_ge(k_masked.sem, k_masked.at(0, KD))
            att.pe_first(pe, scores)
            for i, par in pairs_by_two(pe):
                def before(u):
                    if u == 1:
                        ring.wait_slot(pe, i, 4)
                    if u == 2:
                        pe.wait_ge(k_masked.sem, k_masked.at(i, 2 * KD))
                    if u == 6:
                        ring.wait_slot(pe, i + 1, 3)
                        pe.wait_ge(k_masked.sem, k_masked.at(i + 1, KD))

                def after(u):
                    if u == 0:
                        ring.wait_slot(pe, i + 1, 0)
                        ring.wait_slot(pe, i + 1, 1)
                    for r in AFTER.get(u, ()):
                        produce(i + (1 if r >= 2 else 2), r)

                att.on_pe(pe, i, par, scores, head_values, before, after)
                after(UNITS)
                att.pe_project(pe, i, lambda b: [(attnT[:, b, k, :], wT[:, k, NO:NO + D]) for k in range(KD)],
                               ones_row, bo)

        @block.scalar
        def _(act):
            def empty(n, r, par):
                bank = ring.arrived(act, n, r)
                if r == 0:
                    last = act.copy(xnT[:, :, :].rearrange("p k t -> p (k t)"), bank[:, :])
                elif r == 2:
                    act.wait_ge(k_masked.sem, k_masked.at(n, 0))
                    for m in range(2):
                        last = act.activation(kT[:, :, m, :],
                                              bank[:, m * 256:(m + 1) * 256].rearrange("p (b k) -> p b k", b=2),
                                              ACT.Identity, bias=bqk[:, 1, m:m + 1])
                else:
                    last = copy_by_parity(act.copy, v[par], bank, HD)
                last.then_inc(ring.done(r), 1)

            turner.on_act(act)
            act.wait_ge(v_zeroed, 2)
            for n, r in ((0, 0), (0, 2), (0, 4), (1, 0)):
                empty(n, r, 0)
            att.act_first(act)
            for i, par in pairs_by_two(act):
                def before(u):
                    for r in AFTER.get(u - 1, ()):
                        if r % 2 == 0:
                            empty(i + (1 if r >= 2 else 2), r, 1 - par)

                att.on_act(act, i, before, lambda u: None)
                before(UNITS)
                before(UNITS + 1)

        @block.vector
        def _(dve):
            def empty(n, r, par):
                bank = ring.arrived(dve, n, r)
                if r == 1:
                    last = dve.tensor_copy(ctxT[:, :, :].rearrange("p k t -> p (k t)"), bank[:, :])
                else:
                    for m in range(2):
                        last = dve.tensor_scalar(qT[par][:, m, :], bank[:, m * 256:(m + 1) * 256],
                                                 bqk[:, 0, m:m + 1], 1.0 / 4.0, ALU.add, ALU.mult)
                last.then_inc(ring.done(r), 1)

            ln.statistics(dve, 0)
            ln.apply(dve, 0)
            turner.on_dve(dve)
            ln.statistics(dve, 1)
            for n, r in ((0, 1), (0, 3), (1, 1)):
                empty(n, r, 0)
                if n == 0 and r == 1:
                    ln.apply(dve, 1)
            att.dve_first(dve)
            for i, par in pairs_by_two(dve):
                def before(u):
                    for r in AFTER.get(u - 1, ()):
                        if r % 2 == 1:
                            empty(i + (1 if r >= 2 else 2), r, 1 - par)

                def after(u):
                    if u == 1:
                        ln.statistics(dve, i + 2)
                    if u == 2:
                        ln.apply(dve, i + 2)

                att.on_dve(dve, i, par, before, after)
                before(UNITS + 1)
                att.dve_residual(dve, i, x)


def stage_gated_attention(nc, x, ident, ones_row, head_mask, w_q, b_q, w_k, b_k, w_v, b_v, w_o, b_o, g_in,
                          w_g1, b_g1, w_g2, b_g2):
    HD = D // NH
    GH = P
    NORM_EPS2 = 1e-24
    NQ, NV, NO, NG = 0, 2 * D, 3 * D, 4 * D
    SLOTS = 8
    AFTER = {0: (4,), 1: (3,), 3: (6, 5), 4: (0,), 5: (7,), 6: (1,), 7: (2,)}

    def ahead(r):
        return 2 if r <= 2 else 1

    with ExitStack() as ctx:
        s = Scope(nc, ctx, "a1")
        w_nat = s.sb("w_nat", [P, 9, D])
        wT = s.sb("wT", [P, KD, 9 * P])
        wg2 = s.sb("wg2", [NH, GH])
        wg2T = s.sb("wg2T", [P, NH])
        bqk, bv, bo = s.sb("bqk", [1, 2 * D]), s.sb("bv", [1, D]), s.sb("bo", [1, D])
        bg1 = s.sb("bg1", [P, 1])
        bg2, g_row = s.sb("bg2", [1, NH]), s.sb("g_row", [1, NH])
        xnT = [s.sb(f"xnT{n}", [P, KD, 2 * P]) for n in range(2)]
        qk = s.sb("qk", [P, 2, 2 * D])
        sq = s.sb("sq", [P, 2, 2 * D])
        ss = s.sb("ss", [P, 2 * 2 * NH])
        inv = s.sb("inv", [P, 2 * 2 * NH])
        inv_power = s.sb("inv_power", [P, 2 * 2 * NH])
        qT = [s.sb(f"qT{n}", [P, 2, KD, P]) for n in range(2)]
        kT = s.sb("kT", [P, 2, KD, P])
        kM = [s.sb(f"kM{n}", [P, 2, KD, 8, P]) for n in range(2)]
        v = [s.sb(f"v{n}", [P, 2, 2, D]) for n in range(2)]
        attnT = s.sb("attnT", [P, 2, KD, P])
        gelu = s.sb("gelu", [P, 2 * P])
        hsum = s.sb("hsum", [P, 2])
        hrep = s.sb("hrep", [P, 2, P])
        gate_static = s.sb("gate_static", [P, NH])
        gate = [s.sb(f"gate{n}", [P, 2, NH]) for n in range(2)]
        gate_bias = s.sb("gate_bias", [P, NH])
        ones_sq = s.sb("ones_sq", [P, P])
        ln = LayerNorm(s, x)
        ring = Ring(s, SLOTS)
        att = HeadAttention(s, HD, ident, None, lambda b: attnT[:, b, :, :].rearrange("p k t -> p (k t)"), gated=True)
        turner = Turner(s, ring.bank, ident)
        turner.weight(w_nat, wT, 9)
        turner.jobs.append(([wg2[:, :]], wg2T[:, :]))
        loaded = s.sem("loaded")
        v_zeroed = s.sem("v_zeroed")
        k_masked = Signal(s.sem("k_masked"), 2 * KD)
        static_spread = s.sem("static_spread")
        static_exp = s.sem("static_exp")
        power_set = s.sem("power_set")
        ones_set = s.sem("ones_set")
        squares_ready = s.sem("squares_ready")
        inverse_ready = s.sem("inverse_ready")
        scaled = s.sem("scaled")
        hidden_spread = s.sem("hidden_spread")
        logits_exp = s.sem("logits_exp")
        square_links = Chain(s.sem("square_links"), 2)
        gate_links = Chain(s.sem("gate_links"), 4)
        first_links = Chain(s.sem("first_links"))
        block = s.block()

        @block.sync
        def _(sp):
            for n, w in enumerate((w_q, w_k, w_v, w_o)):
                sp.dma_start(w_nat[:, 2 * n:2 * n + 2, :], w.rearrange("(t p) n -> p t n", p=P)).then_inc(loaded, 16)
            sp.dma_start(w_nat[:, 8, :], w_g1).then_inc(loaded, 16)
            sp.dma_start(wg2[:, :], w_g2).then_inc(loaded, 16)
            for dst, b in ((bqk[:, 0:D], b_q), (bqk[:, D:2 * D], b_k), (bv[:, :], b_v), (bo[:, :], b_o),
                           (bg2[:, :], b_g2), (g_row[:, :], g_in)):
                sp.dma_start(dst, b.rearrange("(a d) -> a d", a=1)).then_inc(loaded, 16)
            sp.dma_start(bg1[:, :], b_g1.rearrange("(p a) -> p a", a=1)).then_inc(loaded, 16)

        @block.gpsimd
        def _(pool):
            ln.setup(pool)
            pool.memset(inv_power[:, :], -0.5).then_inc(power_set, 1)
            pool.memset(ones_sq[:, :], 1.0).then_inc(ones_set, 1)
            for n in range(2):
                pool.memset(v[n][:, :, :, :], 0.0).then_inc(v_zeroed, 1)
            pool.wait_ge(power_set, 1)

            def invert(n):
                pool.wait_ge(squares_ready, n + 1)
                pool.tensor_tensor(inv[:, :], ss[:, :], inv_power[:, :], ALU.pow).then_inc(inverse_ready, 1)

            def mask_keys(n, par):
                for b in range(2):
                    ring.wait_slot(pool, n, (6, 5)[b])
                    for t in range(KD):
                        masked_keys(pool, kM[par], kT, head_mask, b, t).then_inc(k_masked.sem, 1)

            ln.root(pool, 0)
            ln.root(pool, 1)
            invert(0)
            mask_keys(0, 0)
            invert(1)
            for i, par in pairs_by_two(pool):
                ln.root(pool, i + 2)
                mask_keys(i + 1, 1 - par)
                invert(i + 2)

        @block.tensor
        def _(pe):
            def produce(n, r, par):
                bank = ring.free(pe, n, r)
                if r == 0:
                    last = ln.transposed(pe, bank, ident, n)
                elif r in (1, 2):
                    b = r - 1
                    last = token_major(pe, bank[:, :], lambda k: xnT[par][:, k, b * P:(b + 1) * P],
                                       lambda k: wT[:, k, NQ:NQ + 2 * D], ones_row, bqk[:, :])
                elif r == 4:
                    for k in range(KD):
                        last = pe.matmul(bank[:, 0:2 * P], wT[:, k, NG:NG + GH], xnT[par][:, k, :],
                                         start=(k == 0), stop=(k == KD - 1))
                elif r == 7:
                    for b in range(2):
                        last = token_major(pe, bank[:, b * D:(b + 1) * D], lambda k: xnT[par][:, k, b * P:(b + 1) * P],
                                           lambda k: wT[:, k, NV:NV + D], ones_row, bv[:, :])
                elif r == 3:
                    pe.wait_ge(hidden_spread, n + 1)
                    for b in range(2):
                        pe.matmul(bank[:, b * NH:(b + 1) * NH], hrep[:, b, :], wg2T[:, :], start=True, stop=True)
                    last = pe.matmul(bank[:, 2 * NH:3 * NH], ones_row[:, :], bg2[:, :], start=True, stop=True)
                else:
                    pe.wait_ge(scaled, n + 1)
                    for t in range(4):
                        last = pe.transpose(bank[:, t * P:(t + 1) * P], qk[:, 0 if r == 6 else 1, t * P:(t + 1) * P], ident[:, :])
                last.then_inc(ring.filled(r), 1)

            def scores(par, bank, b, g, fresh):
                return pe.matmul(bank[:, :], qT[par][:, b, g // 2, :],
                                 kM[par][:, b, g // 2, 4 * (g % 2):4 * (g % 2) + 4, :].rearrange("p a k -> p (a k)"),
                                 start=fresh, stop=True, skip_group_check=True)

            def head_values(par, b, h):
                return v[par][:, b, h % 2, 32 * (h // 2):32 * (h // 2) + 32]

            pe.wait_ge(loaded, 13 * 16)
            turner.on_pe(pe)
            turner.wait_all(pe)
            pe.matmul(ring.bank[1][:, 0:NH], ones_row[:, :], g_row[:, :], start=True, stop=True) \
                .then_inc(static_spread, 1)
            produce(0, 0, 0)
            pe.wait_ge(static_exp, 1)
            ring.wait_slot(pe, 0, 0)
            for r in (1, 2, 4, 3, 6, 5, 7):
                produce(0, r, 0)
            produce(1, 0, 1)
            ring.wait_slot(pe, 1, 0)
            produce(1, 1, 1)
            produce(1, 2, 1)
            ring.wait_slot(pe, 0, 5)
            pe.wait_ge(k_masked.sem, k_masked.at(0, KD))
            att.pe_first(pe, scores)
            for i, par in pairs_by_two(pe):
                def before(u):
                    if u == 1:
                        ring.wait_slot(pe, i, 7)
                    if u == 2:
                        pe.wait_ge(k_masked.sem, k_masked.at(i, 2 * KD))
                    if u == 6:
                        ring.wait_slot(pe, i + 1, 6)
                        ring.wait_slot(pe, i + 1, 5)
                        pe.wait_ge(k_masked.sem, k_masked.at(i + 1, KD))

                def after(u):
                    if u == 6:
                        ring.wait_slot(pe, i + 2, 0)
                    for r in AFTER.get(u, ()):
                        produce(i + ahead(r), r, (par + ahead(r)) % 2)

                att.on_pe(pe, i, par, scores, head_values, before, after)
                att.pe_project(pe, i, lambda b: [(attnT[:, b, k, :], wT[:, k, NO:NO + D]) for k in range(KD)],
                               ones_row, bo)

        @block.scalar
        def _(act):
            def empty(n, r, par):
                bank = ring.arrived(act, n, r)
                if r == 0:
                    last = act.copy(xnT[par][:, :, :].rearrange("p k t -> p (k t)"), bank[:, :])
                elif r == 2:
                    last = act.copy(qk[:, 1, :], bank[:, :])
                elif r == 4:
                    for b in range(2):
                        last = act.activation(gelu[:, b * P:(b + 1) * P], bank[:, b * P:(b + 1) * P], ACT.Gelu,
                                              bias=bg1[:, :], accum_out=hsum[:, b:b + 1])
                else:
                    act.wait_ge(k_masked.sem, k_masked.at(n, 0))
                    act.activation(qT[par][:, 0, :, :].rearrange("p k t -> p (k t)"), bank[:, 0:D], ACT.Copy,
                                   scale=1.0 / 4.0)
                    last = act.copy(kT[:, 0, :, :].rearrange("p k t -> p (k t)"), bank[:, D:2 * D])
                last.then_inc(ring.done(r), 1)
                if r == 4:
                    ring.wait_slot(act, n, 4)
                    for b in range(2):
                        last = act.activation(hrep[:, b, :], ones_sq[:, :], ACT.Copy, scale=hsum[:, b:b + 1])
                    last.then_inc(hidden_spread, 1)

            def exp_logits(n, par):
                ring.wait_slot(act, n, 3)
                act.activation(gate[par][:, :, :], gate[par][:, :, :], ACT.Exp, scale=-1.0).then_inc(logits_exp, 1)

            turner.on_act(act)
            act.wait_ge(static_spread, 1)
            act.activation(gate_static[:, :], ring.bank[1][:, 0:NH], ACT.Exp, scale=-1.0).then_inc(static_exp, 1)
            act.wait_ge(loaded, 13 * 16)
            act.wait_ge(ones_set, 1)
            for r in (0, 2, 4):
                empty(0, r, 0)
            exp_logits(0, 0)
            empty(0, 6, 0)
            empty(1, 0, 1)
            empty(1, 2, 1)
            att.act_first(act)
            for i, par in pairs_by_two(act):
                def before(u):
                    for r in AFTER.get(u - 1, ()):
                        if r % 2 == 0:
                            empty(i + ahead(r), r, (par + ahead(r)) % 2)
                    if u == 3:
                        exp_logits(i + 1, 1 - par)

                att.on_act(act, i, before, lambda u: None)
                before(UNITS)

        @block.vector
        def _(dve):
            def empty(n, r, par):
                bank = ring.arrived(dve, n, r)
                if r == 1:
                    last = dve.tensor_copy(qk[:, 0, :], bank[:, :])
                elif r == 7:
                    last = copy_by_parity(dve.tensor_copy, v[par], bank, HD)
                elif r == 3:
                    gate_links.begin(n)
                    gate_links.link(dve, dve.tensor_copy(gate_bias[:, :], bank[:, 2 * NH:3 * NH]))
                    last = dve.scalar_tensor_tensor(gate[par][:, :, :],
                                                    bank[:, 0:2 * NH].rearrange("p (b h) -> p b h", b=2), 1.0 / P,
                                                    gate_bias[:, :].unsqueeze(1).broadcast_to([P, 2, NH]),
                                                    ALU.mult, ALU.add)
                else:
                    dve.wait_ge(k_masked.sem, k_masked.at(n, 0))
                    dve.tensor_scalar(qT[par][:, 1, :, :].rearrange("p k t -> p (k t)"), bank[:, 0:D],
                                      1.0 / 4.0, None, ALU.mult)
                    last = dve.tensor_copy(kT[:, 1, :, :].rearrange("p k t -> p (k t)"), bank[:, D:2 * D])
                last.then_inc(ring.done(r), 1)

            def sum_squares(n):
                square_links.begin(n)
                ring.wait_slot(dve, n, 1)
                ring.wait_slot(dve, n, 2)
                square_links.link(dve, dve.tensor_tensor(sq[:, :, :], qk[:, :, :], qk[:, :, :], ALU.mult))
                square_links.link(dve, dve.tensor_reduce(ss[:, :], sq[:, :, :].rearrange("p b (h d) -> p (b h) d", d=HD),
                                                  AX.X, ALU.add))
                dve.tensor_scalar(ss[:, :], ss[:, :], NORM_EPS2, None, ALU.max).then_inc(squares_ready, 1)

            def scale_heads(n):
                dve.wait_ge(inverse_ready, n + 1)
                dve.tensor_tensor(qk[:, :, :].rearrange("p b (h d) -> p (b h) d", d=HD),
                                  qk[:, :, :].rearrange("p b (h d) -> p (b h) d", d=HD),
                                  inv[:, :].unsqueeze(2).broadcast_to([P, 4 * NH, HD]), ALU.mult).then_inc(scaled, 1)

            def finish_gate(n, par):
                dve.wait_ge(logits_exp, n + 1)
                logits = gate[par][:, :, :]
                gate_links.link(dve, dve.tensor_scalar(logits, logits, 1.0, None, ALU.add))
                gate_links.link(dve, dve.reciprocal(logits, logits))
                gate_links.link(dve, dve.tensor_tensor(logits, logits, gate_static[:, :].unsqueeze(1).broadcast_to([P, 2, NH]),
                                                  ALU.mult))
                gate_links.end()

            def gate_of(par, b, g):
                return gate[par][:, b, 4 * g:4 * g + 4]

            ln.statistics(dve, 0)
            ln.apply(dve, 0)
            ln.statistics(dve, 1)
            turner.on_dve(dve)
            dve.wait_ge(static_exp, 1)
            first_links.link(dve, dve.tensor_scalar(gate_static[:, :], gate_static[:, :], 1.0, None, ALU.add))
            first_links.link(dve, dve.reciprocal(gate_static[:, :], gate_static[:, :]))
            empty(0, 1, 0)
            ln.apply(dve, 1)
            sum_squares(0)
            empty(0, 3, 0)
            finish_gate(0, 0)
            scale_heads(0)
            empty(0, 5, 0)
            dve.wait_ge(v_zeroed, 2)
            empty(0, 7, 0)
            empty(1, 1, 1)
            sum_squares(1)
            att.dve_first(dve, gate_of)
            for i, par in pairs_by_two(dve):
                def before(u):
                    for r in AFTER.get(u - 1, ()):
                        if r % 2 == 1:
                            empty(i + ahead(r), r, (par + ahead(r)) % 2)

                def after(u):
                    if u == 2:
                        ln.statistics(dve, i + 2)
                        scale_heads(i + 1)
                    if u == 3:
                        ln.apply(dve, i + 2)
                    if u == 4:
                        finish_gate(i + 1, 1 - par)

                att.on_dve(dve, i, par, before, after, gate_of)
                sum_squares(i + 2)
                att.dve_residual(dve, i, x)


def stage_aligned_attention(nc, x, ident, ones_row, ctx_in, w_in, b_in):
    RING = 6
    with ExitStack() as ctx:
        s = Scope(nc, ctx, "x1")
        w_nat = s.sb("w_nat", [P, 2, D])
        wT = s.sb("wT", [P, KD, D])
        bias = s.sb("bias", [P, KD])
        ctx_next = s.sb("ctx_next", [P, 2, D])
        ctx_now = s.sb("ctx_now", [P, 2, D])
        ctxT = s.sb("ctxT", [P, KD, 2 * P])
        xnT = s.sb("xnT", [P, KD, 2 * P])
        exT = s.sb("exT", [P, KD, 2 * P])
        eoT = s.sb("eoT", [P, KD, 2 * P])
        neg_max, row_sum, norm = (s.sb(n, [P, 2]) for n in ("neg_max", "row_sum", "norm"))
        prob = s.sb("prob", [P, 2, P])
        probT = s.sb("probT", [P, 2, P])
        ln = LayerNorm(s, x)
        proj_bank = [s.ps(f"proj{n}", [P, 512]) for n in range(2)]
        out_bank = s.ps("out", [P, 512])
        turner = Turner(s, proj_bank, ident)
        turner.weight(w_nat, wT, 2)
        loaded = s.sem("loaded")
        ctx_loaded = s.sem("ctx_loaded")
        ctx_turned = s.sem("ctx_turned")
        values_loaded = s.sem("values_loaded")
        first_T = s.sem("first_T")
        first_copied = s.sem("first_copied")
        max_ready = s.sem("max_ready")
        weighted = s.sem("weighted")
        added = s.sem("added")
        produced = [Signal(s.sem("produced0"), RING // 2 - 1), Signal(s.sem("produced1"), RING // 2)]
        evacuated = [Signal(s.sem(f"evacuated{n}"), RING // 2) for n in range(2)]
        links = Chain(s.sem("links"), 1)
        first_links = Chain(s.sem("first_links"))
        block = s.block()

        @block.sync
        def _(sp):
            ctx_pairs = ctx_in.rearrange("b t d -> t b d")
            sp.dma_start(w_nat[:, :, :], w_in.rearrange("(t p) n -> p t n", p=P)).then_inc(loaded, 16)
            sp.dma_start(bias[:, :], b_in.rearrange("(k p) -> p k", p=P),
                         allow_slow_non_contiguous=True).then_inc(loaded, 16)
            sp.dma_start(ctx_next[:, :, :], ctx_pairs[:, 0:2, :]).then_inc(ctx_loaded, 16)
            with sp.Fori(0, PAIRS - 1) as n:
                sp.wait_ge(weighted, n)
                sp.dma_start(ctx_now[:, :, :], ctx_pairs[:, bass.ds(2 * n, 2), :]).then_inc(values_loaded, 16)
                sp.wait_ge(ctx_turned, n + 1)
                sp.dma_start(ctx_next[:, :, :], ctx_pairs[:, bass.ds(2 * n + 2, 2), :]).then_inc(ctx_loaded, 16)
            sp.wait_ge(weighted, PAIRS - 1)
            sp.dma_start(ctx_now[:, :, :], ctx_pairs[:, NB - 2:NB, :]).then_inc(values_loaded, 16)
            sp.wait_ge(ctx_turned, PAIRS)
            sp.dma_start(ctx_next[:, :, :], ctx_pairs[:, 0:2, :]).then_inc(ctx_loaded, 16)
            sp.wait_ge(ctx_loaded, 16 * PAIRS + 16)

        @block.gpsimd
        def _(pool):
            ln.setup(pool)
            ln.root(pool, 0)
            with pool.Fori(0, PAIRS) as i:
                ln.root(pool, i + 1)

        def turn_context(pe, bank):
            for b in range(2):
                for k in range(KD):
                    last = pe.transpose(bank[:, k * 2 * P + b * P:k * 2 * P + (b + 1) * P],
                                        ctx_next[:, b, k * P:(k + 1) * P], ident[:, :])
            return last

        @block.tensor
        def _(pe):
            pe.wait_ge(loaded, 32)
            turner.on_pe(pe)
            turner.wait_all(pe)
            ln.transposed(pe, proj_bank[0], ident, 0).then_inc(first_T, 1)
            pe.wait_ge(ctx_loaded, 16)
            turn_context(pe, proj_bank[1]).then_inc(ctx_turned, 1)
            pe.wait_ge(first_copied, 2)
            with pe.Fori(0, PAIRS) as i:
                def free(r):
                    pe.wait_ge(evacuated[r % 2].sem, evacuated[r % 2].at(i, r // 2))

                for r, act in ((0, xnT), (1, ctxT)):
                    free(0)
                    free(1)
                    for m in range(2):
                        for k in range(KD):
                            last = pe.matmul(proj_bank[r][:, m * 256:(m + 1) * 256], wT[:, k, m * P:(m + 1) * P],
                                             act[:, k, :], start=(k == 0), stop=(k == KD - 1))
                    last.then_inc(produced[r].sem, 1)
                free(2)
                pe.wait_ge(evacuated[1].sem, evacuated[1].at(i, 1))
                for b in range(2):
                    for k in range(KD):
                        last = pe.matmul(proj_bank[0][:, b * P:(b + 1) * P], exT[:, k, b * P:(b + 1) * P],
                                         eoT[:, k, b * P:(b + 1) * P], start=(k == 0), stop=(k == KD - 1))
                last.then_inc(produced[0].sem, 1)
                free(3)
                ln.transposed(pe, proj_bank[1], ident, i + 1).then_inc(produced[1].sem, 1)
                free(4)
                pe.wait_ge(ctx_loaded, 16 * i + 32)
                turn_context(pe, proj_bank[0]).then_inc(ctx_turned, 1)
                free(5)
                for b in range(2):
                    last = pe.transpose(proj_bank[1][:, b * P:(b + 1) * P], prob[:, b, :], ident[:, :])
                last.then_inc(produced[1].sem, 1)
                pe.wait_ge(evacuated[1].sem, evacuated[1].at(i, 3))
                pe.wait_ge(values_loaded, 16 * i + 16)
                pe.wait_ge(added, i)
                for b in range(2):
                    last = pe.matmul(out_bank[:, b * D:(b + 1) * D], probT[:, b, :], ctx_now[:, b, :],
                                     start=True, stop=True)
                last.then_inc(weighted, 1)

        @block.scalar
        def _(act):
            turner.on_act(act)
            act.wait_ge(first_T, 1)
            act.copy(xnT[:, :, :].rearrange("p k t -> p (k t)"), proj_bank[0][:, :]).then_inc(first_copied, 1)
            act.wait_ge(loaded, 32)
            with act.Fori(0, PAIRS) as i:
                act.wait_ge(produced[0].sem, produced[0].at(i, 1))
                for m in range(2):
                    last = act.activation(exT[:, m, :], proj_bank[0][:, m * 256:(m + 1) * 256], ACT.Identity,
                                          bias=bias[:, m:m + 1])
                last.then_inc(evacuated[0].sem, 1)
                act.wait_ge(max_ready, i + 1)
                for b in range(2):
                    last = act.activation(prob[:, b, :], proj_bank[0][:, b * P:(b + 1) * P], ACT.Exp,
                                          bias=neg_max[:, b:b + 1], accum_out=row_sum[:, b:b + 1])
                last.then_inc(evacuated[0].sem, 1)
                act.wait_ge(ctx_turned, i + 2)
                act.copy(ctxT[:, :, :].rearrange("p k t -> p (k t)"), proj_bank[0][:, :]) \
                    .then_inc(evacuated[0].sem, 1)

        @block.vector
        def _(dve):
            ln.statistics(dve, 0)
            ln.apply(dve, 0)
            turner.on_dve(dve)
            dve.wait_ge(ctx_turned, 1)
            dve.tensor_copy(ctxT[:, :, :].rearrange("p k t -> p (k t)"), proj_bank[1][:, :]).then_inc(first_copied, 1)
            dve.wait_ge(loaded, 32)
            with dve.Fori(0, PAIRS) as i:
                links.begin(i)
                dve.wait_ge(produced[1].sem, produced[1].at(i, 1))
                for m in range(2):
                    last = dve.tensor_scalar(eoT[:, m, :], proj_bank[1][:, m * 256:(m + 1) * 256],
                                             bias[:, m:m + 1], None, ALU.add)
                last.then_inc(evacuated[1].sem, 1)
                ln.statistics(dve, i + 1)
                dve.wait_ge(produced[0].sem, produced[0].at(i, 2))
                dve.tensor_reduce(neg_max[:, :], proj_bank[0][:, 0:2 * P].rearrange("p (b k) -> p b k", b=2),
                                  AX.X, ALU.max, negate=True).then_inc(max_ready, 1)
                ln.apply(dve, i + 1)
                dve.wait_ge(produced[1].sem, produced[1].at(i, 2))
                dve.tensor_copy(xnT[:, :, :].rearrange("p k t -> p (k t)"), proj_bank[1][:, :]) \
                    .then_inc(evacuated[1].sem, 1)
                dve.wait_ge(produced[1].sem, produced[1].at(i, 3))
                dve.tensor_copy(probT[:, :, :].rearrange("p b t -> p (b t)"), proj_bank[1][:, 0:2 * P]) \
                    .then_inc(evacuated[1].sem, 1)
                links.link(dve, dve.reciprocal(norm[:, :], row_sum[:, :]))
                dve.wait_ge(weighted, i + 1)
                for b in range(2):
                    xb = x[:, bass.ds(2 * i + b, 1), :].rearrange("p a d -> p (a d)")
                    last = dve.scalar_tensor_tensor(xb, out_bank[:, b * D:(b + 1) * D], norm[:, b:b + 1], xb,
                                                    ALU.mult, ALU.add)
                last.then_inc(added, 1)
                links.end()


def stage_product_keys(nc, x, ident, gamma, beta, w_q, keys, key_in, key_out):
    H, NK, TOP = 8, 64, 8
    KW = P
    R = NK // 2
    PICKS = H * TOP
    TOKENS = NB * P
    HALF = P // 2
    W_SCALE = 4096.0
    GT = 16
    GU = HALF // GT
    with ExitStack() as ctx:
        s = Scope(nc, ctx, "f")
        hT = s.sb("hT", [P, KD, TOKENS + 2 * P])
        kiT = s.sb("kiT", [P, KD, R, P])
        ko = s.sb("ko", [P, R, D])
        gel = s.sb("gel", [P, R, 2 * P])
        fused = s.sb("fused", [P, KD, 2 * H * NK])
        bn_scale, bn_shift = s.sb("bn_scale", [P, KD]), s.sb("bn_shift", [P, KD])
        with ExitStack() as prep_ctx:
            p = Scope(nc, prep_ctx, "fp")
            wq_nat = p.sb("wq_nat", [P, 2 * H, D])
            keys_nat = p.sb("keys_nat", [NK, H, 2, KW])
            keysT = p.sb("keysT", [P, H, 2, NK])
            gamma_col, beta_col = p.sb("gamma_col", [P, KD]), p.sb("beta_col", [P, KD])
            stats, mv = p.sb("stats", [P, KD, 4, 6]), p.sb("mv", [P, KD, 2])
            bn_scale_power = p.sb("bn_power", [P, KD])
            var_eps, rstd = p.sb("var_eps", [P, KD]), p.sb("rstd", [P, KD])
            ln = LayerNorm(p, x)
            banks = [p.ps(f"bank{n}", [P, 512]) for n in range(2)]
            pair_bank = p.ps("pair", [P, 512])
            turner = Turner(p, banks, ident)
            for k in range(KD):
                for r in range(0, R, 4):
                    turner.jobs.append(([gel[:, r + j, k * P:(k + 1) * P] for j in range(4)],
                                        kiT[:, k, r:r + 4, :].rearrange("p r c -> p (r c)")))
            for h in range(0, H, 4):
                turner.jobs.append(([keys_nat[:, h + j, ax, :] for j in range(4) for ax in range(2)],
                                    keysT[:, h:h + 4, :, :].rearrange("p h a n -> p (h a n)")))
            loaded = p.sem("loaded")
            kept = p.sem("kept")
            fused_ready = [p.sem(f"fused_ready{n}") for n in range(2)]
            fused_copied = [p.sem(f"fused_copied{n}") for n in range(2)]
            pair_turned = p.sem("pair_turned")
            pair_copied = p.sem("pair_copied")
            power_set = p.sem("power_set")
            bn_var_ready = p.sem("bn_var_ready")
            bn_rstd_ready = p.sem("bn_rstd_ready")
            bn_links = Chain(p.sem("bn_links"))
            block = p.block()

            @block.sync
            def _(sp):
                for b in range(2):
                    sp.dma_start(gel[b * NK:(b + 1) * NK, :, :],
                                 key_in.rearrange("(i r b) d -> b i r d", r=R, b=2)[b]).then_inc(loaded, 16)
                sp.dma_start(keys_nat[:, :, :, :], keys.rearrange("h n a w -> n h a w")).then_inc(loaded, 16)
                sp.dma_start(wq_nat[:, :, :], w_q.rearrange("(j p) d -> p j d", p=P)).then_inc(loaded, 16)
                for dst, src in ((gamma_col, gamma), (beta_col, beta)):
                    sp.dma_start(dst[:, :], src.rearrange("(k p) -> p k", p=P),
                                 allow_slow_non_contiguous=True).then_inc(loaded, 16)
                for b in range(2):
                    sp.dma_start(ko[b * NK:(b + 1) * NK, :, :],
                                 key_out.rearrange("(i r b) d -> b i r d", r=R, b=2)[b]).then_inc(kept, 16)
                sp.wait_ge(kept, 32)

            @block.gpsimd
            def _(pool):
                ln.setup(pool)
                pool.memset(hT[:, :, TOKENS:TOKENS + 2 * P], 0.0)
                pool.memset(bn_scale_power[:, :], -0.5).then_inc(power_set, 1)
                with pool.Fori(0, PAIRS) as i:
                    ln.root(pool, i)
                pool.wait_ge(power_set, 1)
                pool.wait_ge(bn_var_ready, 1)
                pool.tensor_tensor(rstd[:, :], var_eps[:, :], bn_scale_power[:, :], ALU.pow).then_inc(bn_rstd_ready, 1)

            @block.tensor
            def _(pe):
                with pe.Fori(0, PAIRS) as i:
                    pe.wait_ge(pair_copied, i)
                    ln.transposed(pe, pair_bank, ident, i).then_inc(pair_turned, 1)
                pe.wait_ge(loaded, 96)
                turner.on_pe(pe)
                turner.wait_all(pe)
                for n in range(4):
                    k, ax = n // 2, n % 2
                    pe.wait_ge(fused_copied[n % 2], n // 2)
                    for h in range(H):
                        last = pe.matmul(banks[n % 2][:, h * NK:(h + 1) * NK],
                                         wq_nat[:, ax * H + h, k * P:(k + 1) * P], keysT[:, h, ax, :],
                                         start=True, stop=True)
                    last.then_inc(fused_ready[n % 2], 1)

            def copy_fused(eng, copy, par):
                for n in range(par, 4, 2):
                    eng.wait_ge(fused_ready[par], n // 2 + 1)
                    copy(fused[:, n // 2, par * H * NK:(par + 1) * H * NK], banks[par][:, :]) \
                        .then_inc(fused_copied[par], 1)

            @block.scalar
            def _(act):
                with act.Fori(0, PAIRS) as i:
                    act.wait_ge(pair_turned, i + 1)
                    act.copy(hT[:, :, bass.ds(i * 2 * P, 2 * P)],
                             pair_bank[:, :].rearrange("p (k t) -> p k t", k=KD)).then_inc(pair_copied, 1)
                turner.on_act(act)
                copy_fused(act, act.copy, 0)

            @block.vector
            def _(dve):
                with dve.Fori(0, PAIRS) as i:
                    ln.statistics(dve, i)
                    dve.wait_ge(pair_turned, i)
                    ln.apply(dve, i)
                dve.wait_ge(pair_copied, PAIRS)
                for k in range(KD):
                    for c in range(4):
                        last = dve.bn_stats(stats[:, k, c, :], hT[:, k, c * 512:(c + 1) * 512])
                bn_links.link(dve, last)
                for k in range(KD):
                    last = dve.bn_aggr(mv[:, k, :], stats[:, k, :, :].rearrange("p c s -> p (c s)"))
                bn_links.link(dve, last)
                dve.tensor_scalar(var_eps[:, :], mv[:, :, 1], LN_EPS, None, ALU.add).then_inc(bn_var_ready, 1)
                turner.on_dve(dve)
                dve.wait_ge(loaded, 96)
                dve.wait_ge(bn_rstd_ready, 1)
                bn_links.link(dve, dve.tensor_tensor(bn_scale[:, :], gamma_col[:, :], rstd[:, :], ALU.mult))
                bn_links.link(dve, dve.tensor_tensor(bn_shift[:, :], mv[:, :, 0], bn_scale[:, :], ALU.mult))
                dve.tensor_tensor(bn_shift[:, :], beta_col[:, :], bn_shift[:, :], ALU.subtract)
                copy_fused(dve, dve.tensor_copy, 1)

        xbT = s.sb("xbT", [P, KD, 2 * P])
        spare = s.sb("spare", [1, 1])
        ints = s.sb("ints", [P, P], mybir.dt.int32)
        iota = s.sb("iota", [P, P])
        best = s.sb("best", [P, 2, H, TOP])
        best_key = s.sb("best_key", [P, 2, H, TOP], U32)
        sums = s.sb("sums", [P, H, TOP, TOP])
        pick = s.sb("pick", [P, H, TOP])
        pick_at = s.sb("pick_at", [P, H, TOP], U32)
        rank = s.sb("rank", [P, 2, PICKS], U32)
        match = s.sb("match", [P, 2, PICKS, TOP])
        index = s.sb("index", [P, 2, PICKS], U32)
        high = s.sb("high", [P, 2, PICKS], U32)
        weight = s.sb("weight", [P, H, TOP])
        weight_sum = s.sb("weight_sum", [P, H])
        codes = s.sb("codes", [P, 3, 2, PICKS])
        codesT = s.sb("codesT", [P, 3, HALF])
        w_split = s.sb("w_split", [P, 2, HALF], F16)
        row_hot = [s.sb(f"row_hot{t}", [P, HALF, P], F16) for t in range(2)]
        col_hot = [s.sb(f"col_hot{t}", [P, 2, HALF, R], F16) for t in range(2)]
        sim_bank = [s.ps(f"sim{n}", [P, 512]) for n in range(2)]
        act_bank = [s.ps(f"act{n}", [P, 512]) for n in range(2)]
        g_bank = [s.ps(f"g{n}", [P, 512]) for n in range(2)]
        out_bank = s.ps("out", [P, 2, D])
        turn_bank = s.ps("turn", [P, 512])
        iota_made = s.sem("iota_made")
        iota_ready = s.sem("iota_ready")
        xb_ready = s.sem("xb_ready")
        sims_ready = s.sem("sims_ready")
        sims_used = s.sem("sims_used")
        weight_in = s.sem("weight_in")
        weight_exp = s.sem("weight_exp")
        codes_ready = s.sem("codes_ready")
        codes_turned = s.sem("codes_turned")
        codes_copied = s.sem("codes_copied")
        hot_ready = s.sem("hot_ready")
        g_ready = [s.sem(f"g_ready{q}") for q in range(2)]
        g_used = [s.sem(f"g_used{q}") for q in range(2)]
        act_ready = [s.sem(f"act_ready{q}") for q in range(2)]
        act_used = [s.sem(f"act_used{q}") for q in range(2)]
        out_ready = s.sem("out_ready")
        out_used = [s.sem(f"out_used{t}") for t in range(2)]
        PICK_LINKS, HOT_LINKS = 11, 3
        first_links = Chain(s.sem("first_links"))
        links = Chain(s.sem("links"), 2 * (PICK_LINKS + HOT_LINKS))
        block = s.block()

        @block.gpsimd
        def _(pool):
            pool.iota(ints[:, :], pattern=[[1, P]], base=0, channel_multiplier=0).then_inc(iota_made, 1)

        def batch_norm(act, n):
            for k in range(KD):
                last = act.activation(xbT[:, k, :], hT[:, k, bass.ds(n * 2 * P, 2 * P)], ACT.Identity,
                                      bias=bn_shift[:, k:k + 1], scale=bn_scale[:, k:k + 1])
            last.then_inc(xb_ready, 1)

        @block.tensor
        def _(pe):
            def similarities(i, t):
                n = 2 * i + t
                pe.wait_ge(xb_ready, i + 1)
                pe.wait_ge(sims_used, n)
                for ax in range(2):
                    for k in range(KD):
                        last = pe.matmul(sim_bank[ax][:, :], xbT[:, k, t * P:(t + 1) * P],
                                         fused[:, k, ax * 512:(ax + 1) * 512], start=(k == 0), stop=(k == KD - 1))
                last.then_inc(sims_ready, 1)

            def turn_codes(i, t):
                n = 2 * i + t
                pe.wait_ge(codes_ready, n + 1)
                pe.wait_ge(codes_copied, n)
                for m in range(3):
                    last = pe.transpose(turn_bank[:, m * P:(m + 1) * P],
                                        codes[:, m, :, :].rearrange("p a n -> p (a n)"), ident[:, :])
                last.then_inc(codes_turned, 1)

            similarities(0, 0)
            turn_codes(0, 0)
            similarities(0, 1)
            with pe.Fori(0, PAIRS) as i:
                def activations(u):
                    q = u % 2
                    pe.wait_ge(act_used[q], 8 * i + u // 2)
                    for j in range(2):
                        for k in range(KD):
                            last = pe.matmul(act_bank[q][:, j * 2 * P:(j + 1) * 2 * P], kiT[:, k, 2 * u + j, :],
                                             hT[:, k, bass.ds(i * 2 * P, 2 * P)], start=(k == 0), stop=(k == KD - 1))
                    last.then_inc(act_ready[q], 1)

                def weights(t):
                    n = 2 * i + t
                    pe.wait_ge(hot_ready, n + 1)
                    for m in range(GU):
                        for q in range(2):
                            rows = slice(q * HALF, (q + 1) * HALF)
                            pe.wait_ge(g_used[q], GU * n + m)
                            for j in range(GT):
                                for part in range(2):
                                    last = pe.matmul(g_bank[q][:, j * R:(j + 1) * R], row_hot[t][rows, GT * m + j, :],
                                                     col_hot[t][rows, part, GT * m + j, :],
                                                     start=(part == 0), stop=(part == 1))
                            last.then_inc(g_ready[q], 1)

                def outputs(t):
                    n = 2 * i + t
                    for q in range(2):
                        pe.wait_ge(g_used[q], GU * n + GU)
                    pe.wait_ge(out_used[t], i)
                    for r in range(R):
                        last = pe.matmul(out_bank[:, t, :], gel[:, r, t * P:(t + 1) * P], ko[:, r, :],
                                         start=(r == 0), stop=(r == R - 1))
                    last.then_inc(out_ready, 1)

                for u in range(4):
                    activations(u)
                turn_codes(i, 1)
                for u in range(4, 16):
                    activations(u)
                weights(0)
                similarities(i + 1, 0)
                outputs(0)
                turn_codes(i + 1, 0)
                weights(1)
                similarities(i + 1, 1)
                outputs(1)

        @block.scalar
        def _(act):
            def exponentials(i, t):
                n = 2 * i + t
                act.wait_ge(weight_in, n + 1)
                act.activation(weight[:, :, :], weight[:, :, :], ACT.Exp).then_inc(weight_exp, 1)

            batch_norm(act, 0)
            exponentials(0, 0)
            exponentials(0, 1)
            with act.Fori(0, PAIRS) as i:
                act.wait_ge(sims_ready, 2 * i + 2)
                batch_norm(act, i + 1)
                act.wait_ge(out_ready, 2 * i)
                for u in range(16):
                    q = u % 2
                    act.wait_ge(act_ready[q], 8 * i + u // 2 + 1)
                    act.activation(gel[:, 2 * u:2 * u + 2, :].rearrange("p r t -> p (r t)"), act_bank[q][:, :],
                                   ACT.Gelu).then_inc(act_used[q], 1)
                exponentials(i + 1, 0)
                exponentials(i + 1, 1)

        @block.vector
        def _(dve):
            def choose(chain, i, t):
                n = 2 * i + t
                dve.wait_ge(sims_ready, n + 1)
                dve.memset(spare[:, :], 0.0)
                for ax in range(2):
                    for h in range(H):
                        last = dve.max(best[:, ax, h, :], sim_bank[ax][:, h * NK:(h + 1) * NK])
                chain.link(dve, last)
                dve.memset(spare[:, :], 0.0)
                for ax in range(2):
                    for h in range(H):
                        last = dve.max_index(best_key[:, ax, h, :], best[:, ax, h, :],
                                             sim_bank[ax][:, h * NK:(h + 1) * NK])
                last.then_inc(sims_used, 1)
                chain.link(dve, dve.tensor_tensor(
                    sums[:, :, :, :], best[:, 0, :, :].unsqueeze(3).broadcast_to([P, H, TOP, TOP]),
                    best[:, 1, :, :].unsqueeze(2).broadcast_to([P, H, TOP, TOP]), ALU.add))
                dve.memset(spare[:, :], 0.0)
                for h in range(H):
                    last = dve.max(pick[:, h, :], sums[:, h, :, :].rearrange("p a b -> p (a b)"))
                chain.link(dve, last)
                dve.tensor_tensor(weight[:, :, :], pick[:, :, :], pick[:, :, 0:1].broadcast_to([P, H, TOP]),
                                  ALU.subtract).then_inc(weight_in, 1)
                for h in range(H):
                    last = dve.max_index(pick_at[:, h, :], pick[:, h, :], sums[:, h, :, :].rearrange("p a b -> p (a b)"))
                chain.link(dve, last)
                dve.tensor_single_scalar(rank[:, 0, :], pick_at[:, :, :].rearrange("p h k -> p (h k)"), 3,
                                         ALU.logical_shift_right)
                chain.link(dve, dve.tensor_single_scalar(rank[:, 1, :], pick_at[:, :, :].rearrange("p h k -> p (h k)"), 7,
                                                         ALU.bitwise_and))
                chain.link(dve, dve.tensor_tensor(
                    match[:, :, :, :].rearrange("p a n k -> p (a n) k"),
                    rank[:, :, :].rearrange("p a n -> p (a n)").unsqueeze(2).broadcast_to([P, 2 * PICKS, TOP]),
                    iota[:, 0:TOP].unsqueeze(1).broadcast_to([P, 2 * PICKS, TOP]), ALU.is_equal))
                mv4 = match[:, :, :, :].rearrange("p a (h n) k -> p (a h) n k", h=H)
                chain.link(dve, dve.tensor_tensor(
                    mv4, mv4, best_key[:, :, :, :].rearrange("p a h k -> p (a h) k").unsqueeze(2)
                    .broadcast_to([P, 2 * H, TOP, TOP]), ALU.mult))
                with nc.allow_low_precision(reason="one key below 64 and seven zeros: exact"):
                    chain.link(dve, dve.tensor_reduce(index[:, :, :].rearrange("p a n -> p (a n)"),
                                                      match[:, :, :, :].rearrange("p a n k -> p (a n) k"), AX.X, ALU.add))
                dve.tensor_scalar(high[:, 0, :], index[:, 1, :], 1, 6, ALU.bitwise_and, ALU.logical_shift_left)
                chain.link(dve, dve.tensor_single_scalar(high[:, 1, :], index[:, 1, :], 1, ALU.logical_shift_right))
                dve.wait_ge(codes_turned, n)
                for d in range(2):
                    dve.tensor_tensor(codes[:, 0, d, :], high[:, 0, :], index[:, 0, :], ALU.add)
                    dve.tensor_copy(codes[:, 1, d, :], high[:, 1, :])
                dve.wait_ge(weight_exp, n + 1)
                chain.link(dve, dve.tensor_reduce(weight_sum[:, :], weight[:, :, :], AX.X, ALU.add))
                chain.link(dve, dve.reciprocal(weight_sum[:, :], weight_sum[:, :]))
                for d in range(2):
                    last = dve.scalar_tensor_tensor(
                        codes[:, 2, d, :].rearrange("p (h k) -> p h k", h=H), weight[:, :, :], W_SCALE,
                        weight_sum[:, :].unsqueeze(2).broadcast_to([P, H, TOP]), ALU.mult, ALU.mult)
                last.then_inc(codes_ready, 1)

            def one_hot(chain, i, t):
                n = 2 * i + t
                dve.wait_ge(codes_turned, n + 1)
                turned = turn_bank[:, 0:3 * P].rearrange("p (m a t) -> p m a t", m=3, a=2)
                for q in range(2):
                    rows = slice(q * HALF, (q + 1) * HALF)
                    last = dve.tensor_copy(codesT[rows, :, :], turned[rows, :, q, :])
                last.then_inc(codes_copied, 1)
                dve.wait_ge(codes_copied, n + 1)
                if chain is not first_links:
                    dve.wait_ge(g_ready[1], GU * (n - 1))
                chain.link(dve, dve.tensor_copy(w_split[:, 0, :], codesT[:, 2, :]))
                dve.tensor_tensor(w_split[:, 1, :], codesT[:, 2, :], w_split[:, 0, :], ALU.subtract)
                match_r, w_low = col_hot[t][:, 0, :, :], col_hot[t][:, 1, :, :]
                chain.link(dve, dve.tensor_tensor(
                    match_r, codesT[:, 1, :].unsqueeze(2).broadcast_to([P, HALF, R]),
                    iota[:, 0:R].unsqueeze(1).broadcast_to([P, HALF, R]), ALU.is_equal))
                chain.link(dve, dve.tensor_tensor(
                    w_low, match_r, w_split[:, 1, :].unsqueeze(2).broadcast_to([P, HALF, R]), ALU.mult))
                dve.tensor_tensor(match_r, match_r, w_split[:, 0, :].unsqueeze(2).broadcast_to([P, HALF, R]), ALU.mult)
                dve.tensor_tensor(row_hot[t][:, :, :], codesT[:, 0, :].unsqueeze(2).broadcast_to([P, HALF, P]),
                                  iota[:, :].unsqueeze(1).broadcast_to([P, HALF, P]), ALU.is_equal).then_inc(hot_ready, 1)

            def apply_weights(i, t):
                n = 2 * i + t
                for q in range(2):
                    dve.wait_ge(act_used[q], 8 * i + 8)
                for m in range(GU):
                    for q in range(2):
                        t0 = t * P + q * HALF + GT * m
                        g = gel[:, :, t0:t0 + GT].rearrange("p r t -> p t r")
                        dve.wait_ge(g_ready[q], GU * n + m + 1)
                        dve.scalar_tensor_tensor(g, g_bank[q][:, :].rearrange("p (t r) -> p t r", r=R), 1.0 / W_SCALE, g,
                                                 ALU.mult, ALU.mult).then_inc(g_used[q], 1)

            def residual(i, t):
                dve.wait_ge(out_ready, 2 * i + t + 1)
                xb = x[:, bass.ds(2 * i + t, 1), :].rearrange("p a d -> p (a d)")
                dve.tensor_tensor(xb, out_bank[:, t, :], xb, ALU.add).then_inc(out_used[t], 1)

            dve.wait_ge(iota_made, 1)
            dve.tensor_copy(iota[:, :], ints[:, :]).then_inc(iota_ready, 1)
            dve.wait_ge(iota_ready, 1)
            choose(first_links, 0, 0)
            one_hot(first_links, 0, 0)
            choose(first_links, 0, 1)
            with dve.Fori(0, PAIRS) as i:
                links.begin(i)
                one_hot(links, i, 1)
                apply_weights(i, 0)
                choose(links, i + 1, 0)
                residual(i, 0)
                apply_weights(i, 1)
                one_hot(links, i + 1, 0)
                choose(links, i + 1, 1)
                residual(i, 1)
                links.end()


def stage_experts(nc, x, ident, ones_row, gate_w, gate_b, w_gate, w_up, w_down, s_gate, s_up, s_down):
    NE = 16
    TOP = 8
    ROUTE_SCALE = 2.826
    HID = 256
    TOKENS = NB * P
    GROUP = 512
    GROUPS = TOKENS // GROUP
    TAKEN = -3.0e38
    with ExitStack() as ctx:
        s = Scope(nc, ctx, "m")
        gw = s.sb("gw", [NE, D])
        gwT = s.sb("gwT", [P, KD, NE])
        gb_row = s.sb("gb_row", [1, NE])
        gate_bias = s.sb("gate_bias", [P, NE])
        xnT_pair = s.sb("xnT_pair", [P, KD, 2 * P])
        xnT = s.sb("xnT", [P, KD, TOKENS])
        score = s.sb("score", [P, 2, NE])
        chosen_by = s.sb("chosen_by", [P, 2, NE])
        top = s.sb("top", [P, 2, TOP])
        left = s.sb("left", [P, 2, NE])
        total = s.sb("total", [P, 2])
        combine = s.sb("combine", [P, NB, NE + 1])
        w_nat = s.sb("w_nat", [P, 6, D])
        wT = [s.sb(f"wT{n}", [P, 3, KD, HID]) for n in range(2)]
        silu = s.sb("silu", [P, 2, GROUP])
        hidden = s.sb("hidden", [P, 2, 2, GROUP])
        ln = LayerNorm(s, x)
        gate_bank = [s.ps(f"gate{n}", [P, GROUP]) for n in range(2)]
        up_bank = [s.ps(f"up{n}", [P, GROUP]) for n in range(2)]
        y_bank = [s.ps(f"y{n}", [P, 2 * D]) for n in range(2)]
        turn_bank = s.ps("turn", [P, 512])
        route_bank = s.ps("route", [P, 512])
        loaded = s.sem("loaded")
        gate_T = s.sem("gate_T")
        gate_T_copied = s.sem("gate_T_copied")
        ones_set = s.sem("ones_set")
        pair_turned = s.sem("pair_turned")
        pair_copied = s.sem("pair_copied")
        all_copied = s.sem("all_copied")
        logits_ready = s.sem("logits_ready")
        logits_exp = s.sem("logits_exp")
        routed = s.sem("routed")
        w_loaded = s.sem("w_loaded")
        w_turned = s.sem("w_turned")
        w_copied = s.sem("w_copied")
        gate_ready = [s.sem(f"gate_ready{n}") for n in range(2)]
        up_ready = [s.sem(f"up_ready{n}") for n in range(2)]
        silu_ready = [s.sem(f"silu_ready{n}") for n in range(2)]
        hidden_ready = [s.sem(f"hidden_ready{n}") for n in range(2)]
        y_ready = [s.sem(f"y_ready{n}") for n in range(2)]
        y_added = [s.sem(f"y_added{n}") for n in range(2)]
        links = Chain(s.sem("links"), 9)
        block = s.block()
        UN = GROUPS

        @block.sync
        def _(sp):
            sp.dma_start(gw[:, :], gate_w).then_inc(loaded, 16)
            sp.dma_start(gb_row[:, :], gate_b.rearrange("(a d) -> a d", a=1)).then_inc(loaded, 16)

            def load(n, parts):
                if n is not None:
                    sp.wait_ge(w_turned, n)
                for m, w in enumerate(parts):
                    sp.dma_start(w_nat[:, 2 * m:2 * m + 2, :], w.rearrange("(t p) n -> p t n", p=P)).then_inc(w_loaded, 16)

            load(None, (w_gate[0], w_up[0], w_down[0]))
            with sp.Fori(1, NE) as e:
                load(3 * e, [w[bass.ds(e, 1), :, :].rearrange("a o n -> (a o) n") for w in (w_gate, w_up, w_down)])
            load(3 * NE, (s_gate, s_up, s_down))
            sp.wait_ge(w_loaded, 48 * (NE + 1))

        @block.gpsimd
        def _(pool):
            ln.setup(pool)
            pool.memset(combine[:, :, NE:NE + 1], 1.0).then_inc(ones_set, 1)
            with pool.Fori(0, PAIRS) as i:
                ln.root(pool, i)

        def turn_weights(pe, e, m):
            pe.wait_ge(w_loaded, 48 * e + 16 * 3)
            pe.wait_ge(w_copied, 3 * e + m)
            for k in range(KD):
                for t in range(2):
                    last = pe.transpose(turn_bank[:, k * HID + t * P:k * HID + (t + 1) * P],
                                        w_nat[:, 2 * m + t, k * P:(k + 1) * P], ident[:, :])
            last.then_inc(w_turned, 1)

        def expert_on_pe(pe, e, par, last_one=False):
            w = wT[par]
            pe.wait_ge(w_copied, 3 * e + 3)

            def hidden_unit(g, m):
                pe.wait_ge(silu_ready[m], UN * e + g)
                for k in range(KD):
                    last = pe.matmul(gate_bank[m][:, :], w[:, 0, k, m * P:(m + 1) * P],
                                     xnT[:, k, g * GROUP:(g + 1) * GROUP], start=(k == 0), stop=(k == KD - 1))
                last.then_inc(gate_ready[m], 1)
                pe.wait_ge(hidden_ready[m], UN * e + g)
                for k in range(KD):
                    last = pe.matmul(up_bank[m][:, :], w[:, 1, k, m * P:(m + 1) * P],
                                     xnT[:, k, g * GROUP:(g + 1) * GROUP], start=(k == 0), stop=(k == KD - 1))
                last.then_inc(up_ready[m], 1)

            def down(g):
                for m in range(2):
                    pe.wait_ge(hidden_ready[m], UN * e + g + 1)
                for n in range(2):
                    pe.wait_ge(y_added[n], UN * e + g)
                    for t in range(2):
                        for k in range(2):
                            last = pe.matmul(y_bank[n][:, t * D:(t + 1) * D],
                                             hidden[:, g % 2, k, (2 * n + t) * P:(2 * n + t + 1) * P],
                                             w[:, 2, k, :], start=(k == 0), stop=(k == 1))
                    last.then_inc(y_ready[n], 1)

            for g in range(GROUPS):
                hidden_unit(g, 0)
                hidden_unit(g, 1)
                if g >= 1:
                    down(g - 1)
                if g < 3 and not last_one:
                    turn_weights(pe, e + 1, g)
            down(GROUPS - 1)

        @block.tensor
        def _(pe):
            pe.wait_ge(loaded, 32)
            for k in range(KD):
                last = pe.transpose(gate_bank[0][:, k * NE:(k + 1) * NE], gw[:, k * P:(k + 1) * P], ident[0:NE, 0:NE])
            last.then_inc(gate_T, 1)
            pe.matmul(gate_bank[1][:, 0:NE], ones_row[:, :], gb_row[:, :], start=True, stop=True).then_inc(gate_T, 1)
            for m in range(3):
                turn_weights(pe, 0, m)
            pe.wait_ge(gate_T_copied, 2)
            with pe.Fori(0, PAIRS) as i:
                pe.wait_ge(pair_copied, i)
                pe.wait_ge(all_copied, i)
                ln.transposed(pe, up_bank[0], ident, i).then_inc(pair_turned, 1)
                pe.wait_ge(pair_copied, i + 1)
                for b in range(2):
                    for k in range(KD):
                        last = pe.matmul(route_bank[:, b * NE:(b + 1) * NE], xnT_pair[:, k, b * P:(b + 1) * P],
                                         gwT[:, k, :], start=(k == 0), stop=(k == KD - 1))
                last.then_inc(logits_ready, 1)
                pe.wait_ge(logits_exp, i + 1)
            pe.wait_ge(all_copied, PAIRS)
            with pe.Fori(0, NE // 2) as h:
                for par in range(2):
                    expert_on_pe(pe, 2 * h + par, par)
            expert_on_pe(pe, NE, 0, last_one=True)

        @block.scalar
        def _(act):
            def copy_weights(e, par, m):
                act.wait_ge(w_turned, 3 * e + m + 1)
                act.copy(wT[par][:, m, :, :].rearrange("p k n -> p (k n)"), turn_bank[:, :]).then_inc(w_copied, 1)

            for m in range(3):
                copy_weights(0, 0, m)
            with act.Fori(0, PAIRS) as i:
                act.wait_ge(pair_turned, i + 1)
                act.copy(xnT_pair[:, :, :].rearrange("p k t -> p (k t)"), up_bank[0][:, :]).then_inc(pair_copied, 1)
                act.wait_ge(logits_ready, i + 1)
                act.wait_ge(routed, i)
                act.activation(score[:, :, :].rearrange("p b e -> p (b e)"), route_bank[:, 0:2 * NE], ACT.Exp,
                               scale=-1.0).then_inc(logits_exp, 1)

            def expert_on_act(e, par, last_one=False):
                for g in range(GROUPS):
                    for m in range(2):
                        act.wait_ge(gate_ready[m], UN * e + g + 1)
                        act.wait_ge(hidden_ready[m], UN * e + g)
                        act.activation(silu[:, m, :], gate_bank[m][:, :], ACT.Silu).then_inc(silu_ready[m], 1)
                    if g < 3 and not last_one:
                        if g == 0:
                            act.wait_ge(y_added[1], UN * e)
                        copy_weights(e + 1, 1 - par, g)

            with act.Fori(0, NE // 2) as h:
                for par in range(2):
                    expert_on_act(2 * h + par, par)
            expert_on_act(NE, 0, last_one=True)

        @block.vector
        def _(dve):
            dve.wait_ge(gate_T, 2)
            dve.tensor_copy(gwT[:, :, :].rearrange("p k n -> p (k n)"), gate_bank[0][:, 0:KD * NE]).then_inc(gate_T_copied, 1)
            dve.tensor_copy(gate_bias[:, :], gate_bank[1][:, 0:NE]).then_inc(gate_T_copied, 1)
            dve.wait_ge(gate_T_copied, 2)
            with dve.Fori(0, PAIRS) as i:
                links.begin(i)
                ln.statistics(dve, i)
                dve.wait_ge(pair_turned, i)
                ln.apply(dve, i)
                dve.wait_ge(pair_copied, i + 1)
                dve.tensor_copy(xnT[:, :, bass.ds(i * 2 * P, 2 * P)],
                                up_bank[0][:, :].rearrange("p (k t) -> p k t", k=KD)).then_inc(all_copied, 1)
                dve.wait_ge(logits_exp, i + 1)
                links.link(dve, dve.tensor_scalar(score[:, :, :], score[:, :, :], 1.0, None, ALU.add))
                links.link(dve, dve.reciprocal(score[:, :, :], score[:, :, :]))
                links.link(dve, dve.tensor_tensor(chosen_by[:, :, :], score[:, :, :],
                                                  gate_bias[:, :].unsqueeze(1).broadcast_to([P, 2, NE]), ALU.add))
                ln.nudge(dve)
                for b in range(2):
                    last = dve.max(top[:, b, :], chosen_by[:, b, :])
                links.link(dve, last)
                ln.nudge(dve)
                for b in range(2):
                    last = dve.match_replace(left[:, b, :], top[:, b, :], chosen_by[:, b, :], TAKEN)
                links.link(dve, last)
                links.link(dve, dve.tensor_tensor(left[:, :, :], left[:, :, :], chosen_by[:, :, :], ALU.not_equal))
                links.link(dve, dve.tensor_tensor(score[:, :, :], score[:, :, :], left[:, :, :], ALU.mult))
                links.link(dve, dve.tensor_reduce(total[:, :], score[:, :, :], AX.X, ALU.add))
                links.link(dve, dve.reciprocal(total[:, :], total[:, :]))
                for b in range(2):
                    last = dve.tensor_scalar(combine[:, bass.ds(2 * i + b, 1), 0:NE].rearrange("p a e -> p (a e)"),
                                             score[:, b, :], total[:, b:b + 1], ROUTE_SCALE, ALU.mult, ALU.mult)
                last.then_inc(routed, 1)
                links.end()
            dve.wait_ge(routed, PAIRS)
            dve.wait_ge(ones_set, 1)

            def expert_on_dve(e):
                def add(g):
                    for n in range(2):
                        dve.wait_ge(y_ready[n], UN * e + g + 1)
                        for t in range(2):
                            tile = 4 * g + 2 * n + t
                            weight = combine[:, tile, bass.ds(e, 1)] if not isinstance(e, int) else combine[:, tile, e:e + 1]
                            last = dve.scalar_tensor_tensor(x[:, tile, :], y_bank[n][:, t * D:(t + 1) * D], weight,
                                                            x[:, tile, :], ALU.mult, ALU.add)
                        last.then_inc(y_added[n], 1)

                for g in range(GROUPS):
                    for m in range(2):
                        dve.wait_ge(silu_ready[m], UN * e + g + 1)
                        dve.wait_ge(up_ready[m], UN * e + g + 1)
                        dve.tensor_tensor(hidden[:, g % 2, m, :], silu[:, m, :], up_bank[m][:, :], ALU.mult) \
                            .then_inc(hidden_ready[m], 1)
                    if g >= 1:
                        add(g - 1)
                add(GROUPS - 1)

            with dve.Fori(0, NE // 2) as h:
                for par in range(2):
                    expert_on_dve(2 * h + par)
            expert_on_dve(NE)


def stage_constants(nc, ident, ident_bf, causal_bf, chunk_bf, ones_row, half_mask, head_mask):
    with ExitStack() as ctx:
        s = Scope(nc, ctx, "c")
        filled = s.sem("filled")
        lower_cut = s.sem("lower_cut")
        block = s.block()

        @block.gpsimd
        def _(pool):
            for m in (ident, ident_bf, causal_bf, chunk_bf):
                pool.memset(m[:, :], 0.0).then_inc(filled, 1)
            for m in (ones_row, half_mask, head_mask):
                pool.memset(m[:, :], 1.0).then_inc(filled, 1)
            pool.wait_ge(filled, 7)
            for m in (ident, ident_bf):
                pool.affine_select(out=m[:, :], in_=m[:, :], compare_op=ALU.not_equal, fill=1.0, base=0,
                                   pattern=[[-1, P]], channel_multiplier=1)
            pool.affine_select(out=causal_bf[:, :], in_=causal_bf[:, :], compare_op=ALU.is_ge, fill=NEG, base=0,
                               pattern=[[0, 4], [-1, P]], channel_multiplier=1)
            cv = chunk_bf[:, :].rearrange("p (j c k) -> p j c k", j=4, c=2)
            pool.affine_select(out=cv[:, :, 0, :], in_=cv[:, :, 0, :], compare_op=ALU.is_ge, fill=NEG, base=63,
                               pattern=[[0, 4], [0, 64]], channel_multiplier=-1)
            pool.affine_select(out=cv[:, :, 1, :], in_=cv[:, :, 1, :], compare_op=ALU.is_ge, fill=NEG, base=-64,
                               pattern=[[0, 4], [0, 64]], channel_multiplier=1)
            for m, heads in ((half_mask, 2), (head_mask, 8)):
                pool.affine_select(out=m[:, :], in_=m[:, :], compare_op=ALU.is_ge, fill=0.0, base=0,
                                   pattern=[[-(P // heads), heads]], channel_multiplier=1).then_inc(lower_cut, 1)
            pool.wait_ge(lower_cut, 2)
            for m, heads in ((half_mask, 2), (head_mask, 8)):
                pool.affine_select(out=m[:, :], in_=m[:, :], compare_op=ALU.is_ge, fill=0.0, base=P // heads - 1,
                                   pattern=[[P // heads, heads]], channel_multiplier=-1)


def decoder(nc, out, a):
    with ExitStack() as ctx:
        s = Scope(nc, ctx, "g")
        x = s.sb("x", [P, NB + 4, D])
        ident = s.sb("ident", [P, P])
        ones_row = s.sb("ones_row", [1, P])
        half_mask = s.sb("half_mask", [P, 2])
        head_mask = s.sb("head_mask", [P, 8])
        stored = s.sem("stored")
        with ExitStack() as masks_ctx:
            m = Scope(nc, masks_ctx, "m")
            ident_bf = m.sb("ident_bf", [P, P], BF16)
            causal_bf = m.sb("causal_bf", [P, 4 * P], BF16)
            chunk_bf = m.sb("chunk_bf", [P, 4 * P], BF16)
            stage_constants(nc, ident, ident_bf, causal_bf, chunk_bf, ones_row, half_mask, head_mask)
            stage_causal_attention(nc, x, ident, ones_row, ident_bf, causal_bf, half_mask, a["x"], a["L0_attn_w_q"],
                                   a["L0_attn_w_k"], a["L0_attn_w_v"], a["L0_attn_w_u"], a["L0_attn_b_u"])
            stage_chunked_attention(nc, x, ident, ones_row, ident_bf, chunk_bf, head_mask, a["ctx_1024"],
                                    a["L0_xattn_in_proj_w"], a["L0_xattn_in_proj_b"], a["L0_xattn_out_proj_w"],
                                    a["L0_xattn_out_proj_b"])
        stage_product_keys(nc, x, ident, a["L0_ffn_gamma"], a["L0_ffn_beta"], a["L0_ffn_w_q"], a["L0_ffn_keys"],
                           a["L0_ffn_key_in"], a["L0_ffn_key_out"])
        stage_gated_attention(nc, x, ident, ones_row, head_mask, a["L1_attn_Wq"], a["L1_attn_bq"],
                              a["L1_attn_Wk"], a["L1_attn_bk"], a["L1_attn_Wv"], a["L1_attn_bv"],
                              a["L1_attn_Wo"], a["L1_attn_bo"], a["L1_attn_g"], a["L1_attn_Wg1"],
                              a["L1_attn_bg1"], a["L1_attn_Wg2"], a["L1_attn_bg2"])
        stage_aligned_attention(nc, x, ident, ones_row, a["ctx_1024"], a["L1_xattn_W"], a["L1_xattn_b"])
        stage_experts(nc, x, ident, ones_row, a["L1_ffn_gate_w"], a["L1_ffn_expert_bias"], a["L1_ffn_w_gate"],
                      a["L1_ffn_w_up"], a["L1_ffn_w_down"], a["L1_ffn_shared_gate_w"],
                      a["L1_ffn_shared_up_w"], a["L1_ffn_shared_down_w"])
        block = s.block()

        @block.sync
        def _(sp):
            sp.dma_start(out.rearrange("b t d -> t b d"), x[:, 0:NB, :]).then_inc(stored, 16)
            sp.wait_ge(stored, 16)


_INS = ['x', 'ctx_1024', 'L0_attn_w_q', 'L0_attn_w_k', 'L0_attn_w_v', 'L0_attn_w_u', 'L0_attn_b_u',
        'L0_xattn_in_proj_w', 'L0_xattn_in_proj_b', 'L0_xattn_out_proj_w', 'L0_xattn_out_proj_b',
        'L0_ffn_gamma', 'L0_ffn_beta', 'L0_ffn_w_q', 'L0_ffn_keys', 'L0_ffn_key_in', 'L0_ffn_key_out',
        'L1_attn_Wq', 'L1_attn_bq', 'L1_attn_Wk', 'L1_attn_bk', 'L1_attn_Wv', 'L1_attn_bv', 'L1_attn_Wo',
        'L1_attn_bo', 'L1_attn_g', 'L1_attn_Wg1', 'L1_attn_bg1', 'L1_attn_Wg2', 'L1_attn_bg2',
        'L1_xattn_W', 'L1_xattn_b', 'L1_ffn_gate_w', 'L1_ffn_expert_bias', 'L1_ffn_w_gate', 'L1_ffn_w_up',
        'L1_ffn_w_down', 'L1_ffn_shared_gate_w', 'L1_ffn_shared_up_w', 'L1_ffn_shared_down_w']


def kernel(**inputs):
    import numpy as np
    from concourse import bacc
    from concourse.bass_utils import run_bass_kernel_spmd

    nc = bacc.Bacc("TRN2", target_bir_lowering=False, num_devices=1)
    arrays, args = {}, {}
    for name in _INS:
        a = np.ascontiguousarray(inputs[name])
        arrays[f"in_{name}"] = a
        args[name] = nc.dram_tensor(f"in_{name}", a.shape, mybir.dt.from_np(a.dtype), kind="ExternalInput").ap()
    out = nc.dram_tensor("out", (NB, P, D), F32, kind="ExternalOutput").ap()
    decoder(nc, out, args)
    r = run_bass_kernel_spmd(nc, [arrays], core_ids=[0])
    return r.results[0]["out"]
```

```python
from contextlib import ExitStack

import concourse.bass as bass
from concourse import mybir

P = 128
D = 256
KD = D // P
NB = 16
PAIRS = NB // 2
NH = 16
UNITS = 8
LN_EPS = 1e-5
NEG = -1.0e30

ALU = mybir.AluOpType
ACT = mybir.ActivationFunctionType
AX = mybir.AxisListType
F32 = mybir.dt.float32
F32R = mybir.dt.float32r
BF16 = mybir.dt.bfloat16
F16 = mybir.dt.float16
U32 = mybir.dt.uint32


class Signal:

    def __init__(self, sem, per):
        self.sem, self.per = sem, per

    def at(self, i, k):
        return self.per * i + k + 1


class Chain:

    def __init__(self, sem, per=None, ahead=0):
        self.sem, self.per, self.ahead, self.i, self.k = sem, per, ahead, 0, 0

    def begin(self, i):
        self.i, self.k = i, self.ahead

    def link(self, eng, ins):
        self.k += 1
        ins.then_inc(self.sem, 1)
        eng.wait_ge(self.sem, (self.per or 0) * self.i + self.k)

    def end(self):
        assert self.per is None or self.k == self.per + self.ahead, (self.k, self.per, self.ahead)


class Scope:

    def __init__(self, nc, ctx, tag):
        self.nc, self.ctx, self.tag, self.sems, self.counted = nc, ctx, tag, [], []

    def sb(self, name, shape, dt=F32):
        return self.ctx.enter_context(self.nc.sbuf_tensor(f"{self.tag}_{name}", shape, dt))

    def ps(self, name, shape, dt=F32):
        return self.ctx.enter_context(self.nc.psum_tensor(f"{self.tag}_{name}", shape, dt))

    def sem(self, name):
        sem = self.ctx.enter_context(self.nc.semaphore(f"{self.tag}_{name}"))
        self.sems.append(sem)
        return sem

    def counting(self, name, per):
        self.counted.append(Signal(self.sem(name), per))
        return self.counted[-1]

    def _clear(self):
        for sem in self.sems:
            self.nc.sync.sem_clear(sem)
        self.nc.all_engine_barrier()

    def block(self):
        for signal in self.counted:
            self.nc.sync.sem_inc(signal.sem, 1)
        self.ctx.callback(self._clear)
        return self.ctx.enter_context(self.nc.Block())


class LayerNorm:

    def __init__(self, s, x):
        self.x = x
        self.links = Chain(s.sem("ln_links"), 2)
        self.stats = s.sb("ln_stats", [P, 2, 6])
        self.mv = s.sb("ln_mv", [P, 2, 2])
        self.var_eps = s.sb("ln_var_eps", [P, 2])
        self.rstd = s.sb("ln_rstd", [P, 2])
        self.power = s.sb("ln_power", [P, 2])
        self.xn = s.sb("ln_xn", [P, 2, D])
        self.spare = s.sb("ln_spare", [1, 1])
        self.var_ready = s.sem("ln_var_ready")
        self.rstd_ready = s.sem("ln_rstd_ready")
        self.xn_ready = s.sem("ln_xn_ready")
        self.power_set = s.sem("ln_power_set")

    def setup(self, pool):
        pool.memset(self.power[:, :], -0.5).then_inc(self.power_set, 1)
        pool.wait_ge(self.power_set, 1)

    def statistics(self, dve, n):
        if not exists(n):
            return
        chain = self.links
        chain.begin(n)
        for b in range(2):
            last = dve.bn_stats(self.stats[:, b, :], self.x[:, bass.ds(2 * n + b, 1), :].rearrange("p a d -> p (a d)"))
        chain.link(dve, last)
        self.nudge(dve)
        for b in range(2):
            last = dve.bn_aggr(self.mv[:, b, :], self.stats[:, b, :])
        chain.link(dve, last)
        dve.tensor_scalar(self.var_eps[:, :], self.mv[:, :, 1], LN_EPS, None, ALU.add).then_inc(self.var_ready, 1)

    def nudge(self, dve):
        dve.memset(self.spare[:, :], 0.0)

    def root(self, pool, n):
        if not exists(n):
            return
        pool.wait_ge(self.var_ready, n + 1)
        pool.tensor_tensor(self.rstd[:, :], self.var_eps[:, :], self.power[:, :], ALU.pow).then_inc(self.rstd_ready, 1)

    def apply(self, dve, n):
        if not exists(n):
            return
        dve.wait_ge(self.rstd_ready, n + 1)
        for b in range(2):
            last = dve.tensor_scalar(self.xn[:, b, :], self.x[:, bass.ds(2 * n + b, 1), :].rearrange("p a d -> p (a d)"),
                                     self.mv[:, b, 0:1], self.rstd[:, b:b + 1], ALU.subtract, ALU.mult)
        last.then_inc(self.xn_ready, 1)

    def transposed(self, pe, bank, ident, n, one=None):
        pe.wait_ge(self.xn_ready, n + 1)
        for m, b in enumerate(range(2) if one is None else (one,)):
            for k in range(KD):
                at = (k * 2 + m) * P if one is None else k * P
                last = pe.transpose(bank[:, at:at + P], self.xn[:, b, k * P:(k + 1) * P], ident[:, :])
        return last


class HeadAttention:

    def __init__(self, s, head_dim, ident, mask, attnT, gated=False, vector_copies=()):
        self.ident, self.mask, self.attnT, self.vector_copies = ident, mask, attnT, vector_copies
        per_unit = 2 if gated else 1
        self.links = Chain(s.sem("att_links"), per_unit * UNITS, ahead=per_unit)
        self.rows = 64 if head_dim == 64 else 32
        self.tile_heads = P // head_dim
        self.chunk_units = 2 if head_dim == 64 else 4
        self.chunks = UNITS // self.chunk_units
        self.score_bank = [s.ps(f"score{n}", [P, 512]) for n in range(2)]
        self.probT_bank = [s.ps(f"probT_bank{n}", [P, 512]) for n in range(2)]
        self.out_bank = s.ps("out_bank", [P, 512])
        self.neg_max = s.sb("neg_max", [P, UNITS, 4])
        self.row_sum = s.sb("row_sum", [P, UNITS, 4])
        self.norm = s.sb("norm", [P, UNITS, 4])
        self.prob = s.sb("prob", [P, 4, 4, P])
        self.probT = s.sb("probT", [P, 2, 4 * P])
        self.scored = s.counting("scored", UNITS)
        self.max_ready = s.counting("max_ready", UNITS)
        self.exp_ready = s.counting("exp_ready", UNITS)
        self.normed = s.counting("normed", UNITS)
        self.transposed = s.counting("transposed", UNITS)
        self.probT_ready = [s.counting(f"probT_ready{n}", UNITS // 2) for n in range(2)]
        self.weighted = s.counting("weighted", UNITS)
        self.out_ready = s.counting("out_ready", self.chunks + 1)
        self.projected = s.sem("projected")
        self.bias_added = s.counting("bias_added", 1)

    def pe_scores(self, pe, i, u, par, scores, first=False):
        b, g, n = u // 4, u % 4, u % 2
        if not first:
            pe.wait_ge(self.exp_ready.sem, self.exp_ready.at(i, u - 1))
        if self.mask is not None:
            ident_bf, mask_bf = self.mask
            pe.matmul(self.score_bank[n][:, :], ident_bf[:, :], mask_bf[:, :], start=True, stop=False,
                      skip_group_check=True)
        scores(par, self.score_bank[n], b, g, self.mask is None).then_inc(self.scored.sem, 1)

    def dve_max(self, dve, i, u):
        dve.wait_ge(self.scored.sem, self.scored.at(i, u + 1))
        dve.tensor_reduce(self.neg_max[:, u, :], self.score_bank[u % 2][:, :].rearrange("p (j k) -> p j k", j=4),
                          AX.X, ALU.max, negate=True).then_inc(self.max_ready.sem, 1)

    def act_exp(self, act, i, u, first=False):
        act.wait_ge(self.max_ready.sem, self.max_ready.at(i, u + 1))
        if not first:
            act.wait_ge(self.transposed.sem, self.transposed.at(i, u - 3 if u != 2 else 0))
        for j in range(4):
            last = act.activation(self.prob[:, u % 4, j, :], self.score_bank[u % 2][:, j * P:(j + 1) * P], ACT.Exp,
                                  bias=self.neg_max[:, u, j:j + 1], accum_out=self.row_sum[:, u, j:j + 1])
        last.then_inc(self.exp_ready.sem, 1)

    def dve_normalise(self, dve, i, u, par, gate):
        n = u % 4
        dve.wait_ge(self.exp_ready.sem, self.exp_ready.at(i, u + 1))
        self.links.link(dve, dve.reciprocal(self.norm[:, u, :], self.row_sum[:, u, :]))
        if gate is not None:
            self.links.link(dve, dve.tensor_tensor(self.norm[:, u, :], self.norm[:, u, :], gate(par, u // 4, u % 4), ALU.mult))
        dve.tensor_tensor(self.prob[:, n, :, :], self.prob[:, n, :, :],
                          self.norm[:, u, :].unsqueeze(2).broadcast_to([P, 4, P]), ALU.mult).then_inc(self.normed.sem, 1)

    def pe_transpose(self, pe, i, u):
        pe.wait_ge(self.normed.sem, self.normed.at(i, u + 1))
        before = self.probT_ready[u % 2]
        pe.wait_ge(before.sem, before.at(i, u // 2))
        for j in range(4):
            last = pe.transpose(self.probT_bank[u % 2][:, j * P:(j + 1) * P], self.prob[:, u % 4, j, :], self.ident[:, :])
        last.then_inc(self.transposed.sem, 1)

    def copy_probT(self, eng, i, u, copy):
        eng.wait_ge(self.transposed.sem, self.transposed.at(i, u + 1))
        eng.wait_ge(self.weighted.sem, self.weighted.at(i, max(u - 1, 0)))
        copy(self.probT[:, u % 2, :], self.probT_bank[u % 2][:, :]).then_inc(self.probT_ready[u % 2].sem, 1)

    def pe_weighted(self, pe, i, u, par, v_ap):
        b, g = u // 4, u % 4
        ready = self.probT_ready[u % 2]
        pe.wait_ge(ready.sem, ready.at(i, u // 2 + 1))
        if u % self.chunk_units == 0:
            pe.wait_ge(self.out_ready.sem, self.out_ready.at(i, u // self.chunk_units))
        for j in range(4):
            h = 4 * g + j
            shared = self.rows == 32
            row = 64 * (h % 2) if not shared else 32 * ((h % self.tile_heads) // 2)
            col = (h // self.tile_heads) % (2 * self.chunk_units if not shared else 2)
            last = pe.matmul(self.out_bank[row:row + self.rows, col * P:(col + 1) * P], v_ap(par, b, h),
                             self.probT[:, u % 2, j * P:(j + 1) * P], start=not shared or h % 2 == 0,
                             stop=not shared or h % 2 == 1)
        last.then_inc(self.weighted.sem, 1)

    def copy_out(self, copy, eng, i, c):
        eng.wait_ge(self.weighted.sem, self.weighted.at(i, (c + 1) * self.chunk_units))
        dst = self.attnT(c)
        copy(dst, self.out_bank[:, 0:dst.shape[1]]).then_inc(self.out_ready.sem, 1)


    def pe_first(self, pe, scores):
        self.pe_scores(pe, 0, 0, 0, scores, first=True)
        self.pe_scores(pe, 0, 1, 0, scores, first=True)

    def on_pe(self, pe, i, par, scores, v_ap, before, after):
        for u in range(UNITS):
            before(u)
            if u + 2 < UNITS:
                self.pe_scores(pe, i, u + 2, par, scores)
            elif exists(i + 1):
                self.pe_scores(pe, i + 1, u + 2 - UNITS, 1 - par, scores)
            self.pe_transpose(pe, i, u)
            if u >= 1:
                self.pe_weighted(pe, i, u - 1, par, v_ap)
            after(u)
        self.pe_weighted(pe, i, UNITS - 1, par, v_ap)

    def add_bias(self, pool, i, x, bias, ln):
        pool.wait_ge(ln.xn_ready, i + 1)
        pair = x[:, bass.ds(2 * i, 2), :]
        pool.tensor_tensor(pair, pair, bias[:, :].unsqueeze(1).broadcast_to([P, 2, D]), ALU.add) \
            .then_inc(self.bias_added.sem, 1)

    def pe_project(self, pe, i, terms):
        pe.wait_ge(self.out_ready.sem, self.out_ready.at(i, self.chunks))
        for b in range(2):
            pairs = terms(b)
            for n, (a, w) in enumerate(pairs):
                last = pe.matmul(self.out_bank[:, b * D:(b + 1) * D], a, w, start=(n == 0), stop=(n == len(pairs) - 1))
        last.then_inc(self.projected, 1)

    def dve_residual(self, dve, i, x):
        dve.wait_ge(self.projected, i + 1)
        dve.wait_ge(self.bias_added.sem, self.bias_added.at(i, 1))
        pair = x[:, bass.ds(2 * i, 2), :]
        dve.tensor_tensor(pair, self.out_bank[:, :].rearrange("p (b d) -> p b d", b=2), pair, ALU.add) \
            .then_inc(self.out_ready.sem, 1)

    def act_first(self, act):
        self.act_exp(act, 0, 0, first=True)
        self.act_exp(act, 0, 1, first=True)

    def on_act(self, act, i, before, after):
        for u in range(UNITS):
            before(u)
            if u + 2 < UNITS:
                self.act_exp(act, i, u + 2)
            elif exists(i + 1):
                self.act_exp(act, i + 1, u + 2 - UNITS)
            if u not in self.vector_copies:
                self.copy_probT(act, i, u, act.copy)
            after(u)

    def dve_first(self, dve, gate=None):
        self.dve_max(dve, 0, 0)
        self.dve_max(dve, 0, 1)
        self.dve_normalise(dve, 0, 0, 0, gate)

    def on_dve(self, dve, i, par, before, after, gate=None):
        self.links.begin(i)
        for u in range(UNITS):
            before(u)
            if u + 2 < UNITS:
                self.dve_max(dve, i, u + 2)
            elif exists(i + 1):
                self.dve_max(dve, i + 1, u + 2 - UNITS)
            if u + 1 < UNITS:
                self.dve_normalise(dve, i, u + 1, par, gate)
            elif exists(i + 1):
                self.dve_normalise(dve, i + 1, 0, 1 - par, gate)
            if u in self.vector_copies:
                self.copy_probT(dve, i, u, dve.tensor_copy)
            if u >= 1 and u % self.chunk_units == 0:
                self.copy_out(dve.tensor_copy, dve, i, u // self.chunk_units - 1)
            after(u)
        self.copy_out(dve.tensor_copy, dve, i, self.chunks - 1)
        if exists(i + 1):
            self.links.end()


def stage_causal_attention(nc, x, ident, ones_row, ident_bf, mask_bf, half_mask, x_in, w_q, w_k, w_v, w_u, b_u):
    HD = 64
    HW = NH * HD
    MT = HW // P
    QK_SCALE = 1.0 / HD
    SLOTS = 14
    AFTER = {0: (2, 3), 1: (4, 5), 2: (6, 7), 3: (8, 9), 5: (10, 11), 7: (12, 13)}
    with ExitStack() as ctx:
        s = Scope(nc, ctx, "a0")
        w_nat = s.sb("w_nat", [P, 3, KD, HW])
        w = [s.sb(f"w_{part}", [P, 3, KD, HW], F32R) for part in ("high", "low")]
        wu = s.sb("wu", [P, MT, D])
        bu = s.sb("bu", [P, D])
        xnT = [s.sb(f"xnT_{part}", [P, KD, 2 * P], F32R) for part in ("high", "low")]
        qT = [s.sb(f"qT{n}", [P, MT, 2 * P]) for n in range(2)]
        kM = [s.sb(f"kM{n}", [P, MT, 2, 2, P]) for n in range(2)]
        v = [s.sb(f"v{n}", [P, 2, HW]) for n in range(2)]
        attnT = s.sb("attnT", [P, 2, MT, P])
        ln = LayerNorm(s, x)
        ring = Ring(s, SLOTS)
        att = HeadAttention(s, HD, ident, (ident_bf, mask_bf),
                            lambda c: attnT[:, c // 2, 4 * (c % 2):4 * (c % 2) + 4, :].rearrange("p t q -> p (t q)"),
                            vector_copies=(0, 2, 4, 6))
        loaded = s.sem("loaded")
        high_ready = s.sem("high_ready")
        low_ready = s.sem("low_ready")
        xn_high = s.counting("xn_high", 1)
        xn_links = Chain(s.sem("xn_links"), 1)
        x_loaded = s.sem("x_loaded")
        block = s.block()

        @block.sync
        def _(sp):
            x_tiles = x_in.rearrange("b t d -> t b d")
            sp.dma_start(x[:, 0:4, :], x_tiles[:, 0:4, :]).then_inc(x_loaded, 16)
            for m, src in enumerate((w_q, w_k, w_v)):
                sp.dma_start(w_nat[:, m, :, :], src.rearrange("(k p) n -> p k n", p=P)).then_inc(loaded, 16)
            sp.dma_start(wu[:, :, :], w_u.rearrange("(k p) n -> p k n", p=P)).then_inc(loaded, 16)
            sp.dma_start(bu[:, :], on_all_partitions(b_u)).then_inc(loaded, 16)
            sp.wait_ge(x_loaded, 16)
            sp.dma_start(x[:, 4:NB, :], x_tiles[:, 4:NB, :]).then_inc(x_loaded, 16)

        @block.gpsimd
        def _(pool):
            ln.setup(pool)
            ln.root(pool, 0)
            ln.root(pool, 1)
            pool.wait_ge(loaded, 80)
            for i, _ in pairs_by_two(pool):
                att.add_bias(pool, i, x, bu, ln)
                ln.root(pool, i + 2)

        @block.tensor
        def _(pe):
            def produce(n, r):
                if not exists(n):
                    return
                bank = ring.free(pe, n, r)
                if r < 2:
                    last = ln.transposed(pe, bank, ident, n, r)
                elif r < 10:
                    which = 0 if r < 6 else 1
                    for m in range(2):
                        t = 2 * ((r - 2) % 4) + m
                        for k in range(KD):
                            last = split_product(pe, bank[:, m * 256:(m + 1) * 256],
                                                 [part[:, which, k, t * P:(t + 1) * P] for part in w],
                                                 [part[:, k, :] for part in xnT], k == 0, k == KD - 1)
                else:
                    b, half = (r - 10) // 2, (r - 10) % 2
                    for k in range(KD):
                        last = split_product(pe, bank[:, :], [part[:, k, b * P:(b + 1) * P] for part in xnT],
                                             [part[:, 2, k, half * 512:(half + 1) * 512] for part in w],
                                             k == 0, k == KD - 1)
                last.then_inc(ring.filled(r), 1)

            def produce_all(n):
                ring.wait_slot(pe, n, 0)
                ring.wait_slot(pe, n, 1)
                for r in range(2, SLOTS):
                    produce(n, r)

            produce(0, 0)
            produce(0, 1)
            pe.wait_ge(loaded, 80)
            pe.wait_ge(low_ready, 3)
            produce_all(0)
            produce(1, 0)
            produce(1, 1)

            def scores(par, bank, b, g, fresh):
                for j in range(2):
                    t = 2 * g + j
                    last = pe.matmul(bank[:, j * 2 * P:(j + 1) * 2 * P], qT[par][:, t, b * P:(b + 1) * P],
                                     kM[par][:, t, b, :, :].rearrange("p a k -> p (a k)"), start=fresh,
                                     stop=True, skip_group_check=True)
                return last

            def head_values(par, b, h):
                return v[par][:, b, h * HD:(h + 1) * HD]

            att.pe_first(pe, scores)
            for i, par in pairs_by_two(pe):
                def before(u):
                    if u == 1:
                        ring.wait_slot(pe, i, 12)
                        ring.wait_slot(pe, i, 13)
                    if u == 6 and exists(i + 1):
                        ring.wait_slot(pe, i + 1, 8)
                        ring.wait_slot(pe, i + 1, 9)

                def after(u):
                    if u == 0 and exists(i + 1):
                        ring.wait_slot(pe, i + 1, 0)
                        ring.wait_slot(pe, i + 1, 1)
                    for r in AFTER.get(u, ()):
                        produce(i + 1, r)

                att.on_pe(pe, i, par, scores, head_values, before, after)
                produce(i + 2, 0)
                produce(i + 2, 1)
                att.pe_project(pe, i, lambda b: [(attnT[:, b, t, :], wu[:, t, :]) for t in range(MT)])

        def empty(eng, n, r, par, scaled_copy):
            if not exists(n):
                return
            bank = ring.arrived(eng, n, r)
            if r < 2:
                high = scaled_copy(xnT[0][:, :, r * P:(r + 1) * P], bank[:, 0:2 * P].rearrange("p (k t) -> p k t", k=KD), 1.0)
                if r == 0:
                    high.then_inc(xn_high.sem, 1)
                    return
                xn_links.begin(n)
                xn_links.link(eng, high)
                last = low_part(eng, 1)
            elif r < 6:
                last = scaled_copy(qT[par][:, 2 * r - 4:2 * r - 2, :].rearrange("p a t -> p (a t)"), bank[:, :], QK_SCALE)
            elif r < 10:
                for a in range(2):
                    for m in range(2):
                        last = scaled_copy(kM[par][:, 2 * (r - 6) + m, :, a, :],
                                           bank[:, m * 2 * P:(m + 1) * 2 * P].rearrange("p (b k) -> p b k", b=2),
                                           half_mask[:, a:a + 1])
            else:
                b, half = (r - 10) // 2, (r - 10) % 2
                last = scaled_copy(v[par][:, b, half * 512:(half + 1) * 512], bank[:, :], 1.0)
            last.then_inc(ring.done(r), 1)

        def low_part(dve, r):
            return dve.tensor_tensor(xnT[1][:, :, r * P:(r + 1) * P],
                                     ring.bank[r][:, 0:2 * P].rearrange("p (k t) -> p k t", k=KD),
                                     xnT[0][:, :, r * P:(r + 1) * P], ALU.subtract)

        def finish_first(dve, n):
            if exists(n):
                dve.wait_ge(xn_high.sem, xn_high.at(n, 1))
                low_part(dve, 0).then_inc(ring.done(0), 1)

        @block.scalar
        def _(act):
            def scaled_copy(dst, src, scale):
                return act.activation(dst, src, ACT.Copy, scale=scale)

            empty(act, 0, 0, 0, scaled_copy)
            act.wait_ge(loaded, 80)
            for m in range(3):
                act.copy(w[0][:, m, :, :], w_nat[:, m, :, :]).then_inc(high_ready, 1)
            for r in range(2, SLOTS, 2):
                empty(act, 0, r, 0, scaled_copy)
            empty(act, 1, 0, 1, scaled_copy)
            att.act_first(act)
            for i, par in pairs_by_two(act):
                def before(u):
                    if u - 1 in AFTER:
                        empty(act, i + 1, AFTER[u - 1][0], 1 - par, scaled_copy)

                att.on_act(act, i, before, lambda u: None)
                before(UNITS)
                empty(act, i + 2, 0, par, scaled_copy)

        @block.vector
        def _(dve):
            def scaled_copy(dst, src, scale):
                return dve.tensor_scalar(dst, src, scale, None, ALU.mult)

            dve.memset(x[:, NB:NB + 2, :], 0.0)
            dve.wait_ge(x_loaded, 16)
            ln.statistics(dve, 0)
            ln.apply(dve, 0)
            ln.statistics(dve, 1)
            for r in range(1, SLOTS, 2):
                if r == 1:
                    finish_first(dve, 0)
                empty(dve, 0, r, 0, scaled_copy)
                if r == 1:
                    ln.apply(dve, 1)
                    for m in range(3):
                        dve.wait_ge(high_ready, m + 1)
                        dve.tensor_tensor(w[1][:, m, :, :], w_nat[:, m, :, :], w[0][:, m, :, :], ALU.subtract) \
                            .then_inc(low_ready, 1)
            finish_first(dve, 1)
            empty(dve, 1, 1, 1, scaled_copy)
            dve.wait_ge(x_loaded, 32)
            att.dve_first(dve)
            for i, par in pairs_by_two(dve):
                def before(u):
                    if u - 1 in AFTER:
                        empty(dve, i + 1, AFTER[u - 1][1], 1 - par, scaled_copy)

                def after(u):
                    if u == 3:
                        ln.statistics(dve, i + 2)
                    if u == 5:
                        ln.apply(dve, i + 2)
                    if u == 7:
                        before(UNITS)

                att.on_dve(dve, i, par, before, after)
                finish_first(dve, i + 2)
                empty(dve, i + 2, 1, par, scaled_copy)
                att.dve_residual(dve, i, x)


def split_product(pe, dst, left, right, first, last):
    for n, (a, b) in enumerate(((0, 0), (0, 1), (1, 0))):
        ins = pe.matmul(dst, left[a], right[b], start=first and n == 0, stop=last and n == 2)
    return ins


def masked_keys(eng, kM, kT, head_mask, b, t):
    return eng.tensor_tensor(kM[:, b, t, :, :], kT[:, b, t, :].unsqueeze(1).broadcast_to([P, 8, P]),
                             head_mask[:, :].unsqueeze(2).broadcast_to([P, 8, P]), ALU.mult)


def on_all_partitions(row):
    return row.rearrange("(a d) -> a d", a=1).broadcast_to([P, row.shape[0]])


class Ring:

    def __init__(self, s, slots):
        self.bank = [s.ps(f"ring{n}", [P, 512]) for n in range(2)]
        self.produced = [s.counting(f"produced{n}", (slots + 1 - n) // 2) for n in range(2)]
        self.emptied = [s.counting(f"emptied{n}", (slots + 1 - n) // 2) for n in range(2)]

    def free(self, pe, n, r):
        pe.wait_ge(self.emptied[r % 2].sem, self.emptied[r % 2].at(n, r // 2))
        return self.bank[r % 2]

    def filled(self, r):
        return self.produced[r % 2].sem

    def arrived(self, eng, n, r):
        eng.wait_ge(self.produced[r % 2].sem, self.produced[r % 2].at(n, r // 2 + 1))
        return self.bank[r % 2]

    def done(self, r):
        return self.emptied[r % 2].sem

    def wait_slot(self, eng, n, r):
        eng.wait_ge(self.emptied[r % 2].sem, self.emptied[r % 2].at(n, r // 2 + 1))


def pairs_by_two(eng):
    with eng.Fori(0, PAIRS // 2 - 1) as h:
        for par in range(2):
            yield 2 * h + par, par
    for par in range(2):
        yield PAIRS - 2 + par, par


def pairs_but_last(eng):
    with eng.Fori(0, PAIRS - 1) as i:
        yield i
    yield PAIRS - 1


def exists(n):
    return not isinstance(n, int) or n < PAIRS


class Turner:

    def __init__(self, s, banks, ident, name="w"):
        self.banks, self.ident, self.jobs = banks, ident, []
        self.turned = [s.sem(f"{name}_turned{n}") for n in range(2)]
        self.copied = [s.sem(f"{name}_copied{n}") for n in range(2)]
        self.high_copied = s.sem(f"{name}_high_copied")

    def weight(self, w, wT, tiles):
        for k in range(KD):
            for t in range(0, tiles, 4):
                m = min(4, tiles - t)
                self.jobs.append(([w[:, t + j, k * P:(k + 1) * P] for j in range(m)], wT[:, k, t * P:(t + m) * P]))

    def on_pe(self, pe):
        for n, (blocks, _) in enumerate(self.jobs):
            pe.wait_ge(self.copied[n % 2], n // 2)
            at = 0
            for b in blocks:
                rows = b.shape[0]
                last = pe.transpose(self.banks[n % 2][:, at:at + rows], b, self.ident[0:rows, 0:rows])
                at += rows
            last.then_inc(self.turned[n % 2], 1)

    def _copy(self, eng, copy, parity):
        for n, (blocks, dst) in enumerate(self.jobs):
            if n % 2 == parity:
                eng.wait_ge(self.turned[parity], n // 2 + 1)
                cols = sum(b.shape[0] for b in blocks)
                copy(dst, self.banks[parity][:, 0:cols]).then_inc(self.copied[parity], 1)

    def on_act(self, act):
        self._copy(act, act.copy, 0)

    def on_dve(self, dve):
        self._copy(dve, dve.tensor_copy, 1)

    def split_on_act(self, act):
        for n, (_, (high, _)) in enumerate(self.jobs):
            act.wait_ge(self.turned[n % 2], n // 2 + 1)
            act.copy(high, self.banks[n % 2][:, :]).then_inc(self.high_copied, 1)

    def split_on_dve(self, dve):
        for n, (_, (high, low)) in enumerate(self.jobs):
            dve.wait_ge(self.high_copied, n + 1)
            dve.tensor_tensor(low, self.banks[n % 2][:, :], high, ALU.subtract).then_inc(self.copied[n % 2], 1)

    def wait_all(self, pe):
        for parity in range(2):
            pe.wait_ge(self.copied[parity], len(self.jobs[parity::2]))


def values_by_parity(dve, dst, src, bias, head_dim):
    for a in range(2):
        for b in range(2):
            out, value, bias_heads = (ap.rearrange("p (h a d) -> p h a d", a=2, d=head_dim)[:, :, a, :]
                                      for ap in (dst[:, b, a, :], src[:, b * D:(b + 1) * D], bias[:, :]))
            last = dve.tensor_tensor(out, value, bias_heads, ALU.add)
    return last


def token_major(pe, dst, rows, w):
    for k in range(KD):
        last = pe.matmul(dst, rows(k), w(k), start=(k == 0), stop=(k == KD - 1))
    return last


def stage_chunked_attention(nc, x, ident, ones_row, ident_bf, mask_bf, head_mask, ctx_in, w_in, b_in, w_out, b_out):
    HD = D // NH
    NQ, NK, NV, NO = 0, D, 2 * D, 3 * D
    SLOTS = 5
    AFTER = {0: (2, 3), 7: (4,), 8: (0, 1)}
    with ExitStack() as ctx:
        s = Scope(nc, ctx, "x0")
        w_nat = s.sb("w_nat", [P, 8, D])
        wT = s.sb("wT", [P, KD, 8 * P])
        bqk = s.sb("bqk", [P, 2, 2])
        bv, bo = s.sb("bv", [P, D]), s.sb("bo", [P, D])
        ctx_sb = s.sb("ctx", [P, 2, D])
        ctxT = s.sb("ctxT", [P, KD, 2 * P])
        xnT = s.sb("xnT", [P, KD, 2 * P])
        qT = [s.sb(f"qT{n}", [P, KD, 2 * P]) for n in range(2)]
        kT = s.sb("kT", [P, 2, KD, P])
        kM = [s.sb(f"kM{n}", [P, 2, KD, 8, P]) for n in range(2)]
        v = [s.sb(f"v{n}", [P, 2, 2, D]) for n in range(2)]
        attnT = s.sb("attnT", [P, 2, KD, P])
        ln = LayerNorm(s, x)
        ring = Ring(s, SLOTS)
        att = HeadAttention(s, HD, ident, (ident_bf, mask_bf), lambda b: attnT[:, b, :, :].rearrange("p k t -> p (k t)"))
        turner = Turner(s, ring.bank, ident)
        turner.weight(w_nat, wT, 8)
        loaded = s.sem("loaded")
        ctx_loaded = s.sem("ctx_loaded")
        v_zeroed = s.sem("v_zeroed")
        k_masked = s.counting("k_masked", 2 * KD)
        block = s.block()

        @block.sync
        def _(sp):
            sp.dma_start(w_nat[:, 0:6, :], w_in.rearrange("(t p) n -> p t n", p=P)).then_inc(loaded, 16)
            sp.dma_start(w_nat[:, 6:8, :], w_out.rearrange("(t p) n -> p t n", p=P)).then_inc(loaded, 16)
            sp.dma_start(ctx_sb[:, :, :], ctx_in.rearrange("b t d -> t b d")[:, 0:2, :]).then_inc(ctx_loaded, 16)
            for c in range(2):
                sp.dma_start(bqk[:, c, :], b_in[c * D:(c + 1) * D].rearrange("(k p) -> p k", p=P),
                             allow_slow_non_contiguous=True).then_inc(loaded, 16)
            sp.dma_start(bv[:, :], on_all_partitions(b_in[2 * D:3 * D])).then_inc(loaded, 16)
            sp.dma_start(bo[:, :], on_all_partitions(b_out)).then_inc(loaded, 16)
            with sp.Fori(1, PAIRS) as n:
                ring.arrived(sp, n - 1, 1)
                sp.dma_start(ctx_sb[:, :, :], ctx_in.rearrange("b t d -> t b d")[:, bass.ds(2 * n, 2), :]) \
                    .then_inc(ctx_loaded, 16)
            sp.wait_ge(ctx_loaded, 16 * PAIRS)

        @block.gpsimd
        def _(pool):
            def mask_keys(n, par):
                ring.wait_slot(pool, n, 2)
                for b in range(2):
                    for t in range(KD):
                        masked_keys(pool, kM[par], kT, head_mask, b, t).then_inc(k_masked.sem, 1)

            ln.setup(pool)
            ln.root(pool, 0)
            ln.root(pool, 1)
            for n in range(2):
                pool.memset(v[n][:, :, :, :], 0.0).then_inc(v_zeroed, 1)
            mask_keys(0, 0)
            pool.wait_ge(loaded, 96)
            for i, par in pairs_by_two(pool):
                att.add_bias(pool, i, x, bo, ln)
                ln.root(pool, i + 2)
                if exists(i + 1):
                    mask_keys(i + 1, 1 - par)

        @block.tensor
        def _(pe):
            def produce(n, r):
                if not exists(n):
                    return
                bank = ring.free(pe, n, r)
                if r == 0:
                    last = ln.transposed(pe, bank, ident, n)
                elif r == 1:
                    pe.wait_ge(ctx_loaded, 16 * n + 16)
                    for b in range(2):
                        for k in range(KD):
                            last = pe.transpose(bank[:, k * 2 * P + b * P:k * 2 * P + (b + 1) * P],
                                                ctx_sb[:, b, k * P:(k + 1) * P], ident[:, :])
                elif r < 4:
                    w0, act = (NK, ctxT) if r == 2 else (NQ, xnT)
                    for m in range(2):
                        for k in range(KD):
                            last = pe.matmul(bank[:, m * 256:(m + 1) * 256], wT[:, k, w0 + m * P:w0 + (m + 1) * P],
                                             act[:, k, :], start=(k == 0), stop=(k == KD - 1))
                else:
                    for b in range(2):
                        last = token_major(pe, bank[:, b * D:(b + 1) * D], lambda k: ctxT[:, k, b * P:(b + 1) * P],
                                           lambda k: wT[:, k, NV:NV + D])
                last.then_inc(ring.filled(r), 1)

            def scores(par, bank, b, g, fresh):
                return pe.matmul(bank[:, :], qT[par][:, g // 2, b * P:(b + 1) * P],
                                 kM[par][:, b, g // 2, 4 * (g % 2):4 * (g % 2) + 4, :].rearrange("p a k -> p (a k)"),
                                 start=fresh, stop=True, skip_group_check=True)

            def head_values(par, b, h):
                return v[par][:, b, h % 2, 32 * (h // 2):32 * (h // 2) + 32]

            pe.wait_ge(loaded, 96)
            turner.on_pe(pe)
            turner.wait_all(pe)
            for n, r in ((0, 0), (0, 1), (0, 2), (0, 3), (0, 4), (1, 0), (1, 1)):
                if r == 2:
                    ring.wait_slot(pe, 0, 0)
                    ring.wait_slot(pe, 0, 1)
                produce(n, r)
            ring.wait_slot(pe, 0, 3)
            pe.wait_ge(k_masked.sem, k_masked.at(0, KD))
            att.pe_first(pe, scores)
            for i, par in pairs_by_two(pe):
                def before(u):
                    if u == 1:
                        ring.wait_slot(pe, i, 4)
                    if u == 2:
                        pe.wait_ge(k_masked.sem, k_masked.at(i, 2 * KD))
                    if u == 6 and exists(i + 1):
                        ring.wait_slot(pe, i + 1, 3)
                        pe.wait_ge(k_masked.sem, k_masked.at(i + 1, KD))

                def after(u):
                    if u == 0 and exists(i + 1):
                        ring.wait_slot(pe, i + 1, 0)
                        ring.wait_slot(pe, i + 1, 1)
                    for r in AFTER.get(u, ()):
                        produce(i + (1 if r >= 2 else 2), r)

                att.on_pe(pe, i, par, scores, head_values, before, after)
                after(UNITS)
                att.pe_project(pe, i, lambda b: [(attnT[:, b, k, :], wT[:, k, NO:NO + D]) for k in range(KD)])

        @block.scalar
        def _(act):
            def empty(n, r, par):
                if not exists(n):
                    return
                bank = ring.arrived(act, n, r)
                if r == 0:
                    last = act.copy(xnT[:, :, :].rearrange("p k t -> p (k t)"), bank[:, :])
                else:
                    act.wait_ge(k_masked.sem, k_masked.at(n, 0))
                    for m in range(2):
                        last = act.activation(kT[:, :, m, :],
                                              bank[:, m * 256:(m + 1) * 256].rearrange("p (b k) -> p b k", b=2),
                                              ACT.Identity, bias=bqk[:, 1, m:m + 1])
                last.then_inc(ring.done(r), 1)

            turner.on_act(act)
            act.wait_ge(v_zeroed, 2)
            for n, r in ((0, 0), (0, 2), (1, 0)):
                empty(n, r, 0)
            att.act_first(act)
            for i, par in pairs_by_two(act):
                def before(u):
                    for r in AFTER.get(u - 1, ()):
                        if r in (0, 2):
                            empty(i + (1 if r >= 2 else 2), r, 1 - par)

                att.on_act(act, i, before, lambda u: None)
                before(UNITS + 1)

        @block.vector
        def _(dve):
            def empty(n, r, par):
                if not exists(n):
                    return
                bank = ring.arrived(dve, n, r)
                if r == 1:
                    last = dve.tensor_copy(ctxT[:, :, :].rearrange("p k t -> p (k t)"), bank[:, :])
                elif r == 4:
                    last = values_by_parity(dve, v[par], bank, bv, HD)
                else:
                    for m in range(2):
                        last = dve.tensor_scalar(qT[par][:, m, :], bank[:, m * 256:(m + 1) * 256],
                                                 bqk[:, 0, m:m + 1], 1.0 / 4.0, ALU.add, ALU.mult)
                last.then_inc(ring.done(r), 1)

            ln.statistics(dve, 0)
            ln.apply(dve, 0)
            turner.on_dve(dve)
            ln.statistics(dve, 1)
            dve.wait_ge(loaded, 96)
            dve.wait_ge(v_zeroed, 2)
            for n, r in ((0, 1), (0, 3), (0, 4), (1, 1)):
                empty(n, r, 0)
                if n == 0 and r == 1:
                    ln.apply(dve, 1)
            att.dve_first(dve)
            for i, par in pairs_by_two(dve):
                def before(u):
                    for r in AFTER.get(u - 1, ()):
                        if r not in (0, 2):
                            empty(i + (1 if r >= 2 else 2), r, 1 - par)

                def after(u):
                    if u == 1:
                        ln.statistics(dve, i + 2)
                    if u == 2:
                        ln.apply(dve, i + 2)
                    if u == 7:
                        before(UNITS)

                att.on_dve(dve, i, par, before, after)
                before(UNITS + 1)
                att.dve_residual(dve, i, x)


def stage_gated_attention(nc, x, ident, ones_row, head_mask, w_q, b_q, w_k, b_k, w_v, b_v, w_o, b_o, g_in,
                          w_g1, b_g1, w_g2, b_g2):
    HD = D // NH
    GH = P
    NORM_EPS2 = 1e-24
    NQ, NV, NO, NG = 0, 2 * D, 3 * D, 4 * D
    SLOTS = 8
    AFTER = {0: (4,), 1: (3,), 3: (6, 5), 4: (0,), 5: (7,), 6: (1,), 7: (2,)}

    def ahead(r):
        return 2 if r <= 2 else 1

    with ExitStack() as ctx:
        s = Scope(nc, ctx, "a1")
        w_nat = s.sb("w_nat", [P, 9, D])
        wT = s.sb("wT", [P, KD, 9 * P])
        wg2 = s.sb("wg2", [NH, GH])
        wg2T = s.sb("wg2T", [P, NH])
        bqk, bv, bo = s.sb("bqk", [P, 2 * D]), s.sb("bv", [P, D]), s.sb("bo", [P, D])
        bg1 = s.sb("bg1", [P, 1])
        bg2, g_row = s.sb("bg2", [1, NH]), s.sb("g_row", [1, NH])
        xnT = [s.sb(f"xnT{n}", [P, KD, 2 * P]) for n in range(2)]
        qk = s.sb("qk", [P, 2, 2 * D])
        sq = s.sb("sq", [P, 2, 2 * D])
        ss = s.sb("ss", [P, 2 * 2 * NH])
        inv = s.sb("inv", [P, 2 * 2 * NH])
        inv_power = s.sb("inv_power", [P, 2 * 2 * NH])
        qT = [s.sb(f"qT{n}", [P, 2, KD, P]) for n in range(2)]
        kT = s.sb("kT", [P, 2, KD, P])
        kM = [s.sb(f"kM{n}", [P, 2, KD, 8, P]) for n in range(2)]
        v = [s.sb(f"v{n}", [P, 2, 2, D]) for n in range(2)]
        attnT = s.sb("attnT", [P, 2, KD, P])
        gelu = s.sb("gelu", [P, 2 * P])
        hsum = s.sb("hsum", [P, 2])
        hrep = s.sb("hrep", [P, 2, P])
        gate_static = s.sb("gate_static", [P, NH])
        gate = [s.sb(f"gate{n}", [P, 2, NH]) for n in range(2)]
        gate_bias = s.sb("gate_bias", [P, NH])
        ones_sq = s.sb("ones_sq", [P, P])
        ln = LayerNorm(s, x)
        ring = Ring(s, SLOTS)
        att = HeadAttention(s, HD, ident, None, lambda b: attnT[:, b, :, :].rearrange("p k t -> p (k t)"), gated=True)
        turner = Turner(s, ring.bank, ident)
        turner.weight(w_nat, wT, 9)
        turner.jobs.append(([wg2[:, :]], wg2T[:, :]))
        loaded = s.sem("loaded")
        v_zeroed = s.sem("v_zeroed")
        k_masked = s.counting("k_masked", 2 * KD)
        static_spread = s.sem("static_spread")
        static_exp = s.sem("static_exp")
        power_set = s.sem("power_set")
        ones_set = s.sem("ones_set")
        squares_ready = s.sem("squares_ready")
        inverse_ready = s.sem("inverse_ready")
        scaled = s.sem("scaled")
        hidden_spread = s.sem("hidden_spread")
        logits_exp = s.sem("logits_exp")
        square_links = Chain(s.sem("square_links"), 2)
        gate_links = Chain(s.sem("gate_links"), 4)
        first_links = Chain(s.sem("first_links"))
        block = s.block()

        @block.sync
        def _(sp):
            for n, w in enumerate((w_q, w_k, w_v, w_o)):
                sp.dma_start(w_nat[:, 2 * n:2 * n + 2, :], w.rearrange("(t p) n -> p t n", p=P)).then_inc(loaded, 16)
            sp.dma_start(w_nat[:, 8, :], w_g1).then_inc(loaded, 16)
            sp.dma_start(wg2[:, :], w_g2).then_inc(loaded, 16)
            for dst, b in ((bqk[:, 0:D], b_q), (bqk[:, D:2 * D], b_k), (bv[:, :], b_v), (bo[:, :], b_o)):
                sp.dma_start(dst, on_all_partitions(b)).then_inc(loaded, 16)
            for dst, b in ((bg2[:, :], b_g2), (g_row[:, :], g_in)):
                sp.dma_start(dst, b.rearrange("(a d) -> a d", a=1)).then_inc(loaded, 16)
            sp.dma_start(bg1[:, :], b_g1.rearrange("(p a) -> p a", a=1)).then_inc(loaded, 16)

        @block.gpsimd
        def _(pool):
            ln.setup(pool)
            pool.memset(inv_power[:, :], -0.5).then_inc(power_set, 1)
            pool.memset(ones_sq[:, :], 1.0).then_inc(ones_set, 1)
            for n in range(2):
                pool.memset(v[n][:, :, :, :], 0.0).then_inc(v_zeroed, 1)
            pool.wait_ge(power_set, 1)

            def invert(n):
                pool.wait_ge(squares_ready, n + 1)
                pool.tensor_tensor(inv[:, :], ss[:, :], inv_power[:, :], ALU.pow).then_inc(inverse_ready, 1)

            def mask_keys(n, par):
                for b in range(2):
                    ring.wait_slot(pool, n, (6, 5)[b])
                    for t in range(KD):
                        masked_keys(pool, kM[par], kT, head_mask, b, t).then_inc(k_masked.sem, 1)

            ln.root(pool, 0)
            ln.root(pool, 1)
            invert(0)
            mask_keys(0, 0)
            invert(1)
            pool.wait_ge(loaded, 13 * 16)
            for i, par in pairs_by_two(pool):
                att.add_bias(pool, i, x, bo, ln)
                ln.root(pool, i + 2)
                if exists(i + 1):
                    mask_keys(i + 1, 1 - par)
                if exists(i + 2):
                    invert(i + 2)

        @block.tensor
        def _(pe):
            def produce(n, r, par):
                if not exists(n):
                    return
                bank = ring.free(pe, n, r)
                if r == 0:
                    last = ln.transposed(pe, bank, ident, n)
                elif r in (1, 2):
                    b = r - 1
                    last = token_major(pe, bank[:, :], lambda k: xnT[par][:, k, b * P:(b + 1) * P],
                                       lambda k: wT[:, k, NQ:NQ + 2 * D])
                elif r == 4:
                    for k in range(KD):
                        last = pe.matmul(bank[:, 0:2 * P], wT[:, k, NG:NG + GH], xnT[par][:, k, :],
                                         start=(k == 0), stop=(k == KD - 1))
                elif r == 7:
                    for b in range(2):
                        last = token_major(pe, bank[:, b * D:(b + 1) * D], lambda k: xnT[par][:, k, b * P:(b + 1) * P],
                                           lambda k: wT[:, k, NV:NV + D])
                elif r == 3:
                    pe.wait_ge(hidden_spread, n + 1)
                    for b in range(2):
                        pe.matmul(bank[:, b * NH:(b + 1) * NH], hrep[:, b, :], wg2T[:, :], start=True, stop=True)
                    last = pe.matmul(bank[:, 2 * NH:3 * NH], ones_row[:, :], bg2[:, :], start=True, stop=True)
                else:
                    pe.wait_ge(scaled, n + 1)
                    for t in range(4):
                        last = pe.transpose(bank[:, t * P:(t + 1) * P], qk[:, 0 if r == 6 else 1, t * P:(t + 1) * P], ident[:, :])
                last.then_inc(ring.filled(r), 1)

            def scores(par, bank, b, g, fresh):
                return pe.matmul(bank[:, :], qT[par][:, b, g // 2, :],
                                 kM[par][:, b, g // 2, 4 * (g % 2):4 * (g % 2) + 4, :].rearrange("p a k -> p (a k)"),
                                 start=fresh, stop=True, skip_group_check=True)

            def head_values(par, b, h):
                return v[par][:, b, h % 2, 32 * (h // 2):32 * (h // 2) + 32]

            pe.wait_ge(loaded, 13 * 16)
            turner.on_pe(pe)
            turner.wait_all(pe)
            pe.matmul(ring.bank[1][:, 0:NH], ones_row[:, :], g_row[:, :], start=True, stop=True) \
                .then_inc(static_spread, 1)
            produce(0, 0, 0)
            pe.wait_ge(static_exp, 1)
            ring.wait_slot(pe, 0, 0)
            for r in (1, 2, 4, 3, 6, 5, 7):
                produce(0, r, 0)
            produce(1, 0, 1)
            ring.wait_slot(pe, 0, 5)
            pe.wait_ge(k_masked.sem, k_masked.at(0, KD))
            att.pe_first(pe, scores)
            ring.wait_slot(pe, 1, 0)
            produce(1, 1, 1)
            produce(1, 2, 1)
            for i, par in pairs_by_two(pe):
                def before(u):
                    if u == 1:
                        ring.wait_slot(pe, i, 7)
                    if u == 2:
                        pe.wait_ge(k_masked.sem, k_masked.at(i, 2 * KD))
                    if u == 6 and exists(i + 1):
                        ring.wait_slot(pe, i + 1, 6)
                        ring.wait_slot(pe, i + 1, 5)
                        pe.wait_ge(k_masked.sem, k_masked.at(i + 1, KD))

                def after(u):
                    if u == 6 and exists(i + 2):
                        ring.wait_slot(pe, i + 2, 0)
                    for r in AFTER.get(u, ()):
                        produce(i + ahead(r), r, (par + ahead(r)) % 2)

                att.on_pe(pe, i, par, scores, head_values, before, after)
                att.pe_project(pe, i, lambda b: [(attnT[:, b, k, :], wT[:, k, NO:NO + D]) for k in range(KD)])

        @block.scalar
        def _(act):
            def empty(n, r, par):
                if not exists(n):
                    return
                bank = ring.arrived(act, n, r)
                if r == 0:
                    last = act.copy(xnT[par][:, :, :].rearrange("p k t -> p (k t)"), bank[:, :])
                elif r == 4:
                    for b in range(2):
                        last = act.activation(gelu[:, b * P:(b + 1) * P], bank[:, b * P:(b + 1) * P], ACT.Gelu,
                                              bias=bg1[:, :], accum_out=hsum[:, b:b + 1])
                else:
                    act.wait_ge(k_masked.sem, k_masked.at(n, 0))
                    act.activation(qT[par][:, 0, :, :].rearrange("p k t -> p (k t)"), bank[:, 0:D], ACT.Copy,
                                   scale=1.0 / 4.0)
                    last = act.copy(kT[:, 0, :, :].rearrange("p k t -> p (k t)"), bank[:, D:2 * D])
                last.then_inc(ring.done(r), 1)
                if r == 4:
                    ring.wait_slot(act, n, 4)
                    for b in range(2):
                        last = act.activation(hrep[:, b, :], ones_sq[:, :], ACT.Copy, scale=hsum[:, b:b + 1])
                    last.then_inc(hidden_spread, 1)

            def exp_logits(n, par):
                ring.wait_slot(act, n, 3)
                act.activation(gate[par][:, :, :], gate[par][:, :, :], ACT.Exp, scale=-1.0).then_inc(logits_exp, 1)

            turner.on_act(act)
            act.wait_ge(static_spread, 1)
            act.activation(gate_static[:, :], ring.bank[1][:, 0:NH], ACT.Exp, scale=-1.0).then_inc(static_exp, 1)
            act.wait_ge(loaded, 13 * 16)
            act.wait_ge(ones_set, 1)
            for r in (0, 4):
                empty(0, r, 0)
            exp_logits(0, 0)
            empty(0, 6, 0)
            empty(1, 0, 1)
            att.act_first(act)
            for i, par in pairs_by_two(act):
                def before(u):
                    for r in AFTER.get(u - 1, ()):
                        if r in (0, 4, 6):
                            empty(i + ahead(r), r, (par + ahead(r)) % 2)
                    if u == 3 and exists(i + 1):
                        exp_logits(i + 1, 1 - par)

                att.on_act(act, i, before, lambda u: None)

        @block.vector
        def _(dve):
            def empty(n, r, par):
                if not exists(n):
                    return
                bank = ring.arrived(dve, n, r)
                if r in (1, 2):
                    last = dve.tensor_tensor(qk[:, r - 1, :], bank[:, :], bqk[:, :], ALU.add)
                elif r == 7:
                    last = values_by_parity(dve, v[par], bank, bv, HD)
                elif r == 3:
                    gate_links.begin(n)
                    gate_links.link(dve, dve.tensor_copy(gate_bias[:, :], bank[:, 2 * NH:3 * NH]))
                    last = dve.scalar_tensor_tensor(gate[par][:, :, :],
                                                    bank[:, 0:2 * NH].rearrange("p (b h) -> p b h", b=2), 1.0 / P,
                                                    gate_bias[:, :].unsqueeze(1).broadcast_to([P, 2, NH]),
                                                    ALU.mult, ALU.add)
                else:
                    dve.wait_ge(k_masked.sem, k_masked.at(n, 0))
                    dve.tensor_scalar(qT[par][:, 1, :, :].rearrange("p k t -> p (k t)"), bank[:, 0:D],
                                      1.0 / 4.0, None, ALU.mult)
                    last = dve.tensor_copy(kT[:, 1, :, :].rearrange("p k t -> p (k t)"), bank[:, D:2 * D])
                last.then_inc(ring.done(r), 1)

            def sum_squares(n):
                square_links.begin(n)
                ring.wait_slot(dve, n, 1)
                ring.wait_slot(dve, n, 2)
                square_links.link(dve, dve.tensor_tensor(sq[:, :, :], qk[:, :, :], qk[:, :, :], ALU.mult))
                square_links.link(dve, dve.tensor_reduce(ss[:, :], sq[:, :, :].rearrange("p b (h d) -> p (b h) d", d=HD),
                                                  AX.X, ALU.add))
                dve.tensor_scalar(ss[:, :], ss[:, :], NORM_EPS2, None, ALU.max).then_inc(squares_ready, 1)

            def scale_heads(n):
                dve.wait_ge(inverse_ready, n + 1)
                dve.tensor_tensor(qk[:, :, :].rearrange("p b (h d) -> p (b h) d", d=HD),
                                  qk[:, :, :].rearrange("p b (h d) -> p (b h) d", d=HD),
                                  inv[:, :].unsqueeze(2).broadcast_to([P, 4 * NH, HD]), ALU.mult).then_inc(scaled, 1)

            def finish_gate(n, par):
                dve.wait_ge(logits_exp, n + 1)
                logits = gate[par][:, :, :]
                gate_links.link(dve, dve.tensor_scalar(logits, logits, 1.0, None, ALU.add))
                gate_links.link(dve, dve.reciprocal(logits, logits))
                gate_links.link(dve, dve.tensor_tensor(logits, logits, gate_static[:, :].unsqueeze(1).broadcast_to([P, 2, NH]),
                                                  ALU.mult))
                gate_links.end()

            def gate_of(par, b, g):
                return gate[par][:, b, 4 * g:4 * g + 4]

            ln.statistics(dve, 0)
            ln.apply(dve, 0)
            ln.statistics(dve, 1)
            turner.on_dve(dve)
            dve.wait_ge(static_exp, 1)
            first_links.link(dve, dve.tensor_scalar(gate_static[:, :], gate_static[:, :], 1.0, None, ALU.add))
            first_links.link(dve, dve.reciprocal(gate_static[:, :], gate_static[:, :]))
            dve.wait_ge(loaded, 13 * 16)
            empty(0, 1, 0)
            empty(0, 2, 0)
            ln.apply(dve, 1)
            sum_squares(0)
            empty(0, 3, 0)
            finish_gate(0, 0)
            scale_heads(0)
            empty(0, 5, 0)
            dve.wait_ge(v_zeroed, 2)
            empty(0, 7, 0)
            att.dve_first(dve, gate_of)
            empty(1, 1, 1)
            empty(1, 2, 1)
            sum_squares(1)
            for i, par in pairs_by_two(dve):
                def before(u):
                    for r in AFTER.get(u - 1, ()):
                        if r not in (0, 4, 6):
                            empty(i + ahead(r), r, (par + ahead(r)) % 2)

                def after(u):
                    if u == 2:
                        ln.statistics(dve, i + 2)
                        if exists(i + 1):
                            scale_heads(i + 1)
                    if u == 3:
                        ln.apply(dve, i + 2)
                    if u == 4 and exists(i + 1):
                        finish_gate(i + 1, 1 - par)

                att.on_dve(dve, i, par, before, after, gate_of)
                before(UNITS)
                if exists(i + 2):
                    sum_squares(i + 2)
                att.dve_residual(dve, i, x)


def stage_aligned_attention(nc, x, ident, ctx_in, w_in, b_in):
    SLOTS = 4
    with ExitStack() as ctx:
        s = Scope(nc, ctx, "x1")
        w_nat = s.sb("w_nat", [P, 2, D])
        wT = s.sb("wT", [P, KD, D])
        bias = s.sb("bias", [P, KD])
        ctx_next = s.sb("ctx_next", [P, 2, D])
        ctx_all = s.sb("ctx_all", [P, NB, D])
        ctxT = s.sb("ctxT", [P, KD, 2 * P])
        xnT = s.sb("xnT", [P, KD, 2 * P])
        exT = s.sb("exT", [P, KD, 2 * P])
        eoT = s.sb("eoT", [P, KD, 2 * P])
        neg_max, row_sum, norm = (s.sb(n, [P, 2]) for n in ("neg_max", "row_sum", "norm"))
        prob = s.sb("prob", [P, 2, P])
        probT = s.sb("probT", [P, 2, P])
        ln = LayerNorm(s, x)
        ring = Ring(s, SLOTS)
        score_bank = s.ps("score", [P, 2 * P])
        turn_bank = s.ps("turn", [P, 2 * P])
        out_bank = s.ps("out", [P, 2 * D])
        turner = Turner(s, ring.bank, ident)
        turner.weight(w_nat, wT, 2)
        loaded = s.sem("loaded")
        ctx_loaded = s.sem("ctx_loaded")
        values_loaded = s.sem("values_loaded")
        scored = s.counting("scored", 1)
        max_ready = s.counting("max_ready", 1)
        exp_ready = s.counting("exp_ready", 1)
        turned = s.counting("turned", 1)
        probT_ready = s.counting("probT_ready", 1)
        weighted = s.counting("weighted", 1)
        added = s.counting("added", 1)
        links = Chain(s.sem("links"), 1)
        block = s.block()

        @block.sync
        def _(sp):
            ctx_pairs = ctx_in.rearrange("b t d -> t b d")
            sp.dma_start(w_nat[:, :, :], w_in.rearrange("(t p) n -> p t n", p=P)).then_inc(loaded, 16)
            sp.dma_start(ctx_next[:, :, :], ctx_pairs[:, 0:2, :]).then_inc(ctx_loaded, 16)
            sp.dma_start(bias[:, :], b_in.rearrange("(k p) -> p k", p=P),
                         allow_slow_non_contiguous=True).then_inc(loaded, 16)
            sp.dma_start(ctx_all[:, :, :], ctx_pairs).then_inc(values_loaded, 16)
            with sp.Fori(1, PAIRS) as n:
                ring.arrived(sp, n - 1, 1)
                sp.dma_start(ctx_next[:, :, :], ctx_pairs[:, bass.ds(2 * n, 2), :]).then_inc(ctx_loaded, 16)
            sp.wait_ge(ctx_loaded, 16 * PAIRS)

        @block.gpsimd
        def _(pool):
            ln.setup(pool)
            with pool.Fori(0, PAIRS) as n:
                ln.root(pool, n)

        @block.tensor
        def _(pe):
            def produce(n, r):
                if not exists(n):
                    return
                bank = ring.free(pe, n, r)
                if r == 0:
                    last = ln.transposed(pe, bank, ident, n)
                elif r == 1:
                    pe.wait_ge(ctx_loaded, 16 * n + 16)
                    for b in range(2):
                        for k in range(KD):
                            last = pe.transpose(bank[:, k * 2 * P + b * P:k * 2 * P + (b + 1) * P],
                                                ctx_next[:, b, k * P:(k + 1) * P], ident[:, :])
                else:
                    for m in range(KD):
                        for k in range(KD):
                            last = pe.matmul(bank[:, m * 256:(m + 1) * 256], wT[:, k, m * P:(m + 1) * P],
                                             (xnT if r == 2 else ctxT)[:, k, :], start=(k == 0), stop=(k == KD - 1))
                last.then_inc(ring.filled(r), 1)

            def project(n):
                if exists(n):
                    ring.wait_slot(pe, n, 0)
                    ring.wait_slot(pe, n, 1)
                produce(n, 2)
                produce(n, 3)

            def scores(n, first=False):
                if not exists(n):
                    return
                ring.wait_slot(pe, n, 2)
                ring.wait_slot(pe, n, 3)
                if not first:
                    pe.wait_ge(exp_ready.sem, exp_ready.at(n, 0))
                for b in range(2):
                    for k in range(KD):
                        last = pe.matmul(score_bank[:, b * P:(b + 1) * P], exT[:, k, b * P:(b + 1) * P],
                                         eoT[:, k, b * P:(b + 1) * P], start=(k == 0), stop=(k == KD - 1))
                last.then_inc(scored.sem, 1)

            pe.wait_ge(loaded, 32)
            turner.on_pe(pe)
            turner.wait_all(pe)
            produce(0, 0)
            produce(0, 1)
            project(0)
            produce(1, 0)
            produce(1, 1)
            scores(0, first=True)
            pe.wait_ge(values_loaded, 16)
            for i, _ in pairs_by_two(pe):
                project(i + 1)
                pe.wait_ge(exp_ready.sem, exp_ready.at(i, 1))
                pe.wait_ge(probT_ready.sem, probT_ready.at(i, 0))
                for b in range(2):
                    last = pe.transpose(turn_bank[:, b * P:(b + 1) * P], prob[:, b, :], ident[:, :])
                last.then_inc(turned.sem, 1)
                produce(i + 2, 0)
                produce(i + 2, 1)
                pe.wait_ge(probT_ready.sem, probT_ready.at(i, 1))
                pe.wait_ge(added.sem, added.at(i, 0))
                for b in range(2):
                    last = pe.matmul(out_bank[:, b * D:(b + 1) * D], probT[:, b, :],
                                     ctx_all[:, bass.ds(2 * i + b, 1), :].rearrange("p a d -> p (a d)"),
                                     start=True, stop=True)
                last.then_inc(weighted.sem, 1)
                scores(i + 1)

        @block.scalar
        def _(act):
            def empty(n, r):
                if not exists(n):
                    return
                bank = ring.arrived(act, n, r)
                if r == 0:
                    last = act.copy(xnT[:, :, :].rearrange("p k t -> p (k t)"), bank[:, :])
                else:
                    for m in range(KD):
                        last = act.activation(exT[:, m, :], bank[:, m * 256:(m + 1) * 256], ACT.Identity,
                                              bias=bias[:, m:m + 1])
                last.then_inc(ring.done(r), 1)

            turner.on_act(act)
            act.wait_ge(loaded, 32)
            for n, r in ((0, 0), (0, 2), (1, 0)):
                empty(n, r)
            for i, _ in pairs_by_two(act):
                act.wait_ge(max_ready.sem, max_ready.at(i, 1))
                act.wait_ge(turned.sem, turned.at(i, 0))
                for b in range(2):
                    last = act.activation(prob[:, b, :], score_bank[:, b * P:(b + 1) * P], ACT.Exp,
                                          bias=neg_max[:, b:b + 1], accum_out=row_sum[:, b:b + 1])
                last.then_inc(exp_ready.sem, 1)
                empty(i + 1, 2)
                act.wait_ge(turned.sem, turned.at(i, 1))
                act.wait_ge(weighted.sem, weighted.at(i, 0))
                act.copy(probT[:, :, :].rearrange("p b t -> p (b t)"), turn_bank[:, :]).then_inc(probT_ready.sem, 1)
                empty(i + 2, 0)

        @block.vector
        def _(dve):
            def empty(n, r):
                if not exists(n):
                    return
                bank = ring.arrived(dve, n, r)
                if r == 1:
                    last = dve.tensor_copy(ctxT[:, :, :].rearrange("p k t -> p (k t)"), bank[:, :])
                else:
                    for m in range(KD):
                        last = dve.tensor_scalar(eoT[:, m, :], bank[:, m * 256:(m + 1) * 256],
                                                 bias[:, m:m + 1], None, ALU.add)
                last.then_inc(ring.done(r), 1)

            ln.statistics(dve, 0)
            ln.apply(dve, 0)
            ln.statistics(dve, 1)
            turner.on_dve(dve)
            dve.wait_ge(loaded, 32)
            empty(0, 1)
            ln.apply(dve, 1)
            empty(0, 3)
            empty(1, 1)
            ln.statistics(dve, 2)
            for i, _ in pairs_by_two(dve):
                links.begin(i)
                dve.wait_ge(scored.sem, scored.at(i, 1))
                dve.tensor_reduce(neg_max[:, :], score_bank[:, :].rearrange("p (b k) -> p b k", b=2),
                                  AX.X, ALU.max, negate=True).then_inc(max_ready.sem, 1)
                ln.apply(dve, i + 2)
                empty(i + 1, 3)
                dve.wait_ge(exp_ready.sem, exp_ready.at(i, 1))
                links.link(dve, dve.reciprocal(norm[:, :], row_sum[:, :]))
                empty(i + 2, 1)
                dve.wait_ge(weighted.sem, weighted.at(i, 1))
                for b in range(2):
                    xb = x[:, bass.ds(2 * i + b, 1), :].rearrange("p a d -> p (a d)")
                    last = dve.scalar_tensor_tensor(xb, out_bank[:, b * D:(b + 1) * D], norm[:, b:b + 1], xb,
                                                    ALU.mult, ALU.add)
                last.then_inc(added.sem, 1)
                ln.statistics(dve, i + 3)


def stage_product_keys(nc, x, ident, gamma, beta, w_q, keys, key_in, key_out):
    H, NK, TOP = 8, 64, 8
    KW = P
    R = NK // 2
    SPLIT = 24
    PICKS = H * TOP
    TOKENS = NB * P
    HALF = P // 2
    W_SCALE = 4096.0
    GT = 16
    GU = HALF // GT
    with ExitStack() as ctx:
        s = Scope(nc, ctx, "f")
        hT = s.sb("hT", [P, KD, TOKENS])
        kiT = [s.sb(f"kiT_{part}", [P, KD, SPLIT, P], F32R) for part in ("high", "low")]
        kiT_rest = s.sb("kiT_rest", [P, KD, R - SPLIT, P])
        ko = s.sb("ko", [P, R, D])
        gel = s.sb("gel", [P, R, 2 * P])
        fused = s.sb("fused", [P, KD, 2 * H * NK])
        bn_scale, bn_shift = s.sb("bn_scale", [P, KD]), s.sb("bn_shift", [P, KD])
        kept = s.sem("kept")
        with ExitStack() as prep_ctx:
            p = Scope(nc, prep_ctx, "fp")
            wq_nat = p.sb("wq_nat", [P, 2 * H, D])
            keys_nat = p.sb("keys_nat", [NK, H, 2, KW])
            keysT = p.sb("keysT", [P, H, 2, NK])
            gamma_col, beta_col = p.sb("gamma_col", [P, KD]), p.sb("beta_col", [P, KD])
            stats, mv = p.sb("stats", [P, KD, 4, 6]), p.sb("mv", [P, KD, 2])
            bn_scale_power = p.sb("bn_power", [P, KD])
            var_eps, rstd = p.sb("var_eps", [P, KD]), p.sb("rstd", [P, KD])
            ln = LayerNorm(p, x)
            banks = [p.ps(f"bank{n}", [P, 512]) for n in range(2)]
            pair_bank = p.ps("pair", [P, 512])
            key_turner, rest_turner = Turner(p, banks, ident, "k"), Turner(p, banks, ident, "r")
            turner = Turner(p, banks, ident)
            for k in range(KD):
                for r in range(0, R, 4):
                    blocks = [gel[:, r + j, k * P:(k + 1) * P] for j in range(4)]
                    if r < SPLIT:
                        turner.jobs.append((blocks, [part[:, k, r:r + 4, :].rearrange("p r c -> p (r c)") for part in kiT]))
                    else:
                        rest_turner.jobs.append((blocks, kiT_rest[:, k, r - SPLIT:r - SPLIT + 4, :]
                                                 .rearrange("p r c -> p (r c)")))
            for h in range(0, H, 4):
                key_turner.jobs.append(([keys_nat[:, h + j, ax, :] for j in range(4) for ax in range(2)],
                                        keysT[:, h:h + 4, :, :].rearrange("p h a n -> p (h a n)")))
            loaded = p.sem("loaded")
            in_loaded = p.sem("in_loaded")
            fused_ready = [p.sem(f"fused_ready{n}") for n in range(2)]
            fused_copied = [p.sem(f"fused_copied{n}") for n in range(2)]
            pair_turned = p.sem("pair_turned")
            pair_copied = p.sem("pair_copied")
            power_set = p.sem("power_set")
            bn_var_ready = p.sem("bn_var_ready")
            bn_rstd_ready = p.sem("bn_rstd_ready")
            bn_links = Chain(p.sem("bn_links"))
            block = p.block()

            @block.sync
            def _(sp):
                sp.dma_start(keys_nat[:, :, :, :], keys.rearrange("h n a w -> n h a w")).then_inc(loaded, 16)
                sp.dma_start(wq_nat[:, :, :], w_q.rearrange("(j p) d -> p j d", p=P)).then_inc(loaded, 16)
                for dst, src in ((gamma_col, gamma), (beta_col, beta)):
                    sp.dma_start(dst[:, :], src.rearrange("(k p) -> p k", p=P),
                                 allow_slow_non_contiguous=True).then_inc(loaded, 16)
                for b in range(2):
                    sp.dma_start(gel[b * NK:(b + 1) * NK, :, :],
                                 key_in.rearrange("(i r b) d -> b i r d", r=R, b=2)[b]).then_inc(in_loaded, 16)
                for b in range(2):
                    sp.dma_start(ko[b * NK:(b + 1) * NK, :, :],
                                 key_out.rearrange("(i r b) d -> b i r d", r=R, b=2)[b]).then_inc(kept, 16)

            @block.gpsimd
            def _(pool):
                ln.setup(pool)
                pool.memset(bn_scale_power[:, :], -0.5).then_inc(power_set, 1)
                ln.root(pool, 0)
                with pool.Fori(0, PAIRS) as i:
                    ln.root(pool, i + 1)
                pool.wait_ge(power_set, 1)
                pool.wait_ge(bn_var_ready, 1)
                pool.tensor_tensor(rstd[:, :], var_eps[:, :], bn_scale_power[:, :], ALU.pow).then_inc(bn_rstd_ready, 1)

            @block.tensor
            def _(pe):
                with pe.Fori(0, PAIRS) as i:
                    pe.wait_ge(pair_copied, i)
                    ln.transposed(pe, pair_bank, ident, i).then_inc(pair_turned, 1)
                pe.wait_ge(loaded, 64)
                key_turner.on_pe(pe)
                key_turner.wait_all(pe)
                for n in range(4):
                    k, ax = n // 2, n % 2
                    pe.wait_ge(fused_copied[n % 2], n // 2)
                    for h in range(H):
                        last = pe.matmul(banks[n % 2][:, h * NK:(h + 1) * NK],
                                         wq_nat[:, ax * H + h, k * P:(k + 1) * P], keysT[:, h, ax, :],
                                         start=True, stop=True)
                    last.then_inc(fused_ready[n % 2], 1)
                for n in range(2):
                    pe.wait_ge(fused_copied[n], 2)
                pe.wait_ge(in_loaded, 32)
                rest_turner.on_pe(pe)
                rest_turner.wait_all(pe)
                turner.on_pe(pe)
                turner.wait_all(pe)

            def copy_fused(eng, copy, par):
                for n in range(par, 4, 2):
                    eng.wait_ge(fused_ready[par], n // 2 + 1)
                    copy(fused[:, n // 2, par * H * NK:(par + 1) * H * NK], banks[par][:, :]) \
                        .then_inc(fused_copied[par], 1)

            @block.scalar
            def _(act):
                with act.Fori(0, PAIRS) as i:
                    act.wait_ge(pair_turned, i + 1)
                    act.copy(hT[:, :, bass.ds(i * 2 * P, 2 * P)],
                             pair_bank[:, :].rearrange("p (k t) -> p k t", k=KD)).then_inc(pair_copied, 1)
                key_turner.on_act(act)
                copy_fused(act, act.copy, 0)
                rest_turner.on_act(act)
                turner.split_on_act(act)

            @block.vector
            def _(dve):
                ln.statistics(dve, 0)
                ln.apply(dve, 0)
                with dve.Fori(0, PAIRS) as i:
                    ln.statistics(dve, i + 1)
                    dve.wait_ge(pair_turned, i + 1)
                    ln.apply(dve, i + 1)
                dve.wait_ge(pair_copied, PAIRS)
                for k in range(KD):
                    for c in range(4):
                        last = dve.bn_stats(stats[:, k, c, :], hT[:, k, c * 512:(c + 1) * 512])
                bn_links.link(dve, last)
                for k in range(KD):
                    last = dve.bn_aggr(mv[:, k, :], stats[:, k, :, :].rearrange("p c s -> p (c s)"))
                bn_links.link(dve, last)
                dve.tensor_scalar(var_eps[:, :], mv[:, :, 1], LN_EPS, None, ALU.add).then_inc(bn_var_ready, 1)
                key_turner.on_dve(dve)
                copy_fused(dve, dve.tensor_copy, 1)
                dve.wait_ge(loaded, 64)
                dve.wait_ge(bn_rstd_ready, 1)
                bn_links.link(dve, dve.tensor_tensor(bn_scale[:, :], gamma_col[:, :], rstd[:, :], ALU.mult))
                bn_links.link(dve, dve.tensor_tensor(bn_shift[:, :], mv[:, :, 0], bn_scale[:, :], ALU.mult))
                dve.tensor_tensor(bn_shift[:, :], beta_col[:, :], bn_shift[:, :], ALU.subtract)
                rest_turner.on_dve(dve)
                turner.split_on_dve(dve)

        xbT = s.sb("xbT", [P, KD, 2 * P])
        hT_pair = [s.sb(f"hT_pair_{part}", [P, KD, 2 * P], F32R) for part in ("high", "low")]
        spare = s.sb("spare", [1, 1])
        ints = s.sb("ints", [P, P], mybir.dt.int32)
        iota = s.sb("iota", [P, P])
        best = s.sb("best", [P, 2, H, TOP])
        best_key = s.sb("best_key", [P, 2, H, TOP], U32)
        sums = s.sb("sums", [P, H, TOP, TOP])
        pick = s.sb("pick", [P, H, TOP])
        pick_at = s.sb("pick_at", [P, H, TOP], U32)
        rank = s.sb("rank", [P, 2, PICKS], U32)
        match = s.sb("match", [P, 2, PICKS, TOP])
        index = s.sb("index", [P, 2, PICKS], U32)
        high = s.sb("high", [P, 2, PICKS], U32)
        weight = s.sb("weight", [P, H, TOP])
        weight_sum = s.sb("weight_sum", [P, H])
        codes = s.sb("codes", [P, 3, 2, PICKS])
        codesT = s.sb("codesT", [P, 3, HALF])
        w_split = s.sb("w_split", [P, 2, HALF], F16)
        row_hot = s.sb("row_hot", [P, HALF, P], F16)
        col_hot = s.sb("col_hot", [P, 2, HALF, R], F16)
        sim_bank = [s.ps(f"sim{n}", [P, 512]) for n in range(2)]
        act_bank = [s.ps(f"act{n}", [P, 512]) for n in range(2)]
        g_bank = [s.ps(f"g{n}", [P, 512]) for n in range(2)]
        out_bank = s.ps("out", [P, 2, D])
        turn_bank = s.ps("turn", [P, 512])
        iota_made = s.sem("iota_made")
        iota_ready = s.sem("iota_ready")
        xb_ready = s.sem("xb_ready")
        sims_ready = s.sem("sims_ready")
        sims_used = s.counting("sims_used", 1)
        weight_in = s.sem("weight_in")
        weight_exp = s.sem("weight_exp")
        codes_ready = s.sem("codes_ready")
        codes_turned = s.counting("codes_turned", 1)
        codes_copied = s.counting("codes_copied", 1)
        hot_ready = s.sem("hot_ready")
        match_ready = s.counting("match_ready", 1)
        low_ready = s.counting("low_ready", 1)
        col_ready = s.counting("col_ready", 1)
        g_ready = [s.counting(f"g_ready{q}", GU) for q in range(2)]
        h_high = s.sem("h_high")
        h_low = s.sem("h_low")
        g_used = [s.counting(f"g_used{q}", GU) for q in range(2)]
        act_ready = [s.sem(f"act_ready{q}") for q in range(2)]
        act_used = [s.counting(f"act_used{q}", R // 4) for q in range(2)]
        out_ready = s.counting("out_ready", 2)
        out_used = [s.counting(f"out_used{t}", 1) for t in range(2)]
        PICK_LINKS, HOT_LINKS = 11, 1
        first_links = Chain(s.sem("first_links"))
        links = Chain(s.sem("links"), 2 * (PICK_LINKS + HOT_LINKS))
        block = s.block()

        @block.gpsimd
        def _(pool):
            pool.iota(ints[:, :], pattern=[[1, P]], base=0, channel_multiplier=0).then_inc(iota_made, 1)

            def weigh(n):
                match_r, w_low = col_hot[:, 0, :, :], col_hot[:, 1, :, :]
                pool.wait_ge(match_ready.sem, match_ready.at(n, 1))
                pool.tensor_tensor(w_low, match_r, w_split[:, 1, :].unsqueeze(2).broadcast_to([P, HALF, R]), ALU.mult) \
                    .then_inc(low_ready.sem, 1)
                pool.wait_ge(low_ready.sem, low_ready.at(n, 1))
                pool.tensor_tensor(match_r, match_r, w_split[:, 0, :].unsqueeze(2).broadcast_to([P, HALF, R]), ALU.mult) \
                    .then_inc(col_ready.sem, 1)

            with pool.Fori(0, NB) as n:
                weigh(n)

        def batch_norm(act, n):
            if not exists(n):
                return
            for k in range(KD):
                last = act.activation(xbT[:, k, :], hT[:, k, bass.ds(n * 2 * P, 2 * P)], ACT.Identity,
                                      bias=bn_shift[:, k:k + 1], scale=bn_scale[:, k:k + 1])
            last.then_inc(xb_ready, 1)
            act.copy(hT_pair[0][:, :, :], hT[:, :, bass.ds(n * 2 * P, 2 * P)]).then_inc(h_high, 1)

        @block.tensor
        def _(pe):
            def similarities(i, t, step):
                if not exists(i):
                    return
                n = 2 * i + t
                ax, k = step // 2, step % 2
                if step == 0:
                    pe.wait_ge(xb_ready, i + 1)
                    pe.wait_ge(sims_used.sem, sims_used.at(n, 0))
                last = pe.matmul(sim_bank[ax][:, :], xbT[:, k, t * P:(t + 1) * P],
                                 fused[:, k, ax * 512:(ax + 1) * 512], start=(k == 0), stop=(k == KD - 1))
                if step == 3:
                    last.then_inc(sims_ready, 1)

            def turn_codes(i, t):
                if not exists(i):
                    return
                n = 2 * i + t
                pe.wait_ge(codes_ready, n + 1)
                pe.wait_ge(codes_copied.sem, codes_copied.at(n, 0))
                for m in range(3):
                    last = pe.transpose(turn_bank[:, m * P:(m + 1) * P],
                                        codes[:, m, :, :].rearrange("p a n -> p (a n)"), ident[:, :])
                last.then_inc(codes_turned.sem, 1)

            for step in range(4):
                similarities(0, 0, step)
            pe.wait_ge(kept, 32)
            for i in pairs_but_last(pe):
                def activations(u):
                    q = u % 2
                    pe.wait_ge(act_used[q].sem, act_used[q].at(i, u // 2))
                    for j in range(2):
                        for k in range(KD):
                            dst, r = act_bank[q][:, j * 2 * P:(j + 1) * 2 * P], 2 * u + j
                            if r < SPLIT:
                                last = split_product(pe, dst, [part[:, k, r, :] for part in kiT],
                                                     [part[:, k, :] for part in hT_pair], k == 0, k == KD - 1)
                            else:
                                last = pe.matmul(dst, kiT_rest[:, k, r - SPLIT, :], hT[:, k, bass.ds(i * 2 * P, 2 * P)],
                                                 start=(k == 0), stop=(k == KD - 1))
                    last.then_inc(act_ready[q], 1)

                def weights(t):
                    n = 2 * i + t
                    pe.wait_ge(hot_ready, n + 1)
                    pe.wait_ge(col_ready.sem, col_ready.at(n, 1))
                    for m in range(GU):
                        for q in range(2):
                            rows = slice(q * HALF, (q + 1) * HALF)
                            pe.wait_ge(g_used[q].sem, g_used[q].at(n, m))
                            for j in range(GT):
                                for part in range(2):
                                    last = pe.matmul(g_bank[q][:, j * R:(j + 1) * R], row_hot[rows, GT * m + j, :],
                                                     col_hot[rows, part, GT * m + j, :],
                                                     start=(part == 0), stop=(part == 1))
                            last.then_inc(g_ready[q].sem, 1)
                        if t == 0:
                            similarities(i + 1, 0, m)

                def outputs(t):
                    n = 2 * i + t
                    for q in range(2):
                        pe.wait_ge(g_used[q].sem, g_used[q].at(n, GU))
                    pe.wait_ge(out_used[t].sem, out_used[t].at(i, 0))
                    for r in range(R):
                        last = pe.matmul(out_bank[:, t, :], gel[:, r, t * P:(t + 1) * P], ko[:, r, :],
                                         start=(r == 0), stop=(r == R - 1))
                    last.then_inc(out_ready.sem, 1)

                pe.wait_ge(h_low, i + 1)
                for u in range(16):
                    activations(u)
                    if u == 1:
                        turn_codes(i, 0)
                    if 4 <= u < 8:
                        similarities(i, 1, u - 4)
                weights(0)
                turn_codes(i, 1)
                outputs(0)
                weights(1)
                outputs(1)

        @block.scalar
        def _(act):
            def exponentials(i, t):
                if not exists(i):
                    return
                n = 2 * i + t
                act.wait_ge(weight_in, n + 1)
                act.activation(weight[:, :, :], weight[:, :, :], ACT.Exp).then_inc(weight_exp, 1)

            batch_norm(act, 0)
            exponentials(0, 0)
            for i in pairs_but_last(act):
                act.wait_ge(out_ready.sem, out_ready.at(i, 0))
                for u in range(16):
                    q = u % 2
                    act.wait_ge(act_ready[q], 8 * i + u // 2 + 1)
                    act.activation(gel[:, 2 * u:2 * u + 2, :].rearrange("p r t -> p (r t)"), act_bank[q][:, :],
                                   ACT.Gelu).then_inc(act_used[q].sem, 1)
                    if u == 13:
                        exponentials(i, 1)
                act.wait_ge(sims_ready, 2 * i + 2)
                batch_norm(act, i + 1)
                exponentials(i + 1, 0)

        @block.vector
        def _(dve):
            def choose(chain, i, t):
                if not exists(i):
                    return
                n = 2 * i + t
                dve.wait_ge(sims_ready, n + 1)
                dve.memset(spare[:, :], 0.0)
                for ax in range(2):
                    for h in range(H):
                        last = dve.max(best[:, ax, h, :], sim_bank[ax][:, h * NK:(h + 1) * NK])
                chain.link(dve, last)
                dve.memset(spare[:, :], 0.0)
                for ax in range(2):
                    for h in range(H):
                        last = dve.max_index(best_key[:, ax, h, :], best[:, ax, h, :],
                                             sim_bank[ax][:, h * NK:(h + 1) * NK])
                last.then_inc(sims_used.sem, 1)
                chain.link(dve, dve.tensor_tensor(
                    sums[:, :, :, :], best[:, 0, :, :].unsqueeze(3).broadcast_to([P, H, TOP, TOP]),
                    best[:, 1, :, :].unsqueeze(2).broadcast_to([P, H, TOP, TOP]), ALU.add))
                dve.memset(spare[:, :], 0.0)
                for h in range(H):
                    last = dve.max(pick[:, h, :], sums[:, h, :, :].rearrange("p a b -> p (a b)"))
                chain.link(dve, last)
                dve.tensor_tensor(weight[:, :, :], pick[:, :, :], pick[:, :, 0:1].broadcast_to([P, H, TOP]),
                                  ALU.subtract).then_inc(weight_in, 1)
                for h in range(H):
                    last = dve.max_index(pick_at[:, h, :], pick[:, h, :], sums[:, h, :, :].rearrange("p a b -> p (a b)"))
                chain.link(dve, last)
                dve.tensor_single_scalar(rank[:, 0, :], pick_at[:, :, :].rearrange("p h k -> p (h k)"), 3,
                                         ALU.logical_shift_right)
                chain.link(dve, dve.tensor_single_scalar(rank[:, 1, :], pick_at[:, :, :].rearrange("p h k -> p (h k)"), 7,
                                                         ALU.bitwise_and))
                chain.link(dve, dve.tensor_tensor(
                    match[:, :, :, :].rearrange("p a n k -> p (a n) k"),
                    rank[:, :, :].rearrange("p a n -> p (a n)").unsqueeze(2).broadcast_to([P, 2 * PICKS, TOP]),
                    iota[:, 0:TOP].unsqueeze(1).broadcast_to([P, 2 * PICKS, TOP]), ALU.is_equal))
                mv4 = match[:, :, :, :].rearrange("p a (h n) k -> p (a h) n k", h=H)
                chain.link(dve, dve.tensor_tensor(
                    mv4, mv4, best_key[:, :, :, :].rearrange("p a h k -> p (a h) k").unsqueeze(2)
                    .broadcast_to([P, 2 * H, TOP, TOP]), ALU.mult))
                with nc.allow_low_precision(reason="one key below 64 and seven zeros: exact"):
                    chain.link(dve, dve.tensor_reduce(index[:, :, :].rearrange("p a n -> p (a n)"),
                                                      match[:, :, :, :].rearrange("p a n k -> p (a n) k"), AX.X, ALU.add))
                dve.tensor_scalar(high[:, 0, :], index[:, 1, :], 1, 6, ALU.bitwise_and, ALU.logical_shift_left)
                chain.link(dve, dve.tensor_single_scalar(high[:, 1, :], index[:, 1, :], 1, ALU.logical_shift_right))
                dve.wait_ge(codes_turned.sem, codes_turned.at(n, 0))
                for d in range(2):
                    dve.tensor_tensor(codes[:, 0, d, :], high[:, 0, :], index[:, 0, :], ALU.add)
                    dve.tensor_copy(codes[:, 1, d, :], high[:, 1, :])
                dve.wait_ge(weight_exp, n + 1)
                chain.link(dve, dve.tensor_reduce(weight_sum[:, :], weight[:, :, :], AX.X, ALU.add))
                chain.link(dve, dve.reciprocal(weight_sum[:, :], weight_sum[:, :]))
                for d in range(2):
                    last = dve.scalar_tensor_tensor(
                        codes[:, 2, d, :].rearrange("p (h k) -> p h k", h=H), weight[:, :, :], W_SCALE,
                        weight_sum[:, :].unsqueeze(2).broadcast_to([P, H, TOP]), ALU.mult, ALU.mult)
                last.then_inc(codes_ready, 1)

            def one_hot(chain, i, t):
                if not exists(i):
                    return
                n = 2 * i + t
                dve.wait_ge(codes_turned.sem, codes_turned.at(n, 1))
                dve.wait_ge(col_ready.sem, col_ready.at(n, 0))
                turned = turn_bank[:, 0:3 * P].rearrange("p (m a t) -> p m a t", m=3, a=2)
                for q in range(2):
                    rows = slice(q * HALF, (q + 1) * HALF)
                    last = dve.tensor_copy(codesT[rows, :, :], turned[rows, :, q, :])
                last.then_inc(codes_copied.sem, 1)
                dve.wait_ge(codes_copied.sem, codes_copied.at(n, 1))
                dve.wait_ge(g_ready[1].sem, g_ready[1].at(n, 0))
                chain.link(dve, dve.tensor_copy(w_split[:, 0, :], codesT[:, 2, :]))
                dve.tensor_tensor(w_split[:, 1, :], codesT[:, 2, :], w_split[:, 0, :], ALU.subtract)
                dve.tensor_tensor(col_hot[:, 0, :, :], codesT[:, 1, :].unsqueeze(2).broadcast_to([P, HALF, R]),
                                  iota[:, 0:R].unsqueeze(1).broadcast_to([P, HALF, R]), ALU.is_equal) \
                    .then_inc(match_ready.sem, 1)
                dve.tensor_tensor(row_hot[:, :, :], codesT[:, 0, :].unsqueeze(2).broadcast_to([P, HALF, P]),
                                  iota[:, :].unsqueeze(1).broadcast_to([P, HALF, P]), ALU.is_equal).then_inc(hot_ready, 1)

            def apply_weights(i, t):
                n = 2 * i + t
                for q in range(2):
                    dve.wait_ge(act_used[q].sem, act_used[q].at(i, R // 4))
                for m in range(GU):
                    for q in range(2):
                        t0 = t * P + q * HALF + GT * m
                        g = gel[:, :, t0:t0 + GT].rearrange("p r t -> p t r")
                        dve.wait_ge(g_ready[q].sem, g_ready[q].at(n, m + 1))
                        dve.scalar_tensor_tensor(g, g_bank[q][:, :].rearrange("p (t r) -> p t r", r=R), 1.0 / W_SCALE, g,
                                                 ALU.mult, ALU.mult).then_inc(g_used[q].sem, 1)

            def residual(i, t):
                dve.wait_ge(out_ready.sem, out_ready.at(i, t + 1))
                xb = x[:, bass.ds(2 * i + t, 1), :].rearrange("p a d -> p (a d)")
                dve.tensor_tensor(xb, out_bank[:, t, :], xb, ALU.add).then_inc(out_used[t].sem, 1)

            dve.wait_ge(iota_made, 1)
            dve.tensor_copy(iota[:, :], ints[:, :]).then_inc(iota_ready, 1)
            dve.wait_ge(iota_ready, 1)

            def split_pair(i):
                if exists(i):
                    dve.wait_ge(h_high, i + 1)
                    dve.tensor_tensor(hT_pair[1][:, :, :], hT[:, :, bass.ds(i * 2 * P, 2 * P)], hT_pair[0][:, :, :],
                                      ALU.subtract).then_inc(h_low, 1)

            split_pair(0)
            choose(first_links, 0, 0)
            for i in pairs_but_last(dve):
                links.begin(i)
                one_hot(links, i, 0)
                choose(links, i, 1)
                apply_weights(i, 0)
                one_hot(links, i, 1)
                split_pair(i + 1)
                residual(i, 0)
                apply_weights(i, 1)
                choose(links, i + 1, 0)
                residual(i, 1)
                if exists(i + 1):
                    links.end()


def stage_experts(nc, x, ident, ones_row, gate_w, gate_b, w_gate, w_up, w_down, s_gate, s_up, s_down):
    NE = 16
    TOP = 8
    ROUTE_SCALE = 2.826
    HID = 256
    TOKENS = NB * P
    GROUP = 512
    GROUPS = TOKENS // GROUP
    TAKEN = -3.0e38
    with ExitStack() as ctx:
        s = Scope(nc, ctx, "m")
        gw = s.sb("gw", [NE, D])
        gwT = s.sb("gwT", [P, KD, NE])
        gb_row = s.sb("gb_row", [1, NE])
        gate_bias = s.sb("gate_bias", [P, NE])
        xnT_pair = [s.sb(f"xnT_pair{n}", [P, KD, 2 * P]) for n in range(2)]
        xnT = [s.sb(f"xnT_{part}", [P, KD, TOKENS], F32R) for part in ("high", "low")]
        score = s.sb("score", [P, NB, NE])
        chosen_by = s.sb("chosen_by", [P, NB, NE])
        top = s.sb("top", [P, NB, TOP])
        left = s.sb("left", [P, NB, NE])
        total = s.sb("total", [P, NB])
        combine = s.sb("combine", [P, NB, NE + 1])
        w_nat = s.sb("w_nat", [P, 6, D])
        wT = [[s.sb(f"wT{n}_{part}", [P, 3, KD, HID], F32R) for part in ("high", "low")] for n in range(2)]
        silu = s.sb("silu", [P, 2, GROUP])
        act_up = s.sb("act_up", [P, 2, GROUP])
        hidden = [s.sb(f"hidden_{part}", [P, 2, 2, GROUP], F32R) for part in ("high", "low")]
        ln = LayerNorm(s, x)
        gate_bank = [s.ps(f"gate{n}", [P, GROUP]) for n in range(2)]
        up_bank = [s.ps(f"up{n}", [P, GROUP]) for n in range(2)]
        y_bank = [s.ps(f"y{n}", [P, 2 * D]) for n in range(2)]
        turn_bank = s.ps("turn", [P, 512])
        first_turn_banks = (turn_bank, *y_bank)
        route_bank = s.ps("route", [P, 512])
        loaded = s.sem("loaded")
        gate_T = s.sem("gate_T")
        gate_T_copied = s.sem("gate_T_copied")
        ones_set = s.sem("ones_set")
        pair_turned = s.counting("pair_turned", 1)
        pair_copied = s.counting("pair_copied", 1)
        pair_high = s.counting("pair_high", 1)
        pair_low = s.counting("pair_low", 1)
        logits_ready = s.counting("logits_ready", 1)
        logits_exp = s.sem("logits_exp")
        w_loaded = s.sem("w_loaded")
        w_turned = s.counting("w_turned", 3)
        w_high = s.counting("w_high", 3)
        w_low = s.counting("w_low", 3)
        gate_ready = [s.counting(f"gate_ready{n}", GROUPS) for n in range(2)]
        up_ready = [s.counting(f"up_ready{n}", GROUPS) for n in range(2)]
        silu_ready = [s.counting(f"silu_ready{n}", GROUPS) for n in range(2)]
        product_ready = [s.counting(f"product_ready{n}", GROUPS) for n in range(2)]
        high_ready = [s.counting(f"high_ready{n}", GROUPS) for n in range(2)]
        low_ready = [s.counting(f"low_ready{n}", GROUPS) for n in range(2)]
        y_ready = [s.counting(f"y_ready{n}", GROUPS) for n in range(2)]
        y_added = [s.counting(f"y_added{n}", GROUPS) for n in range(2)]
        route_links = Chain(s.sem("route_links"))
        block = s.block()

        def wait(eng, signal, i, k):
            eng.wait_ge(signal.sem, signal.at(i, k))

        @block.sync
        def _(sp):
            sp.dma_start(gw[:, :], gate_w).then_inc(loaded, 16)
            sp.dma_start(gb_row[:, :], gate_b.rearrange("(a d) -> a d", a=1)).then_inc(loaded, 16)

            def load(parts):
                for m, w in enumerate(parts):
                    sp.dma_start(w_nat[:, 2 * m:2 * m + 2, :], w.rearrange("(t p) n -> p t n", p=P)).then_inc(w_loaded, 16)

            load((s_gate, s_up, s_down))
            with sp.Fori(1, NE + 1) as e:
                wait(sp, w_turned, e, 0)
                load([w[bass.ds(e - 1, 1), :, :].rearrange("a o n -> (a o) n") for w in (w_gate, w_up, w_down)])
            sp.wait_ge(w_loaded, 48 * (NE + 1))

        @block.gpsimd
        def _(pool):
            ln.setup(pool)
            pool.memset(combine[:, :, 0:1], 1.0).then_inc(ones_set, 1)
            with pool.Fori(0, PAIRS) as n:
                ln.root(pool, n)

        def all_experts(eng, on_engine):
            on_engine(0, 0)
            with eng.Fori(0, NE // 2 - 1) as h:
                on_engine(2 * h + 1, 1)
                on_engine(2 * h + 2, 0)
            on_engine(NE - 1, 1)
            on_engine(NE, 0, last_one=True)

        def turn_weights(pe, e, m, bank=turn_bank):
            pe.wait_ge(w_loaded, 48 * e + 16 * 3)
            if bank is turn_bank:
                wait(pe, w_low, e, m)
            for k in range(KD):
                for t in range(2):
                    last = pe.transpose(bank[:, k * HID + t * P:k * HID + (t + 1) * P],
                                        w_nat[:, 2 * m + t, k * P:(k + 1) * P], ident[:, :])
            last.then_inc(w_turned.sem, 1)

        def expert_on_pe(pe, e, par, last_one=False):
            wait(pe, w_low, e, 3)

            def projection(bank, which, g, m):
                for k in range(KD):
                    last = split_product(pe, bank[:, :], [w[:, which, k, m * P:(m + 1) * P] for w in wT[par]],
                                         [part[:, k, g * GROUP:(g + 1) * GROUP] for part in xnT], k == 0, k == KD - 1)
                return last

            def hidden_unit(g, m):
                wait(pe, silu_ready[m], e, g)
                projection(gate_bank[m], 0, g, m).then_inc(gate_ready[m].sem, 1)
                wait(pe, product_ready[m], e, g)
                projection(up_bank[m], 1, g, m).then_inc(up_ready[m].sem, 1)

            def down(g):
                for m in range(2):
                    wait(pe, low_ready[m], e, g + 1)
                for n in range(2):
                    wait(pe, y_added[n], e, g)
                    for t in range(2):
                        for k in range(2):
                            at = (2 * n + t) * P
                            last = split_product(pe, y_bank[n][:, t * D:(t + 1) * D],
                                                 [part[:, g % 2, k, at:at + P] for part in hidden],
                                                 [w[:, 2, k, :] for w in wT[par]], k == 0, k == 1)
                    last.then_inc(y_ready[n].sem, 1)

            for g in range(GROUPS):
                hidden_unit(g, 0)
                hidden_unit(g, 1)
                if g >= 1:
                    down(g - 1)
                if g < 3 and not last_one:
                    turn_weights(pe, e + 1, g)
            down(GROUPS - 1)

        @block.tensor
        def _(pe):
            pe.wait_ge(loaded, 32)
            for k in range(KD):
                last = pe.transpose(gate_bank[0][:, k * NE:(k + 1) * NE], gw[:, k * P:(k + 1) * P], ident[0:NE, 0:NE])
            last.then_inc(gate_T, 1)
            pe.matmul(gate_bank[1][:, 0:NE], ones_row[:, :], gb_row[:, :], start=True, stop=True).then_inc(gate_T, 1)
            pe.wait_ge(gate_T_copied, 2)
            ln.transposed(pe, up_bank[0], ident, 0).then_inc(pair_turned.sem, 1)
            for i in range(PAIRS):
                if i + 1 < PAIRS:
                    if i >= 1:
                        wait(pe, pair_low, i, 0)
                    ln.transposed(pe, up_bank[(i + 1) % 2], ident, i + 1).then_inc(pair_turned.sem, 1)
                wait(pe, pair_copied, i, 1)
                for b in range(2):
                    tile = 2 * i + b
                    for k in range(KD):
                        last = pe.matmul(route_bank[:, tile * NE:(tile + 1) * NE], xnT_pair[i % 2][:, k, b * P:(b + 1) * P],
                                         gwT[:, k, :], start=(k == 0), stop=(k == KD - 1))
                last.then_inc(logits_ready.sem, 1)
            for m in range(3):
                turn_weights(pe, 0, m, first_turn_banks[m])
            wait(pe, pair_low, PAIRS, 0)
            all_experts(pe, lambda e, par, last_one=False: expert_on_pe(pe, e, par, last_one))

        @block.scalar
        def _(act):
            def copy_weights(e, par, m, bank=turn_bank):
                wait(act, w_turned, e, m + 1)
                act.copy(wT[par][0][:, m, :, :].rearrange("p k n -> p (k n)"), bank[:, :]).then_inc(w_high.sem, 1)

            for i in range(PAIRS):
                pair = up_bank[i % 2][:, :].rearrange("p (k t) -> p k t", k=KD)
                wait(act, pair_turned, i, 1)
                if i >= 2:
                    wait(act, logits_ready, i, -1)
                act.copy(xnT_pair[i % 2][:, :, :], pair).then_inc(pair_copied.sem, 1)
                act.copy(xnT[0][:, :, i * 2 * P:(i + 1) * 2 * P], pair).then_inc(pair_high.sem, 1)
            wait(act, logits_ready, PAIRS, 0)
            act.activation(score[:, :, :].rearrange("p b e -> p (b e)"), route_bank[:, 0:NB * NE],
                           ACT.Exp, scale=-1.0).then_inc(logits_exp, 1)
            for m in range(3):
                copy_weights(0, 0, m, first_turn_banks[m])

            def expert_on_act(e, par, last_one=False):
                def round_product(g, m):
                    wait(act, product_ready[m], e, g + 1)
                    if g < 2:
                        wait(act, y_ready[1], e, 0)
                    else:
                        wait(act, y_ready[1], e, g - 1)
                    act.copy(hidden[0][:, g % 2, m, :], act_up[:, m, :]).then_inc(high_ready[m].sem, 1)

                for g in range(GROUPS):
                    for m in range(2):
                        wait(act, gate_ready[m], e, g + 1)
                        wait(act, product_ready[m], e, g)
                        act.activation(silu[:, m, :], gate_bank[m][:, :], ACT.Silu).then_inc(silu_ready[m].sem, 1)
                        if m == 1:
                            round_product(g, 0)
                        elif g >= 1:
                            round_product(g - 1, 1)
                    if g < 3 and not last_one:
                        if g == 0:
                            wait(act, y_ready[1], e, 0)
                        copy_weights(e + 1, 1 - par, g)
                round_product(GROUPS - 1, 1)

            all_experts(act, expert_on_act)

        @block.vector
        def _(dve):
            def copy_weights(e, par, m, bank=turn_bank):
                wait(dve, w_high, e, m + 1)
                high, low = (w[:, m, :, :].rearrange("p k n -> p (k n)") for w in wT[par])
                dve.tensor_tensor(low, bank[:, :], high, ALU.subtract).then_inc(w_low.sem, 1)

            ln.statistics(dve, 0)
            ln.apply(dve, 0)
            dve.wait_ge(gate_T, 2)
            dve.tensor_copy(gwT[:, :, :].rearrange("p k n -> p (k n)"), gate_bank[0][:, 0:KD * NE]).then_inc(gate_T_copied, 1)
            dve.tensor_copy(gate_bias[:, :], gate_bank[1][:, 0:NE]).then_inc(gate_T_copied, 1)

            def low_part(i):
                wait(dve, pair_high, i, 1)
                high, low = (part[:, :, i * 2 * P:(i + 1) * 2 * P] for part in xnT)
                dve.tensor_tensor(low, up_bank[i % 2][:, :].rearrange("p (k t) -> p k t", k=KD), high, ALU.subtract) \
                    .then_inc(pair_low.sem, 1)

            for i in range(PAIRS):
                ln.statistics(dve, i + 1)
                if i >= 1:
                    low_part(i - 1)
                if i + 1 < PAIRS:
                    wait(dve, pair_turned, i, 1)
                    ln.apply(dve, i + 1)
            low_part(PAIRS - 1)
            for m in range(3):
                copy_weights(0, 0, m, first_turn_banks[m])
            dve.wait_ge(ones_set, 1)

            def route(step):
                def link(ins):
                    route_links.link(dve, ins)

                if step == 0:
                    dve.wait_ge(logits_exp, 1)
                    dve.wait_ge(gate_T_copied, 2)
                    link(dve.tensor_scalar(score[:, :, :], score[:, :, :], 1.0, None, ALU.add))
                    link(dve.reciprocal(score[:, :, :], score[:, :, :]))
                    link(dve.tensor_tensor(chosen_by[:, :, :], score[:, :, :],
                                           gate_bias[:, :].unsqueeze(1).broadcast_to([P, NB, NE]), ALU.add))
                elif step == 1:
                    for b in range(NB):
                        last = dve.max(top[:, b, :], chosen_by[:, b, :])
                    link(last)
                elif step == 2:
                    for b in range(NB):
                        last = dve.match_replace(left[:, b, :], top[:, b, :], chosen_by[:, b, :], TAKEN)
                    link(last)
                else:
                    link(dve.tensor_tensor(left[:, :, :], left[:, :, :], chosen_by[:, :, :], ALU.not_equal))
                    link(dve.tensor_tensor(score[:, :, :], score[:, :, :], left[:, :, :], ALU.mult))
                    link(dve.tensor_reduce(total[:, :], score[:, :, :], AX.X, ALU.add))
                    link(dve.reciprocal(total[:, :], total[:, :]))
                    link(dve.tensor_scalar(total[:, :], total[:, :], ROUTE_SCALE, None, ALU.mult))
                    link(dve.tensor_tensor(combine[:, :, 1:NE + 1], score[:, :, :],
                                           total[:, :].unsqueeze(2).broadcast_to([P, NB, NE]), ALU.mult))

            def expert_on_dve(e, par, last_one=False):
                def add(g):
                    for n in range(2):
                        wait(dve, y_ready[n], e, g + 1)
                        for t in range(2):
                            tile = 4 * g + 2 * n + t
                            weight = combine[:, tile, bass.ds(e, 1)] if not isinstance(e, int) else combine[:, tile, e:e + 1]
                            last = dve.scalar_tensor_tensor(x[:, tile, :], y_bank[n][:, t * D:(t + 1) * D], weight,
                                                            x[:, tile, :], ALU.mult, ALU.add)
                        last.then_inc(y_added[n].sem, 1)

                def remainder(g, m):
                    wait(dve, high_ready[m], e, g + 1)
                    dve.tensor_tensor(hidden[1][:, g % 2, m, :], act_up[:, m, :], hidden[0][:, g % 2, m, :],
                                      ALU.subtract).then_inc(low_ready[m].sem, 1)

                for g in range(GROUPS):
                    for m in range(2):
                        wait(dve, silu_ready[m], e, g + 1)
                        wait(dve, up_ready[m], e, g + 1)
                        wait(dve, low_ready[m], e, g)
                        dve.tensor_tensor(act_up[:, m, :], silu[:, m, :], up_bank[m][:, :], ALU.mult) \
                            .then_inc(product_ready[m].sem, 1)
                        if m == 1:
                            remainder(g, 0)
                        elif g >= 1:
                            remainder(g - 1, 1)
                    if g == GROUPS - 1:
                        remainder(g, 1)
                    if g >= 1:
                        add(g - 1)
                    if g < 3 and not last_one:
                        copy_weights(e + 1, 1 - par, g)
                    if isinstance(e, int) and e == 0:
                        route(g)
                add(GROUPS - 1)

            all_experts(dve, expert_on_dve)


def stage_constants(nc, ident, ident_bf, causal_bf, chunk_bf, ones_row, half_mask, head_mask):
    with ExitStack() as ctx:
        s = Scope(nc, ctx, "c")
        filled = s.sem("filled")
        lower_cut = s.sem("lower_cut")
        block = s.block()

        @block.gpsimd
        def _(pool):
            for m in (ident, ident_bf, causal_bf, chunk_bf):
                pool.memset(m[:, :], 0.0).then_inc(filled, 1)
            for m in (ones_row, half_mask, head_mask):
                pool.memset(m[:, :], 1.0).then_inc(filled, 1)
            pool.wait_ge(filled, 7)
            for m in (ident, ident_bf):
                pool.affine_select(out=m[:, :], in_=m[:, :], compare_op=ALU.not_equal, fill=1.0, base=0,
                                   pattern=[[-1, P]], channel_multiplier=1)
            pool.affine_select(out=causal_bf[:, :], in_=causal_bf[:, :], compare_op=ALU.is_ge, fill=NEG, base=0,
                               pattern=[[0, 4], [-1, P]], channel_multiplier=1)
            cv = chunk_bf[:, :].rearrange("p (j c k) -> p j c k", j=4, c=2)
            pool.affine_select(out=cv[:, :, 0, :], in_=cv[:, :, 0, :], compare_op=ALU.is_ge, fill=NEG, base=63,
                               pattern=[[0, 4], [0, 64]], channel_multiplier=-1)
            pool.affine_select(out=cv[:, :, 1, :], in_=cv[:, :, 1, :], compare_op=ALU.is_ge, fill=NEG, base=-64,
                               pattern=[[0, 4], [0, 64]], channel_multiplier=1)
            for m, heads in ((half_mask, 2), (head_mask, 8)):
                pool.affine_select(out=m[:, :], in_=m[:, :], compare_op=ALU.is_ge, fill=0.0, base=0,
                                   pattern=[[-(P // heads), heads]], channel_multiplier=1).then_inc(lower_cut, 1)
            pool.wait_ge(lower_cut, 2)
            for m, heads in ((half_mask, 2), (head_mask, 8)):
                pool.affine_select(out=m[:, :], in_=m[:, :], compare_op=ALU.is_ge, fill=0.0, base=P // heads - 1,
                                   pattern=[[P // heads, heads]], channel_multiplier=-1)


def decoder(nc, out, a):
    with ExitStack() as ctx:
        s = Scope(nc, ctx, "g")
        x = s.sb("x", [P, NB + 2, D])
        ident = s.sb("ident", [P, P])
        ones_row = s.sb("ones_row", [1, P])
        half_mask = s.sb("half_mask", [P, 2])
        head_mask = s.sb("head_mask", [P, 8])
        stored = s.sem("stored")
        with ExitStack() as masks_ctx:
            m = Scope(nc, masks_ctx, "m")
            ident_bf = m.sb("ident_bf", [P, P], BF16)
            causal_bf = m.sb("causal_bf", [P, 4 * P], BF16)
            chunk_bf = m.sb("chunk_bf", [P, 4 * P], BF16)
            stage_constants(nc, ident, ident_bf, causal_bf, chunk_bf, ones_row, half_mask, head_mask)
            stage_causal_attention(nc, x, ident, ones_row, ident_bf, causal_bf, half_mask, a["x"], a["L0_attn_w_q"],
                                   a["L0_attn_w_k"], a["L0_attn_w_v"], a["L0_attn_w_u"], a["L0_attn_b_u"])
            stage_chunked_attention(nc, x, ident, ones_row, ident_bf, chunk_bf, head_mask, a["ctx_1024"],
                                    a["L0_xattn_in_proj_w"], a["L0_xattn_in_proj_b"], a["L0_xattn_out_proj_w"],
                                    a["L0_xattn_out_proj_b"])
        stage_product_keys(nc, x, ident, a["L0_ffn_gamma"], a["L0_ffn_beta"], a["L0_ffn_w_q"], a["L0_ffn_keys"],
                           a["L0_ffn_key_in"], a["L0_ffn_key_out"])
        stage_gated_attention(nc, x, ident, ones_row, head_mask, a["L1_attn_Wq"], a["L1_attn_bq"],
                              a["L1_attn_Wk"], a["L1_attn_bk"], a["L1_attn_Wv"], a["L1_attn_bv"],
                              a["L1_attn_Wo"], a["L1_attn_bo"], a["L1_attn_g"], a["L1_attn_Wg1"],
                              a["L1_attn_bg1"], a["L1_attn_Wg2"], a["L1_attn_bg2"])
        stage_aligned_attention(nc, x, ident, a["ctx_1024"], a["L1_xattn_W"], a["L1_xattn_b"])
        stage_experts(nc, x, ident, ones_row, a["L1_ffn_gate_w"], a["L1_ffn_expert_bias"], a["L1_ffn_w_gate"],
                      a["L1_ffn_w_up"], a["L1_ffn_w_down"], a["L1_ffn_shared_gate_w"],
                      a["L1_ffn_shared_up_w"], a["L1_ffn_shared_down_w"])
        block = s.block()

        @block.sync
        def _(sp):
            sp.dma_start(out.rearrange("b t d -> t b d"), x[:, 0:NB, :]).then_inc(stored, 16)
            sp.wait_ge(stored, 16)


_INS = ['x', 'ctx_1024', 'L0_attn_w_q', 'L0_attn_w_k', 'L0_attn_w_v', 'L0_attn_w_u', 'L0_attn_b_u',
        'L0_xattn_in_proj_w', 'L0_xattn_in_proj_b', 'L0_xattn_out_proj_w', 'L0_xattn_out_proj_b',
        'L0_ffn_gamma', 'L0_ffn_beta', 'L0_ffn_w_q', 'L0_ffn_keys', 'L0_ffn_key_in', 'L0_ffn_key_out',
        'L1_attn_Wq', 'L1_attn_bq', 'L1_attn_Wk', 'L1_attn_bk', 'L1_attn_Wv', 'L1_attn_bv', 'L1_attn_Wo',
        'L1_attn_bo', 'L1_attn_g', 'L1_attn_Wg1', 'L1_attn_bg1', 'L1_attn_Wg2', 'L1_attn_bg2',
        'L1_xattn_W', 'L1_xattn_b', 'L1_ffn_gate_w', 'L1_ffn_expert_bias', 'L1_ffn_w_gate', 'L1_ffn_w_up',
        'L1_ffn_w_down', 'L1_ffn_shared_gate_w', 'L1_ffn_shared_up_w', 'L1_ffn_shared_down_w']


def kernel(**inputs):
    import numpy as np
    from concourse import bacc
    from concourse.bass_utils import run_bass_kernel_spmd

    nc = bacc.Bacc("TRN2", target_bir_lowering=False, num_devices=1)
    arrays, args = {}, {}
    for name in _INS:
        a = np.ascontiguousarray(inputs[name])
        arrays[f"in_{name}"] = a
        args[name] = nc.dram_tensor(f"in_{name}", a.shape, mybir.dt.from_np(a.dtype), kind="ExternalInput").ap()
    out = nc.dram_tensor("out", (NB, P, D), F32, kind="ExternalOutput").ap()
    decoder(nc, out, args)
    r = run_bass_kernel_spmd(nc, [arrays], core_ids=[0])
    return r.results[0]["out"]
```
